# Optimizing a Trainium2 kernel written in Bass

```python
import numpy as np
import jax
import jax.numpy as jnp

def _softmax(x, axis=-1):
    return jax.nn.softmax(x, axis=axis)

def _gelu(x):
    return jax.nn.gelu(x, approximate=True)

def _silu(x):
    return jax.nn.silu(x)

def _sigmoid(x):
    return jax.nn.sigmoid(x)

def _layernorm(x, axis=-1, eps=1e-05):
    m = jnp.mean(x, axis=axis, keepdims=True)
    v = jnp.var(x, axis=axis, keepdims=True)
    return (x - m) / jnp.sqrt(v + eps)

def _scatter_add(tgt, idx, src, axis=0):
    return tgt.at[idx].add(src)

def _segment_sum(src, seg, n):
    return jax.ops.segment_sum(src, seg, n)
kernel_name = 'mk_adaln_ffn_d1_seqx_r4_1af548'

def setup_inputs(seed: int=0):
    np.random.seed(seed)
    _w = jnp.asarray

    def _rec_inputs():
        import jax
        import jax.numpy as jnp
        _rk = jax.random.key(seed)
        x = -0.0001538 + 1 * jax.random.normal(jax.random.fold_in(_rk, 1), (64, 64, 256), jnp.float32)
        _lenS = 64 - jax.random.randint(jax.random.fold_in(_rk, 7), (64,), 0, max(1, 64 // 4) + 1, jnp.int32)
        _lenS2 = 64 - jax.random.randint(jax.random.fold_in(_rk, 8), (64,), 0, max(1, 64 // 4) + 1, jnp.int32)
        cond_1024 = 0.00782532 + 1.00527 * jax.random.normal(jax.random.fold_in(_rk, 11), (64, 256), jnp.float32)
        return (x, cond_1024)
    x, cond_1024 = _rec_inputs()

    def _L0_cond_setup():
        import jax, jax.numpy as jnp
        import numpy as np
        NUM_EXPERTS = 4
        TOP_K = 2
        key = jax.random.key(seed)
        ks = jax.random.split(key, 16)
        B, L, D, E, H = (8, 192, 256, NUM_EXPERTS, 1024)
        s = 0.02
        return {'context_c': jax.random.normal(ks[0], (B, L, D), jnp.float32), 'time_cond': jax.random.normal(ks[1], (B, D), jnp.float32), 'gate_w': jax.random.normal(ks[2], (3 * D, E), jnp.float32) * s, 'gate_b': jnp.zeros((E,), jnp.float32), 'time_w': jax.random.normal(ks[3], (D, 2 * E), jnp.float32) * s, 'time_b': jnp.zeros((2 * E,), jnp.float32), 'ew1': jax.random.normal(ks[4], (E, D, H), jnp.float32) * s, 'eb1': jnp.zeros((E, H), jnp.float32), 'ew2': jax.random.normal(ks[5], (E, H, D), jnp.float32) * s, 'eb2': jnp.zeros((E, D), jnp.float32), 'sw1': jax.random.normal(ks[6], (D, H), jnp.float32) * s, 'sb1': jnp.zeros((H,), jnp.float32), 'sw2': jax.random.normal(ks[7], (H, D), jnp.float32) * s, 'sb2': jnp.zeros((D,), jnp.float32)}
    _L0_cond_all = _L0_cond_setup()
    _L0_cond_in = {k: v for k, v in _L0_cond_all.items() if k in ('gate_w', 'gate_b', 'time_w', 'time_b', 'ew1', 'eb1', 'ew2', 'eb2', 'sw1', 'sb1', 'sw2', 'sb2')}
    del _L0_cond_all

    def _L0_ffn_setup():
        import jax, jax.numpy as jnp
        import numpy as np
        EPS = 1e-05

        def _ln(x, g, b):
            mu = jnp.mean(x, axis=-1, keepdims=True)
            var = jnp.mean(jnp.square(x - mu), axis=-1, keepdims=True)
            return (x - mu) * jax.lax.rsqrt(var + EPS) * g + b

        def _forward(x, index_b, index_t, sw1, sb1, sw2, sb2, sw3, sb3, s_ln_g, s_ln_b, sg_w, sg_b, eg_w, eg_b, exp_bias, ew1, eb1, ew2, eb2, ew3, eb3, sel_ln_g, sel_ln_b):
            x1 = jnp.einsum('btd,hd->bth', x, sw1) + sb1
            x2 = jnp.einsum('btd,hd->bth', x, sw2) + sb2
            sh = _ln(jax.nn.silu(x1) * x2, s_ln_g, s_ln_b)
            shared_out = jnp.einsum('bth,dh->btd', sh, sw3) + sb3
            x_moe = x[index_b, index_t]
            shared_scores = jax.nn.sigmoid(x_moe @ sg_w.T + sg_b)
            expert_scores = jax.nn.sigmoid(x_moe @ eg_w.T + eg_b)
            top1_idx = jnp.argmax(expert_scores + exp_bias, axis=-1)
            top1_score = jnp.take_along_axis(expert_scores, top1_idx[:, None], axis=-1)
            weights = jax.nn.softmax(jnp.concatenate([shared_scores, top1_score], axis=-1), axis=-1)
            shared_w, expert_w = (weights[:, 0], weights[:, 1])
            shared_moe_out = shared_out[index_b, index_t] * shared_w[:, None]
            h1 = jnp.einsum('md,ehd->meh', x_moe, ew1) + eb1
            h2 = jnp.einsum('md,ehd->meh', x_moe, ew2) + eb2
            z = _ln(jax.nn.silu(h1) * h2, sel_ln_g, sel_ln_b)
            out_all = jnp.einsum('meh,edh->med', z, ew3) + eb3
            expert_out = jnp.take_along_axis(out_all, top1_idx[:, None, None], axis=1)[:, 0]
            expert_moe_out = expert_out * expert_w[:, None]
            final_out = shared_out.at[index_b, index_t].set(shared_moe_out + expert_moe_out)
            return final_out
        B, T, D, E, H, M = (2, 512, 256, 8, 128, 512)
        key = jax.random.key(seed)
        ks = jax.random.split(key, 24)
        s = 0.02
        inp = {}
        inp['x'] = jax.random.normal(ks[0], (B, T, D), jnp.float32)
        flat = jnp.arange(M, dtype=jnp.int32) * 2
        inp['index_b'] = flat // T
        inp['index_t'] = flat % T
        inp['sw1'] = jax.random.normal(ks[1], (H, D), jnp.float32) * s
        inp['sb1'] = jnp.zeros((H,), jnp.float32)
        inp['sw2'] = jax.random.normal(ks[2], (H, D), jnp.float32) * s
        inp['sb2'] = jnp.zeros((H,), jnp.float32)
        inp['sw3'] = jax.random.normal(ks[3], (D, H), jnp.float32) * s
        inp['sb3'] = jnp.zeros((D,), jnp.float32)
        inp['s_ln_g'] = jnp.ones((H,), jnp.float32)
        inp['s_ln_b'] = jnp.zeros((H,), jnp.float32)
        inp['sg_w'] = jax.random.normal(ks[4], (1, D), jnp.float32) * s
        inp['sg_b'] = jnp.zeros((1,), jnp.float32)
        inp['eg_w'] = jax.random.normal(ks[5], (E, D), jnp.float32) * s
        inp['eg_b'] = jnp.zeros((E,), jnp.float32)
        inp['exp_bias'] = jnp.zeros((E,), jnp.float32)
        inp['ew1'] = jax.random.normal(ks[6], (E, H, D), jnp.float32) * s
        inp['eb1'] = jnp.zeros((E, H), jnp.float32)
        inp['ew2'] = jax.random.normal(ks[7], (E, H, D), jnp.float32) * s
        inp['eb2'] = jnp.zeros((E, H), jnp.float32)
        inp['ew3'] = jax.random.normal(ks[8], (E, D, H), jnp.float32) * s
        inp['eb3'] = jnp.zeros((E, D), jnp.float32)
        inp['sel_ln_g'] = jnp.ones((H,), jnp.float32)
        inp['sel_ln_b'] = jnp.zeros((H,), jnp.float32)
        return inp
    _L0_ffn_all = _L0_ffn_setup()
    _L0_ffn_in = {k: v for k, v in _L0_ffn_all.items() if k in ('index_b', 'index_t', 'sw1', 'sb1', 'sw2', 'sb2', 'sw3', 'sb3', 's_ln_g', 's_ln_b', 'sg_w', 'sg_b', 'eg_w', 'eg_b', 'exp_bias', 'ew1', 'eb1', 'ew2', 'eb2', 'ew3', 'eb3', 'sel_ln_g', 'sel_ln_b')}
    del _L0_ffn_all
    return {'x': x, 'cond_1024': cond_1024, 'L0_cond_gate_w': _L0_cond_in['gate_w'], 'L0_cond_gate_b': _L0_cond_in['gate_b'], 'L0_cond_time_w': _L0_cond_in['time_w'], 'L0_cond_time_b': _L0_cond_in['time_b'], 'L0_cond_ew1': _L0_cond_in['ew1'], 'L0_cond_eb1': _L0_cond_in['eb1'], 'L0_cond_ew2': _L0_cond_in['ew2'], 'L0_cond_eb2': _L0_cond_in['eb2'], 'L0_cond_sw1': _L0_cond_in['sw1'], 'L0_cond_sb1': _L0_cond_in['sb1'], 'L0_cond_sw2': _L0_cond_in['sw2'], 'L0_cond_sb2': _L0_cond_in['sb2'], 'L0_ffn_index_b': _L0_ffn_in['index_b'], 'L0_ffn_index_t': _L0_ffn_in['index_t'], 'L0_ffn_sw1': _L0_ffn_in['sw1'], 'L0_ffn_sb1': _L0_ffn_in['sb1'], 'L0_ffn_sw2': _L0_ffn_in['sw2'], 'L0_ffn_sb2': _L0_ffn_in['sb2'], 'L0_ffn_sw3': _L0_ffn_in['sw3'], 'L0_ffn_sb3': _L0_ffn_in['sb3'], 'L0_ffn_s_ln_g': _L0_ffn_in['s_ln_g'], 'L0_ffn_s_ln_b': _L0_ffn_in['s_ln_b'], 'L0_ffn_sg_w': _L0_ffn_in['sg_w'], 'L0_ffn_sg_b': _L0_ffn_in['sg_b'], 'L0_ffn_eg_w': _L0_ffn_in['eg_w'], 'L0_ffn_eg_b': _L0_ffn_in['eg_b'], 'L0_ffn_exp_bias': _L0_ffn_in['exp_bias'], 'L0_ffn_ew1': _L0_ffn_in['ew1'], 'L0_ffn_eb1': _L0_ffn_in['eb1'], 'L0_ffn_ew2': _L0_ffn_in['ew2'], 'L0_ffn_eb2': _L0_ffn_in['eb2'], 'L0_ffn_ew3': _L0_ffn_in['ew3'], 'L0_ffn_eb3': _L0_ffn_in['eb3'], 'L0_ffn_sel_ln_g': _L0_ffn_in['sel_ln_g'], 'L0_ffn_sel_ln_b': _L0_ffn_in['sel_ln_b']}

def reference(x, cond_1024, L0_cond_gate_w, L0_cond_gate_b, L0_cond_time_w, L0_cond_time_b, L0_cond_ew1, L0_cond_eb1, L0_cond_ew2, L0_cond_eb2, L0_cond_sw1, L0_cond_sb1, L0_cond_sw2, L0_cond_sb2, L0_ffn_index_b, L0_ffn_index_t, L0_ffn_sw1, L0_ffn_sb1, L0_ffn_sw2, L0_ffn_sb2, L0_ffn_sw3, L0_ffn_sb3, L0_ffn_s_ln_g, L0_ffn_s_ln_b, L0_ffn_sg_w, L0_ffn_sg_b, L0_ffn_eg_w, L0_ffn_eg_b, L0_ffn_exp_bias, L0_ffn_ew1, L0_ffn_eb1, L0_ffn_ew2, L0_ffn_eb2, L0_ffn_ew3, L0_ffn_eb3, L0_ffn_sel_ln_g, L0_ffn_sel_ln_b):
    import jax
    import jax.numpy as jnp

    def _L0_cond_ref(context_c, time_cond, gate_w, gate_b, time_w, time_b, ew1, eb1, ew2, eb2, sw1, sb1, sw2, sb2):
        import jax, jax.numpy as jnp
        import numpy as np
        NUM_EXPERTS = 4
        TOP_K = 2
        B, L, D = context_c.shape
        E, K = (NUM_EXPERTS, TOP_K)
        L_head = L_wrist = L // 3
        head = context_c[:, :L_head]
        wrist = context_c[:, L_head:L_head + L_wrist]
        proprio = context_c[:, L_head + L_wrist:]
        full_agg = context_c.mean(axis=1)
        hp_agg = jnp.concatenate([head, proprio], axis=1).mean(axis=1)
        wp_agg = jnp.concatenate([wrist, proprio], axis=1).mean(axis=1)
        gate_in = jnp.concatenate([full_agg, hp_agg, wp_agg], axis=-1)
        gate_logits = gate_in @ gate_w + gate_b
        mod = jax.nn.silu(time_cond) @ time_w + time_b
        scale, shift = jnp.split(mod, 2, axis=-1)
        gate_logits = gate_logits * (1.0 + scale) + shift
        gate_scores = jax.nn.softmax(gate_logits, axis=-1)
        topk_w, topk_i = jax.lax.top_k(gate_scores, K)
        topk_w = topk_w / (topk_w.sum(axis=-1, keepdims=True) + 1e-08)
        onehot = (topk_i[..., None] == jnp.arange(E)[None, None, :]).astype(context_c.dtype)
        w_be = jnp.sum(topk_w[..., None] * onehot, axis=1)
        mask = np.ones((E, L), dtype=np.float32)
        mask[1, L_head:L_head + L_wrist] = 0.0
        mask[2, :L_head] = 0.0
        mask = jnp.asarray(mask)
        out = jnp.zeros_like(context_c)
        for e in range(E):
            h = jax.nn.gelu(context_c @ ew1[e] + eb1[e], approximate=True)
            y = h @ ew2[e] + eb2[e]
            out = out + w_be[:, e][:, None, None] * mask[e][None, :, None] * y
        shared = jax.nn.gelu(context_c @ sw1 + sb1, approximate=True) @ sw2 + sb2
        return out + shared

    def _L0_ffn_ref(x, index_b, index_t, sw1, sb1, sw2, sb2, sw3, sb3, s_ln_g, s_ln_b, sg_w, sg_b, eg_w, eg_b, exp_bias, ew1, eb1, ew2, eb2, ew3, eb3, sel_ln_g, sel_ln_b):
        import jax, jax.numpy as jnp
        import numpy as np
        EPS = 1e-05

        def _ln(x, g, b):
            mu = jnp.mean(x, axis=-1, keepdims=True)
            var = jnp.mean(jnp.square(x - mu), axis=-1, keepdims=True)
            return (x - mu) * jax.lax.rsqrt(var + EPS) * g + b

        def _forward(x, index_b, index_t, sw1, sb1, sw2, sb2, sw3, sb3, s_ln_g, s_ln_b, sg_w, sg_b, eg_w, eg_b, exp_bias, ew1, eb1, ew2, eb2, ew3, eb3, sel_ln_g, sel_ln_b):
            x1 = jnp.einsum('btd,hd->bth', x, sw1) + sb1
            x2 = jnp.einsum('btd,hd->bth', x, sw2) + sb2
            sh = _ln(jax.nn.silu(x1) * x2, s_ln_g, s_ln_b)
            shared_out = jnp.einsum('bth,dh->btd', sh, sw3) + sb3
            x_moe = x[index_b, index_t]
            shared_scores = jax.nn.sigmoid(x_moe @ sg_w.T + sg_b)
            expert_scores = jax.nn.sigmoid(x_moe @ eg_w.T + eg_b)
            top1_idx = jnp.argmax(expert_scores + exp_bias, axis=-1)
            top1_score = jnp.take_along_axis(expert_scores, top1_idx[:, None], axis=-1)
            weights = jax.nn.softmax(jnp.concatenate([shared_scores, top1_score], axis=-1), axis=-1)
            shared_w, expert_w = (weights[:, 0], weights[:, 1])
            shared_moe_out = shared_out[index_b, index_t] * shared_w[:, None]
            h1 = jnp.einsum('md,ehd->meh', x_moe, ew1) + eb1
            h2 = jnp.einsum('md,ehd->meh', x_moe, ew2) + eb2
            z = _ln(jax.nn.silu(h1) * h2, sel_ln_g, sel_ln_b)
            out_all = jnp.einsum('meh,edh->med', z, ew3) + eb3
            expert_out = jnp.take_along_axis(out_all, top1_idx[:, None, None], axis=1)[:, 0]
            expert_moe_out = expert_out * expert_w[:, None]
            final_out = shared_out.at[index_b, index_t].set(shared_moe_out + expert_moe_out)
            return final_out
        return _forward(x, index_b, index_t, sw1, sb1, sw2, sb2, sw3, sb3, s_ln_g, s_ln_b, sg_w, sg_b, eg_w, eg_b, exp_bias, ew1, eb1, ew2, eb2, ew3, eb3, sel_ln_g, sel_ln_b)
    x = x + _L0_ffn_ref(_L0_cond_ref(x, cond_1024, L0_cond_gate_w, L0_cond_gate_b, L0_cond_time_w, L0_cond_time_b, L0_cond_ew1, L0_cond_eb1, L0_cond_ew2, L0_cond_eb2, L0_cond_sw1, L0_cond_sb1, L0_cond_sw2, L0_cond_sb2), L0_ffn_index_b, L0_ffn_index_t, L0_ffn_sw1, L0_ffn_sb1, L0_ffn_sw2, L0_ffn_sb2, L0_ffn_sw3, L0_ffn_sb3, L0_ffn_s_ln_g, L0_ffn_s_ln_b, L0_ffn_sg_w, L0_ffn_sg_b, L0_ffn_eg_w, L0_ffn_eg_b, L0_ffn_exp_bias, L0_ffn_ew1, L0_ffn_eb1, L0_ffn_ew2, L0_ffn_eb2, L0_ffn_ew3, L0_ffn_eb3, L0_ffn_sel_ln_g, L0_ffn_sel_ln_b)
    return x

_drawn_inputs = setup_inputs


def setup_inputs(seed=0):
    import zlib

    import numpy as np

    out = dict(_drawn_inputs(seed))
    spreads = {'L0_cond_gate_b': (0.0, 0.1),
     'L0_cond_time_b': (0.0, 0.1),
     'L0_cond_eb1': (0.0, 0.47),
     'L0_cond_eb2': (0.0, 0.1),
     'L0_cond_sb1': (0.0, 0.311),
     'L0_cond_sb2': (0.0, 0.1),
     'L0_ffn_sb1': (0.0, 0.1),
     'L0_ffn_sb2': (0.0, 0.1),
     'L0_ffn_sb3': (0.0, 0.1),
     'L0_ffn_s_ln_g': (1.0, 0.2),
     'L0_ffn_s_ln_b': (0.0, 0.344),
     'L0_ffn_eg_b': (0.0, 2.0),
     'L0_ffn_exp_bias': (0.0, 0.444),
     'L0_ffn_eb1': (0.0, 0.569),
     'L0_ffn_eb2': (0.0, 0.603),
     'L0_ffn_eb3': (0.0, 0.8),
     'L0_ffn_sel_ln_g': (1.0, 0.6),
     'L0_ffn_sel_ln_b': (0.0, 0.8)}
    factors = {'L0_ffn_sg_w': 40.237,
     'L0_ffn_eg_w': 56.538,
     'L0_ffn_ew1': 8.0,
     'L0_ffn_ew2': 7.71,
     'L0_ffn_ew3': 4.063}
    for name, (base, spread) in spreads.items():
        noise = np.random.default_rng([zlib.crc32(name.encode()), seed]).standard_normal(out[name].shape)
        drawn = base * np.exp(spread * noise) if base else spread * noise
        out[name] = jnp.asarray(drawn.astype(out[name].dtype))
    for name, factor in factors.items():
        out[name] = (out[name] * factor).astype(out[name].dtype)
    return out
```

```python
from contextlib import ExitStack, contextmanager

import concourse.bass as bass
from concourse import mybir

F32 = mybir.dt.float32
F16 = mybir.dt.float16
I32 = mybir.dt.int32
ACT = mybir.ActivationFunctionType
ALU = mybir.AluOpType
AX = mybir.AxisListType

P = 128
NB, NT, D = 64, 64, 256
TOK = NB * NT
H = 1024
E, SH = 4, 4
DB, HB = D // P, H // P
HEAD = NT // 3
HP = HEAD + (NT - 2 * HEAD)
WS = 1024.0
CH = 256
SLOTS = CH // NT
NS = TOK // CH
NR = (2 * NB + E * (SLOTS - 1)) // SLOTS
NSLOT = NR * SLOTS
COLS = TOK + SLOTS * NT
WE = 8192
FE, FH, M = 8, 128, 512
MG = M // P
EPS = 1e-5
NJ = FE + 1
FC = 512
NQ = TOK // FC
NK = NQ + NJ
IDX = 2 * 2 * (M + MG)


@contextmanager
def by_two(eng, start, end):
    with eng.Fori(0, (end - start) // 2) as i:
        yield i * 2 + start


def program(nc, a):
    with ExitStack() as ctx:
        def sb(name, shape, dt=F32):
            return ctx.enter_context(nc.sbuf_tensor(name, shape, dt))

        def sem(name):
            return ctx.enter_context(nc.semaphore(name))

        W = sb("W", [P, (E + 1) * WE], F16)
        X = sb("X", [P, 2 * DB, COLS], F16)
        acc = sb("acc", [P, DB, COLS])
        hbuf = sb("hbuf", [P, 2, 2, HB, CH], F16)
        h32 = sb("h32", [P, 4, 2 * CH])
        xs = sb("xs", [P, 2, 2 * DB, CH], F16)
        ytmp = sb("ytmp", [P, DB, CH])
        stage = sb("stage", [P, 2, 1024])
        F0 = sb("F0", [P, 1024], F16)
        V = sb("V", [P, NJ, 2, D], F16)
        b1 = sb("b1", [P, (E + 1) * HB])
        b2 = sb("b2", [P, (E + 1) * DB])
        b2s = sb("b2s", [P, (E + 1) * DB])
        mask = sb("mask", [P, E, NT])
        wrow = sb("wrow", [P, NSLOT])
        tab = sb("tab", [1, NR * 8], I32)
        gsum = sb("gsum", [P, DB, 3, NB])
        gin = sb("gin", [P, 3 * DB, NB])
        cond = sb("cond", [P, DB, NB])
        silc = sb("silc", [P, DB, NB])
        gw = sb("gw", [P, 3 * DB, E])
        tw = sb("tw", [P, DB, 2 * E])
        gb = sb("gb", [NB, E])
        tb = sb("tb", [NB, 2 * E])
        G = sb("G", [NB, 24, E])
        gcnt = sb("gcnt", [NB, E, 16])
        fb1 = sb("fb1", [P, NJ])
        fb2 = sb("fb2", [P, NJ])
        gam = sb("gam", [P, 2])
        bet = sb("bet", [P, 2])
        gid = sb("gid", [P, MG], I32)
        sid = sb("sid", [P, MG], I32)
        f4 = sb("f4", [P, 8, MG])

        W32 = W[:, :].bitcast(F32)
        ws32 = W32[:, 0:WE // 2]
        x32 = W32[:, WE // 2:WE // 2 + DB * TOK].rearrange("p (d t) -> p d t", d=DB)
        acc_hi = acc[:, 0, TOK - IDX:TOK]
        acc_hi1 = acc[:, 1, TOK - IDX:TOK]
        kidx = acc_hi[:, 0:2 * 516].rearrange("p (w m) -> p w m", w=2)
        kint = acc_hi[:, 1032:2064].bitcast(I32).rearrange("p (w m) -> p w m", w=2)
        ktmp = acc_hi1[:, 0:1032].rearrange("p (w m) -> p w m", w=2)
        iot = acc_hi1[:, 1032:1032 + M]
        kcmp = acc_hi1[:, 1544:1544 + M]
        rt = xs[0:NB, :, :, :].rearrange("p a b c -> p (a b c)").bitcast(F32)[:, 0:2 * NB + 5 * NSLOT]
        tri = rt[:, 0:NB]
        ones64 = rt[:, NB:2 * NB]
        onehot = rt[:, 2 * NB:2 * NB + 4 * NSLOT].rearrange("p (e s) -> p e s", e=E)
        siota = rt[:, 2 * NB + 4 * NSLOT:]
        wrep = ytmp[0:NB, 0:1, :].rearrange("p o (a c) -> p (o a) c", a=2)

        ps1 = [ctx.enter_context(nc.psum_tensor(f"ps_hidden{j}", [P, 512], F32)) for j in range(4)]
        psy = [ctx.enter_context(nc.psum_tensor(f"ps_out{j}", [P, 512], F32)) for j in range(2)]
        psg = ctx.enter_context(nc.psum_tensor("ps_small", [P, 512], F32))
        pst = ctx.enter_context(nc.psum_tensor("ps_turn", [P, 512], F32))

        def w1(e, part, db, hb):
            return W[:, bass.ds(e * WE + (part * 2048 + db * 1024 + hb * P), P)]

        def w2(e, part, hb, db):
            return W[:, bass.ds(e * WE + (4096 + part * 2048 + hb * D + db * P), P)]

        def fw(j, part, which, db):
            at = (part * 2 + which) * 2 * P + db * P
            if isinstance(j, int) and j == 0:
                return F0[:, at:at + P]
            return W[:, bass.ds((j - 1) * 1024 + (SH * WE + at), P)]

        x_in = [sem(f"x_in{q}") for q in range(8)]
        ws_in = [sem(f"ws_in{q}") for q in range(2)]
        small_in = sem("small_in")
        idx_in = sem("idx_in")
        wr_in = [sem(f"wr_in{q}") for q in range(2)]
        w_split = sem("w_split")
        x_split = sem("x_split")
        r_split = sem("r_split")
        const_ready = sem("const_ready")
        x_staged = sem("x_staged")
        l1_done = sem("l1_done")
        h32_ready = sem("h32_ready")
        h_hi = sem("h_hi")
        h_ready = sem("h_ready")
        y_done = sem("y_done")
        y_free = sem("y_free")
        y_scaled = sem("y_scaled")
        dv = sem("dv")
        cond_exp = sem("cond_exp")
        gate_in = sem("gate_in")
        gate_mm = sem("gate_mm")
        gate_log = sem("gate_log")
        gate_exp = sem("gate_exp")
        sel_ready = sem("sel_ready")
        rank_mm = sem("rank_mm")
        hot_ready = sem("hot_ready")
        tab_mm = sem("tab_mm")
        tab_ready = sem("tab_ready")
        sums_done = sem("sums_done")
        pool_step = sem("pool_step")

        block = ctx.enter_context(nc.Block())
        R0 = NS

        def piece_src(n):
            if n < 4 * E:
                e, k = (E - 1, 0, 1, 2)[n // 4], n % 4
                if k < 2:
                    return a["ew1"][e, k * P:(k + 1) * P, :]
                return a["ew2"][e, (k - 2) * 512:(k - 1) * 512, :].rearrange("(h p) d -> p h d", p=P)
            n -= 4 * E
            if n == 0:
                return a["fw"][:, 0:512]
            if n < 4:
                j0, j1 = ((0, 4), (4, 8), (8, 9))[n - 1]
                return a["w3t"][:, j0 * D:j1 * D]
            return a["fw"][:, 512 + (n - 4) * 1024:512 + (n - 3) * 1024]

        def piece_size(n):
            n -= 4 * E
            return {0: 512, 3: 256}.get(n, 1024)

        NPIECE = 4 * E + 4 + 4

        y_all = R0 + NR
        SW = W32[:, 0:E * WE // 2]

        def take(base, lo, shape, dt=F32):
            n = 1
            for s in shape:
                n *= s
            words = n if dt is not F16 else n // 2
            v = base[:, lo:lo + words]
            if dt is not F32:
                v = v.bitcast(dt)
            names = "abc"[:len(shape)]
            if len(shape) == 1:
                return v
            return v.rearrange(f"p ({' '.join(names)}) -> p {' '.join(names)}",
                               **{c: s for c, s in zip(names, shape)})

        gcs = take(SW, 0, [NK, 2, FC], F16)
        w3r = take(SW, 8704, [NJ, D])
        cg = take(SW, 11008, [MG, 4, P], F16)
        xg = take(SW, 12032, [MG, D])
        cgT = take(SW, 13056, [2 * DB, M], F16)
        tev = take(SW, 14080, [2, 1024], F16)
        moe = take(SW, 15104, [MG, D])
        hw = hbuf[:, :, :, :, :].rearrange("p a b c d -> p (a b c d)").bitcast(F32)
        s32 = take(hw, 0, [2, FC])
        x2 = take(hw, 1024, [2, FC])
        g32 = take(hw, 2048, [2, FC])
        ghl = take(hw, 3072, [2, 2, FC], F16)
        gc32 = h32[:, 0:2, :]
        sq = h32[:, 2:4, :]
        turned = pst[:, :].bitcast(F16)
        xrow = X[:, :, :].rearrange("p k t -> p (k t)").bitcast(F32)[:, 0:TOK // P * D] \
            .rearrange("p (n d) -> p n d", d=D)
        stf = stage[:, :, :].rearrange("p a b -> p (a b)")
        ident = stf[:, 0:P]
        id16 = take(stf, 512, [P], F16)
        betrep = stf[:, 128:256]
        betm = take(stf, 256, [FE, FE])
        onesm = stf[:, 320:448]
        Cm = take(stf, 448, [P], F16)
        b3s = stf[0:1, 1024:1280]
        b3e = stf[0:FE, 1280:1536]
        rwr = take(stf, 1536, [DB, 9])
        rws = take(stf, 1560, [2, DB, 10], F16)
        rb = stf[:, 1584:1593]
        eb = stf[:, 1600:1608]
        io8 = stf[:, 1608:1616]
        rlg = take(stf, 1616, [MG, 9])
        rsg = take(stf, 1656, [MG, 9])
        rsel = take(stf, 1696, [MG, FE])
        rcand = take(stf, 1728, [MG, FE])
        roh = take(stf, 1760, [MG, FE])
        rm = take(stf, 1792, [8, MG])
        rstd = take(stf, 1824, [NK, MG])
        rse = take(stf, 1896, [MG, FE])
        c0b = ytmp[:, 0, :]
        ce8 = ytmp[0:FE, 1, :]
        ohT = xs[0:FE, :, :, :].rearrange("p a b c -> p (a b c)").bitcast(F32)[:, 0:M] \
            .rearrange("p (g t) -> p g t", g=MG)

        misc_in, xg_in, cg_in = sem("misc_in"), sem("xg_in"), sem("cg_in")
        x_rows_in = [sem(f"x_rows_in{q}") for q in range(4)]
        w3_in = sem("w3_in")
        const2_ready = sem("const2_ready")
        c_hi, c_lo, c_lo_pool = sem("c_hi"), sem("c_lo"), sem("c_lo_pool")
        ab_done, s_ready, x2_ready = sem("ab_done"), sem("s_ready"), sem("x2_ready")
        g_made, g_hi, g_ready = sem("g_made"), sem("g_hi"), sem("g_ready")
        c_done, gc32_ready, gc_hi, gc_ready, sq_ready = (sem("c_done"), sem("gc32_ready"), sem("gc_hi"),
                                                        sem("gc_ready"), sem("sq_ready"))
        turn_done, turn_act, turn_dve = sem("turn_done"), sem("turn_act"), sem("turn_dve")
        row_out = [sem("row_out_act"), sem("row_out_dve")]
        back_done, cg_hi, cg_ready = sem("back_done"), sem("cg_hi"), sem("cg_ready")
        const_mm, rw_ready, router_mm, const_taken = (sem("const_mm"), sem("rw_ready"), sem("router_mm"),
                                                      sem("const_taken"))
        logit_ready, score_ready, diff_ready, mix_ready = (sem("logit_ready"), sem("score_ready"),
                                                           sem("diff_ready"), sem("mix_ready"))
        hot2_ready, hot_turned, hot_taken, pick_mm = (sem("hot2_ready"), sem("hot_turned"), sem("hot_taken"),
                                                      sem("pick_mm"))
        var_mm, var_ready, std_ready = sem("var_mm"), sem("var_ready"), sem("std_ready")
        u_done, u_free = sem("u_done"), sem("u_free")
        x_const, moe_step, out_done, scat_done = (sem("x_const"), sem("moe_step"), sem("out_done"),
                                                  sem("scat_done"))
        scratch = a["scratch"]

        def stage2_loads(sp):
            sp.wait_ge(r_split, NPIECE)
            for dst, src in ((b3s, a["b3s"]), (b3e, a["b3e"]), (rwr, a["rw"]),
                             (rb, a["rb"].partition_broadcast(P)), (eb, a["eb"].partition_broadcast(P))):
                sp.dma_start(dst, src).then_inc(misc_in, 16)
            sp.wait_ge(y_done, y_all)
            sp.dma_start(w3r, a["w3t"].rearrange("p (j d) -> p j d", d=D)).then_inc(w3_in, 16)
            rows = scratch.rearrange("(k s p) d -> p k s d", p=P, s=2)
            with sp.Fori(0, NQ) as k:
                for f, ready in enumerate((turn_act, turn_dve)):
                    sp.wait_ge(ready, k + 1)
                    sp.dma_start(rows[:, bass.ds(2 * k + f, 1), :, :].rearrange("p o s d -> p (o s) d"),
                                 tev[:, f, :].rearrange("p (s d) -> p s d", s=2)).then_inc(row_out[f], 16)
            sp.wait_ge(ab_done, 2 * NQ)
            for q in range(4):
                n = TOK // P // 4
                sp.dma_start(xrow[:, q * n:(q + 1) * n, :],
                             a["xR"][q * n * P:(q + 1) * n * P, :].rearrange("(n p) d -> p n d", p=P)) \
                    .then_inc(x_rows_in[q], 16)
            with sp.Fori(0, TOK // P // 2) as t:
                sp.wait_ge(u_free, t + 1)
                sp.dma_start(a["out"].rearrange("(t s p) d -> p t s d", p=P, s=2)
                             [:, bass.ds(t, 1), :, :].rearrange("p o s d -> p (o s) d"),
                             xrow[:, bass.ds(2 * t, 2), :]).then_inc(out_done, 16)
            sp.wait_ge(scat_done, 16 * MG)

        def pair_loop(eng, body):
            body(0)
            with by_two(eng, 2, NQ) as k:
                body(k)

        def stage2_act(act):
            act.wait_ge(y_free, y_all)
            act.wait_ge(x_staged, NR)

            def c_high(k):
                nc.scalar.activation(X[:, 0:DB, bass.ds(k * FC, FC)], acc[:, :, bass.ds(k * FC, FC)],
                                     ACT.Copy).then_inc(c_hi, 1)

            def factors(k, j, parity, first):
                act.wait_ge(ab_done, k * 2 + 1)
                if not first:
                    act.wait_ge(g_made, k - 1)
                nc.scalar.activation(s32[:, parity, :], ps1[2 * parity][:, :], ACT.Silu,
                                     bias=fb1[:, bass.ds(j, 1)], scale=1.0 / WS)
                act.wait_ge(ab_done, k * 2 + 2)
                nc.scalar.activation(x2[:, parity, :], ps1[2 * parity + 1][:, :], ACT.Identity,
                                     bias=fb2[:, bass.ds(j, 1)], scale=1.0 / WS).then_inc(x2_ready, 1)

            def centred(k, parity, first):
                act.wait_ge(c_done, k + 1)
                if not first:
                    act.wait_ge(gc_ready, k - 1)
                    act.wait_ge(sq_ready, k - 1)
                nc.scalar.activation(gc32[:, parity, :], psy[parity][:, :], ACT.Copy).then_inc(gc32_ready, 1)

            def body(k):
                first = isinstance(k, int) and k == 0
                for u in range(2):
                    factors(k + u, 0, u, first)
                    act.wait_ge(turn_done, (k + u) * 2 + 1)
                    if not (first and u == 0):
                        act.wait_ge(row_out[0], (k + u) * 16)
                    nc.scalar.activation(tev[:, 0, :], turned, ACT.Copy).then_inc(turn_act, 1)
                for u in range(2):
                    centred(k + u, u, first)

            c_high(0)
            c_high(1)
            with_next = [True]

            def body_next(k):
                c_high(k + 2)
                c_high(k + 3)
                body(k)

            body_next(0)
            with by_two(act, 2, NQ - 2) as k:
                body_next(k)
            with by_two(act, NQ - 2, NQ) as k:
                body(k)
            act.wait_ge(back_done, 1)
            nc.scalar.activation(cgT[:, 0:2, :], ps1[0][:, :].bitcast(F16).rearrange("p (n t) -> p n t", n=2),
                                 ACT.Copy).then_inc(cg_hi, 1)
            factors(NQ, 0, 0, False)
            centred(NQ, 0, False)
            with by_two(act, NQ + 1, NK) as k:
                for u in range(2):
                    factors(k + u, k + (u - NQ), 1 - u, False)
                for u in range(2):
                    centred(k + u, 1 - u, False)
            act.wait_ge(logit_ready, 1)
            nc.scalar.activation(rsg[:, :, :], rlg[:, :, :], ACT.Sigmoid).then_inc(score_ready, 1)
            act.wait_ge(diff_ready, 1)
            nc.scalar.activation(rm[:, 3, :], rm[:, 2, :], ACT.Sigmoid)
            nc.scalar.activation(rm[:, 4, :], rm[:, 2, :], ACT.Sigmoid, scale=-1.0).then_inc(mix_ready, 1)
            act.wait_ge(var_ready, 1)
            nc.scalar.activation(rstd[:, :, :], rstd[:, :, :], ACT.Sqrt).then_inc(std_ready, 1)

        def stage2_pe(pe):
            pe.wait_ge(y_free, y_all)
            pe.wait_ge(const2_ready, 1)

            def products(k, j, parity, rhs, first):
                if not first:
                    pe.wait_ge(x2_ready, k - 1)
                for which in range(2):
                    out = ps1[2 * parity + which][:, :]
                    n = 0
                    for wp, xp in ((0, 0), (0, 1), (1, 0)):
                        for db in range(DB):
                            mm = pe.matmul(out, fw(j, wp, which, db), rhs(xp, db), start=(n == 0), stop=(n == 5))
                            n += 1
                    mm.then_inc(ab_done, 1)

            def centre(k, parity, first):
                pe.wait_ge(g_ready, k + 1)
                if not first:
                    pe.wait_ge(gc32_ready, k - 1)
                for part in range(2):
                    mm = pe.matmul(psy[parity][:, :], Cm, ghl[:, parity, part, :], start=(part == 0), stop=(part == 1))
                mm.then_inc(c_done, 1)

            def turn(k, f, first):
                if f == 1:
                    pe.wait_ge(turn_act, k + 1)
                elif not first:
                    pe.wait_ge(turn_dve, k)
                for s in range(2):
                    for n in range(2 * DB):
                        mm = pe.transpose(turned[:, (4 * s + n) * P:(4 * s + n + 1) * P],
                                          X[:, n, bass.ds(k * FC + (2 * f + s) * P, P)], id16)
                mm.then_inc(turn_done, 1)

            def variance(k, parity):
                pe.wait_ge(sq_ready, k + 1)
                for g in range(MG):
                    mm = pe.matmul(psg[:, bass.ds(k * MG + g, 1)], sq[:, parity, g * P:(g + 1) * P],
                                   onesm[:, 0:1], start=True, stop=True)
                mm.then_inc(var_mm, 1)

            def body(k):
                first = isinstance(k, int) and k == 0
                for u in range(2):
                    if first:
                        pe.wait_ge(c_lo, u + 1)
                    else:
                        pe.wait_ge(c_lo_pool, k + (u - 1))
                    products(k + u, 0, u, lambda xp, db: X[:, 2 * xp + db, bass.ds((k + u) * FC, FC)], first)
                    turn(k + u, 0, first and u == 0)
                    turn(k + u, 1, first and u == 0)
                if not first:
                    variance(k - 2, 0)
                    variance(k - 1, 1)
                for u in range(2):
                    centre(k + u, u, first)

            pair_loop(pe, body)
            pe.wait_ge(w3_in, 16)
            pe.wait_ge(misc_in, 5 * 16)
            pe.wait_ge(turn_dve, NQ)
            pe.matmul(pst[:, 0:D], betrep, w3r[:, 0, :], start=True, stop=False)
            pe.matmul(pst[:, 0:D], onesm[0:1, :], b3s, start=False, stop=True)
            for e in range(FE):
                pe.matmul(pst[0:FE, D:2 * D], betm[:, e, :], w3r[:, 1 + e, :], start=(e == 0), stop=False)
            pe.matmul(pst[0:FE, D:2 * D], ident[0:FE, 0:FE], b3e, start=False, stop=True).then_inc(const_mm, 1)
            pe.wait_ge(cg_in, 16 * MG)
            pe.wait_ge(x2_ready, NQ)
            for n in range(2 * DB):
                for g in range(MG):
                    mm = pe.transpose(ps1[n // 2][:, :].bitcast(F16)[:, (n % 2) * M + g * P:(n % 2) * M + (g + 1) * P],
                                      cg[:, g, n, :], id16)
                if n % 2 == 1:
                    mm.then_inc(back_done, 1)
            pe.wait_ge(cg_hi, 1)
            pe.wait_ge(cg_ready, 1)
            gathered = lambda xp, db: cgT[:, 2 * xp + db, :]
            products(NQ, 0, 0, gathered, False)
            pe.wait_ge(rw_ready, 1)
            pe.wait_ge(const_taken, 1)
            for g in range(MG):
                n = 0
                for xp, wp in ((0, 0), (0, 1), (1, 0)):
                    for db in range(DB):
                        mm = pe.matmul(pst[:, g * 9:(g + 1) * 9], cgT[:, 2 * xp + db, g * P:(g + 1) * P],
                                       rws[:, wp, db, 0:9], start=(n == 0), stop=(n == 5))
                        n += 1
            mm.then_inc(router_mm, 1)
            variance(NQ - 2, 0)
            centre(NQ, 0, False)
            with by_two(pe, NQ + 1, NK) as k:
                for u in range(2):
                    products(k + u, k + (u - NQ), 1 - u, gathered, False)
                variance(k - 2, 1)
                variance(k - 1, 0)
                for u in range(2):
                    centre(k + u, 1 - u, False)
            pe.wait_ge(hot2_ready, 1)
            for g in range(MG):
                mm = pe.transpose(pst[0:FE, g * P:(g + 1) * P], roh[:, g, :], ident)
            mm.then_inc(hot_turned, 1)
            variance(NK - 2, 1)
            variance(NK - 1, 0)

            def last(bank, s, k, g, j):
                out = bank[:, s * D:(s + 1) * D]
                for n, (gp, vp) in enumerate(((0, 0), (0, 1), (1, 0))):
                    mm = pe.matmul(out, gcs[:, bass.ds(k, 1), gp, bass.ds(g * P, P)].rearrange("p o t -> p (o t)"),
                                   V[:, bass.ds(j, 1), vp, :].rearrange("p o d -> p (o d)"),
                                   start=(n == 0), stop=(n == 2))
                return mm

            pe.wait_ge(gc_ready, NK)
            def main_last(q, first):
                for f in range(4):
                    if not first:
                        pe.wait_ge(u_free, q * 2 + (f - 3))
                    for s in range(2):
                        mm = last(ps1[f], s, q + f // 2, 2 * (f % 2) + s, 0)
                    mm.then_inc(u_done, 1)
            main_last(0, True)
            with by_two(pe, 2, NQ) as q:
                main_last(q, False)
            base = 2 * NQ

            def moe_last(j, parity):
                for f in range(2):
                    pe.wait_ge(u_free, j * 2 + (base + f - 3))
                    for s in range(2):
                        mm = last(ps1[2 * parity + f], s, j + NQ, 2 * f + s, j)
                    mm.then_inc(u_done, 1)

            moe_last(0, 0)
            pe.wait_ge(hot_taken, 1)
            for g in range(MG):
                mm = pe.matmul(psy[g // 2][:, (g % 2) * D:(g % 2 + 1) * D], ohT[:, g, :], ce8, start=True, stop=True)
            mm.then_inc(pick_mm, 1)
            with by_two(pe, 1, NJ) as j:
                moe_last(j, 1)
                moe_last(j + 1, 0)

        def stage2_dve(dve, link):
            dve.wait_ge(y_free, y_all)

            def c_low(k):
                cols = slice(k * FC, (k + 1) * FC)
                dve.wait_ge(c_hi, k + 1)
                nc.vector.tensor_tensor(X[:, DB:2 * DB, cols], acc[:, :, cols], X[:, 0:DB, cols],
                                        ALU.subtract).then_inc(c_lo, 1)

            def gate_product(k, parity, first):
                dve.wait_ge(x2_ready, k + 1)
                nc.vector.tensor_tensor(g32[:, parity, :], s32[:, parity, :], x2[:, parity, :],
                                        ALU.mult).then_inc(g_made, 1)
                dve.wait_ge(g_made, k + 1)
                if not first:
                    dve.wait_ge(c_done, k - 1)
                nc.vector.tensor_copy(ghl[:, parity, 0, :], g32[:, parity, :]).then_inc(g_hi, 1)
                dve.wait_ge(g_hi, k + 1)
                nc.vector.tensor_tensor(ghl[:, parity, 1, :], g32[:, parity, :], ghl[:, parity, 0, :],
                                        ALU.subtract).then_inc(g_ready, 1)

            def keep(k, parity):
                dve.wait_ge(gc32_ready, k + 1)
                out = [gcs[:, bass.ds(k, 1), part, :].rearrange("p o t -> p (o t)") for part in range(2)]
                nc.vector.tensor_copy(out[0], gc32[:, parity, :]).then_inc(gc_hi, 1)
                dve.wait_ge(gc_hi, k + 1)
                nc.vector.tensor_tensor(out[1], gc32[:, parity, :], out[0], ALU.subtract).then_inc(gc_ready, 1)

            def body(k):
                first = isinstance(k, int) and k == 0
                for u in range(2):
                    gate_product(k + u, u, first)
                    dve.wait_ge(turn_done, (k + u) * 2 + 2)
                    if not (first and u == 0):
                        dve.wait_ge(row_out[1], (k + u) * 16)
                    nc.vector.tensor_copy(tev[:, 1, :], turned).then_inc(turn_dve, 1)
                for u in range(2):
                    keep(k + u, u)

            c_low(0)
            c_low(1)
            pair_loop(dve, body)
            dve.wait_ge(const_mm, 1)
            link(nc.vector.tensor_copy(c0b, pst[:, 0:D]))
            nc.vector.tensor_copy(ce8, pst[0:FE, D:2 * D]).then_inc(const_taken, 1)
            link(nc.vector.tensor_scalar(rws[:, 0, :, 0:9], rwr, WS, None, ALU.mult))
            nc.vector.scalar_tensor_tensor(rws[:, 1, :, 0:9], rwr, WS, rws[:, 0, :, 0:9],
                                           ALU.mult, ALU.subtract).then_inc(rw_ready, 1)
            dve.wait_ge(back_done, 2)
            nc.vector.tensor_copy(cgT[:, 2:4, :], ps1[1][:, :].bitcast(F16)
                                  .rearrange("p (n t) -> p n t", n=2)).then_inc(cg_ready, 1)
            gate_product(NQ, 0, False)
            keep(NQ, 0)
            dve.wait_ge(router_mm, 1)
            nc.vector.scalar_tensor_tensor(rlg[:, :, :], pst[:, 0:MG * 9].rearrange("p (g e) -> p g e", e=9),
                                           1.0 / WS, rb.unsqueeze(1).to_broadcast([P, MG, 9]),
                                           ALU.mult, ALU.add).then_inc(logit_ready, 1)
            with by_two(dve, NQ + 1, NK) as k:
                for u in range(2):
                    gate_product(k + u, 1 - u, False)
                for u in range(2):
                    keep(k + u, 1 - u)
            dve.wait_ge(score_ready, 1)

            def over_e(v):
                return v.unsqueeze(2).to_broadcast([P, MG, FE])

            iob = io8.unsqueeze(1).to_broadcast([P, MG, FE])
            link(nc.vector.tensor_tensor(rsel, rsg[:, :, 1:9], eb.unsqueeze(1).to_broadcast([P, MG, FE]), ALU.add))
            link(nc.vector.tensor_reduce(rm[:, 0, :], rsel, AX.X, ALU.max))
            link(nc.vector.tensor_tensor(rcand, rsel, over_e(rm[:, 0, :]), ALU.is_equal))
            link(nc.vector.tensor_tensor(rcand, rcand, iob, ALU.mult))
            link(nc.vector.tensor_reduce(rm[:, 1, :], rcand, AX.X, ALU.min))
            nc.vector.tensor_tensor(roh, iob, over_e(rm[:, 1, :]), ALU.is_equal).then_inc(hot2_ready, 1)
            dve.wait_ge(hot2_ready, 1)
            link(nc.vector.tensor_tensor(rcand, roh, rsg[:, :, 1:9], ALU.mult))
            link(nc.vector.tensor_reduce(rm[:, 5, :], rcand, AX.X, ALU.add))
            nc.vector.tensor_tensor(rm[:, 2, :], rsg[:, :, 0], rm[:, 5, :], ALU.subtract).then_inc(diff_ready, 1)
            dve.wait_ge(hot_turned, 1)
            nc.vector.tensor_copy(ohT, pst[0:FE, :].rearrange("p (g t) -> p g t", g=MG)).then_inc(hot_taken, 1)
            dve.wait_ge(mix_ready, 1)
            dve.wait_ge(var_mm, NK)
            nc.vector.tensor_scalar(rstd[:, :, :], psg[:, 0:NK * MG].rearrange("p (k g) -> p k g", g=MG),
                                    1.0 / FH, EPS, ALU.mult, ALU.add).then_inc(var_ready, 1)
            dve.wait_ge(std_ready, 1)
            link(nc.vector.reciprocal(rstd[:, :, :], rstd[:, :, :]))
            link(nc.vector.tensor_scalar(rstd[:, :, :], rstd[:, :, :], 1.0 / WS, None, ALU.mult))
            link(nc.vector.tensor_tensor(rse, roh, over_e(rm[:, 4, :]), ALU.mult))
            link(nc.vector.tensor_tensor(rse, rse, rstd[:, NQ + 1:NK, :].rearrange("p e g -> p g e"), ALU.mult))
            rflat = rstd.rearrange("p k g -> p (k g)")
            with dve.Fori(0, 4) as q:
                dve.wait_ge(x_const, q + 1)
                for f in range(4):
                    dve.wait_ge(u_done, q * 4 + (f + 1))
                    for s in range(2):
                        row = xrow[:, bass.ds(q * 8 + (2 * f + s), 1), :].rearrange("p o d -> p (o d)")
                        i = nc.vector.scalar_tensor_tensor(row, ps1[f][:, s * D:(s + 1) * D],
                                                           rflat[:, bass.ds(q * 8 + (2 * f + s), 1)], row,
                                                           ALU.mult, ALU.add)
                    i.then_inc(u_free, 1)
            dve.wait_ge(xg_in, 16 * MG)
            for g in range(MG):
                if g % 2 == 0:
                    dve.wait_ge(u_done, 2 * NQ + g // 2 + 1)
                i = nc.vector.scalar_tensor_tensor(moe[:, g, :], ps1[g // 2][:, (g % 2) * D:(g % 2 + 1) * D],
                                                   rstd[:, NQ, g:g + 1], c0b, ALU.mult, ALU.add)
                if g % 2 == 1:
                    i.then_inc(u_free, 1)
            dve.wait_ge(u_free, 2 * NQ + 2)
            for g in range(MG):
                i = nc.vector.scalar_tensor_tensor(moe[:, g, :], moe[:, g, :], rm[:, 3, g:g + 1], xg[:, g, :],
                                                   ALU.mult, ALU.add)
            i.then_inc(moe_step, 1)
            dve.wait_ge(moe_step, 1)
            dve.wait_ge(pick_mm, 1)
            for g in range(MG):
                i = nc.vector.scalar_tensor_tensor(moe[:, g, :], psy[g // 2][:, (g % 2) * D:(g % 2 + 1) * D],
                                                   rm[:, 4, g:g + 1], moe[:, g, :], ALU.mult, ALU.add)
            i.then_inc(moe_step, 1)
            dve.wait_ge(moe_step, 2)
            sflat = rse.rearrange("p g e -> p (g e)")
            with by_two(dve, 1, NJ) as j:
                for u in range(2):
                    dve.wait_ge(u_free, j * 2 + (2 * NQ + 2 * u))
                    for g in range(MG):
                        if g % 2 == 0:
                            dve.wait_ge(u_done, j * 2 + (2 * NQ + 2 * u + g // 2 + 1))
                        bank = ps1[2 * (1 - u) + g // 2]
                        i = nc.vector.scalar_tensor_tensor(moe[:, g, :], bank[:, (g % 2) * D:(g % 2 + 1) * D],
                                                           sflat[:, bass.ds(j + (g * FE + u - 1), 1)],
                                                           moe[:, g, :], ALU.mult, ALU.add)
                        if g == 1:
                            i.then_inc(u_free, 1)
                    i.then_inc(u_free, 1)

        def stage2_pool(pool, link):
            link(nc.gpsimd.memset(onesm, 1.0))
            link(nc.gpsimd.affine_select(out=ident, in_=onesm, compare_op=ALU.is_equal, fill=0.0,
                                         base=0, pattern=[[1, P]], channel_multiplier=-1))
            link(nc.gpsimd.tensor_copy(id16, ident))
            link(nc.gpsimd.tensor_scalar(Cm, ident, -1.0 / FH, None, ALU.add))
            link(nc.gpsimd.tensor_scalar(betrep, onesm, bet[:, 0:1], None, ALU.mult))
            link(nc.gpsimd.memset(betm[:, :, :], 0.0))
            for e in range(FE):
                link(nc.gpsimd.tensor_copy(betm[:, e, e:e + 1], bet[:, 1:2]))
            nc.gpsimd.iota(io8, pattern=[[1, FE]], base=-FE, channel_multiplier=0,
                           allow_small_or_imprecise_dtypes=True).then_inc(const2_ready, 1)
            pool.wait_ge(y_free, y_all)
            for g in range(MG):
                nc.gpsimd.indirect_dma_start(
                    out=xg[:, g, :], out_offset=None, in_=a["xR"],
                    in_offset=bass.IndirectOffsetOnAxis(ap=gid[:, g:g + 1], axis=0)).then_inc(xg_in, 16)

            def c_low(k):
                pool.wait_ge(c_hi, k + 1)
                cols = bass.ds(k * FC, FC)
                nc.gpsimd.tensor_tensor(X[:, DB:2 * DB, cols], acc[:, :, cols], X[:, 0:DB, cols],
                                        ALU.subtract).then_inc(c_lo_pool, 1)

            def squares(k, parity):
                pool.wait_ge(gc32_ready, k + 1)
                if not (isinstance(k, int) and k < 2):
                    pool.wait_ge(var_mm, k - 1)
                nc.gpsimd.tensor_tensor(sq[:, parity, :], gc32[:, parity, :], gc32[:, parity, :],
                                        ALU.mult).then_inc(sq_ready, 1)

            def body(k):
                c_low(k + 2)
                c_low(k + 3)
                squares(k, 0)
                squares(k + 1, 1)

            body(0)
            with by_two(pool, 2, NQ - 2) as k:
                body(k)
            squares(NQ - 2, 0)
            squares(NQ - 1, 1)
            for f in range(2):
                pool.wait_ge(row_out[f], 16 * NQ)
            for g in range(MG):
                nc.gpsimd.indirect_dma_start(
                    out=cg[:, g, :, :].rearrange("p n d -> p (n d)"), out_offset=None, in_=scratch,
                    in_offset=bass.IndirectOffsetOnAxis(ap=gid[:, g:g + 1], axis=0)).then_inc(cg_in, 16)
            pool.wait_ge(const_taken, 1)
            squares(NQ, 0)
            for q in range(4):
                squares(NQ + 1 + 2 * q, 1)
                squares(NQ + 2 + 2 * q, 0)
                pool.wait_ge(x_rows_in[q], 16)
                rows = xrow[:, q * 8:(q + 1) * 8, :]
                nc.gpsimd.tensor_tensor(rows, rows, c0b.unsqueeze(1).to_broadcast([P, 8, D]),
                                        ALU.add).then_inc(x_const, 1)
            pool.wait_ge(out_done, 16 * 2 * NQ)
            pool.wait_ge(u_free, 2 * NQ + 2 * NJ)
            for g in range(MG):
                nc.gpsimd.indirect_dma_start(
                    out=a["out"], out_offset=bass.IndirectOffsetOnAxis(ap=sid[:, g:g + 1], axis=0),
                    in_=moe[:, g, :], in_offset=None, bounds_check=TOK - 1,
                    oob_is_err=False).then_inc(scat_done, 16)
            pool.wait_ge(scat_done, 16 * MG)

        @block.sync
        def _(sp):
            sp.dma_start(ws32[:, 0:2048].rearrange("p (k h) -> p k h", k=DB),
                         a["sw1"].rearrange("(k p) h -> p k h", p=P)).then_inc(ws_in[0], 16)
            sp.dma_start(x32[:, :, 0:512], a["xT"][:, :, 0:512]).then_inc(x_in[0], 16)
            sp.dma_start(b1[:, :], a["b1"]).then_inc(small_in, 16)
            sp.dma_start(ws32[:, 2048:4096].rearrange("p (k h) -> p k h", k=HB),
                         a["sw2"].rearrange("(k p) h -> p k h", p=P)).then_inc(ws_in[1], 16)
            for q in range(1, 8):
                sp.dma_start(x32[:, :, q * 512:(q + 1) * 512],
                             a["xT"][:, :, q * 512:(q + 1) * 512]).then_inc(x_in[q], 16)
            for n in range(NPIECE):
                if n >= 2:
                    sp.wait_ge(r_split, n - 1)
                src = piece_src(n)
                dst = stage[:, n % 2, 0:piece_size(n)]
                if len(src.shape) == 3:
                    dst = dst.rearrange("p (h d) -> p h d", d=D)
                sp.dma_start(dst, src).then_inc(wr_in[n % 2], 16)
            stage2_loads(sp)

        @block.scalar
        def _(act):
            act.dma_start(cond[:, :, :], a["condT"]).then_inc(small_in, 16)
            act.dma_start(b2[:, :], a["b2"]).then_inc(small_in, 16)
            act.dma_start(gw[:, :, :], a["gate_w"].rearrange("(k p) e -> p k e", p=P)).then_inc(small_in, 16)
            act.dma_start(tw[:, :, :], a["time_w"].rearrange("(k p) e -> p k e", p=P)).then_inc(small_in, 16)
            act.dma_start(gb[:, :], a["gate_b"].partition_broadcast(NB)).then_inc(small_in, 16)
            act.dma_start(tb[:, :], a["time_b"].partition_broadcast(NB)).then_inc(small_in, 16)
            act.dma_start(fb1[:, :], a["fb1"]).then_inc(small_in, 16)
            act.dma_start(fb2[:, :], a["fb2"]).then_inc(small_in, 16)
            act.dma_start(gam[:, :], a["gam"]).then_inc(small_in, 16)
            act.dma_start(bet[:, :], a["bet"]).then_inc(small_in, 16)
            act.dma_start(kint[:, 0, 0:M], a["index_b"].partition_broadcast(P)).then_inc(idx_in, 16)
            act.dma_start(kint[:, 1, 0:M], a["index_t"].partition_broadcast(P)).then_inc(idx_in, 16)
            act.dma_start(kint[:, 0, M:M + MG], a["index_b4"]).then_inc(idx_in, 16)
            act.dma_start(kint[:, 1, M:M + MG], a["index_t4"]).then_inc(idx_in, 16)
            act.wait_ge(small_in, 11 * 16)
            nc.scalar.activation(silc[:, :, :], cond[:, :, :], ACT.Exp, scale=-1.0).then_inc(cond_exp, 1)

            def gelus(g, e):
                first = isinstance(g, int) and g == 0
                for j in range(4):
                    act.wait_ge(l1_done, g * 4 + (j + 1))
                    if not first:
                        act.wait_ge(h_ready, g * 4 + (j - 3))
                    for k in range(2):
                        hb = 2 * j + k
                        i = nc.scalar.activation(
                            h32[:, j, k * CH:(k + 1) * CH], ps1[j][:, k * CH:(k + 1) * CH],
                            ACT.Gelu_apprx_tanh, bias=b1[:, bass.ds(e * HB + hb, 1)], scale=1.0 / WS)
                    i.then_inc(h32_ready, 1)

            def store(g, parity):
                act.wait_ge(y_done, g + 1)
                for db in range(DB):
                    i = nc.scalar.activation(
                        acc[:, db, bass.ds(g * CH, CH)], psy[parity][:, db * CH:(db + 1) * CH],
                        ACT.Identity, bias=b2[:, SH * DB + db:SH * DB + db + 1], scale=1.0 / WS)
                i.then_inc(y_free, 1)

            gelus(0, SH)
            gelus(1, SH)
            store(0, 0)
            gelus(2, SH)
            store(1, 1)
            with by_two(act, 2, 10) as g:
                for u in range(2):
                    gelus(g + (u + 1), SH)
                    store(g + u, u)
            act.wait_ge(gate_log, 1)
            nc.scalar.activation(G[:, 4, :], G[:, 2, :], ACT.Exp, bias=G[:, 3, 0:1]).then_inc(gate_exp, 1)
            for g in range(10, NS - 1):
                gelus(g + 1, SH)
                store(g, g % 2)

            def expert_gelus(g):
                e = act.value_load(tab[0:1, bass.ds(g * 8 + (4 - R0 * 8), 1)], min_val=0, max_val=E - 1)
                gelus(g, e)

            act.wait_ge(tab_ready, 1)
            expert_gelus(R0)
            store(NS - 1, 1)
            with act.Fori(R0 + 1, R0 + NR) as g:
                expert_gelus(g)
            stage2_act(act)

        @block.tensor
        def _(pe):
            def hidden(g, e, rhs):
                first = isinstance(g, int) and g == 0
                for j in range(4):
                    if not first:
                        pe.wait_ge(h32_ready, g * 4 + (j - 3))
                    for k in range(2):
                        hb = 2 * j + k
                        out = ps1[j][:, k * CH:(k + 1) * CH]
                        n = 0
                        for wp, xp in ((0, 0), (0, 1), (1, 0)):
                            for db in range(DB):
                                mm = pe.matmul(out, w1(e, wp, db, hb), rhs(xp, db),
                                               start=(n == 0), stop=(n == 5))
                                n += 1
                    mm.then_inc(l1_done, 1)

            def hidden_shared(g, parity=None):
                if isinstance(g, int):
                    if g % 2 == 0 and g >= 2:
                        pe.wait_ge(x_split, g // 2)
                    lo = g * CH
                    hidden(g, SH, lambda xp, db: X[:, 2 * xp + db, lo:lo + CH])
                else:
                    hidden(g, SH, lambda xp, db: X[:, 2 * xp + db, bass.ds(g * CH, CH)])

            def hidden_expert(g, parity):
                pe.wait_ge(x_staged, g - (R0 - 1))
                e = pe.value_load(tab[0:1, bass.ds(g * 8 + (4 - R0 * 8), 1)], min_val=0, max_val=E - 1)
                hidden(g, e, lambda xp, db: xs[:, parity, 2 * xp + db, :])
                return e

            def output(g, e, parity):
                if not (isinstance(g, int) and g < 2):
                    pe.wait_ge(y_free, g - 1)
                pe.wait_ge(h_ready, g * 4 + 4)
                for db in range(DB):
                    out = psy[parity][:, db * CH:(db + 1) * CH]
                    n = 0
                    for hb in range(HB):
                        for wp, hp in ((0, 0), (0, 1), (1, 0)):
                            mm = pe.matmul(out, w2(e, wp, hb, db), hbuf[:, parity, hp, hb, :],
                                           start=(n == 0), stop=(n == 3 * HB - 1))
                            n += 1
                mm.then_inc(y_done, 1)

            pe.wait_ge(w_split, 2)
            hidden_shared(0)
            hidden_shared(1)
            pe.wait_ge(w_split, 3)
            output(0, SH, 0)
            hidden_shared(2)
            output(1, SH, 1)
            with pe.Fori(1, 5) as q:
                hidden_shared(q * 2 + 1)
                output(q * 2, SH, 0)
                pe.wait_ge(x_split, q + 1)
                hidden_shared(q * 2 + 2)
                output(q * 2 + 1, SH, 1)
            pe.wait_ge(gate_in, 1)
            for k in range(3 * DB):
                pe.matmul(psg[0:NB, 0:E], gin[:, k, :], gw[:, k, :], start=(k == 0), stop=(k == 3 * DB - 1))
            for k in range(DB):
                mm = pe.matmul(psg[0:NB, 8:8 + 2 * E], silc[:, k, :], tw[:, k, :], start=(k == 0), stop=(k == DB - 1))
            mm.then_inc(gate_mm, 1)
            hidden_shared(11)
            output(10, SH, 0)
            pe.wait_ge(sel_ready, 1)
            pe.matmul(psg[0:NB, 0:E], tri, G[:, 9, :], start=True, stop=True)
            pe.matmul(psg[0:NB, 8:8 + E], ones64, G[:, 9, :], start=True, stop=True).then_inc(rank_mm, 1)
            hidden_shared(12)
            output(11, SH, 1)
            pe.wait_ge(hot_ready, 1)
            for e in range(E):
                pe.matmul(psg[0:1, 0:NSLOT], G[:, 21, 0:1], onehot[:, e, :], start=(e == 0), stop=(e == E - 1))
            for e in range(E):
                pe.matmul(psg[0:1, NSLOT:2 * NSLOT], ones64[:, 0:1], onehot[:, e, :], start=(e == 0), stop=(e == E - 1))
            for e in range(E):
                pe.wait_ge(hot_ready, e + 2)
                mm = pe.matmul(psg[:, 2 * NSLOT:3 * NSLOT], wrep[:, e % 2, :], onehot[:, e, :],
                               start=(e == 0), stop=(e == E - 1))
                mm.then_inc(tab_mm, 1)
            for g in range(12, NS - 1):
                hidden_shared(g + 1)
                output(g, SH, g % 2)
            pe.wait_ge(r_split, 4 * E)
            hidden_expert(R0, 0)
            output(NS - 1, SH, 1)
            with by_two(pe, R0, R0 + NR - 1) as g:
                for u in range(2):
                    e_now = pe.value_load(tab[0:1, bass.ds((g + u) * 8 + (4 - R0 * 8), 1)], min_val=0, max_val=E - 1)
                    hidden_expert(g + (u + 1), 1 - u)
                    output(g + u, e_now, u)
            e_now = pe.value_load(tab[0:1, (NR - 1) * 8 + 4:(NR - 1) * 8 + 5], min_val=0, max_val=E - 1)
            output(R0 + NR - 1, e_now, 0)
            stage2_pe(pe)

        @block.vector
        def _(dve):
            steps = [0]

            def link(i):
                steps[0] += 1
                i.then_inc(dv, 1)
                dve.wait_ge(dv, steps[0])

            def split_shared(k, lo, n, part_off):
                src = ws32[:, lo:lo + n]
                hi = W[:, SH * WE + part_off:SH * WE + part_off + n]
                low = W[:, SH * WE + part_off + 2048:SH * WE + part_off + 2048 + n]
                dve.wait_ge(ws_in[k], 16)
                link(nc.vector.tensor_scalar(hi, src, WS, None, ALU.mult))
                return nc.vector.scalar_tensor_tensor(low, src, WS, hi, ALU.mult, ALU.subtract)

            split_shared(0, 0, 2048, 0).then_inc(w_split, 1)
            dve.wait_ge(x_in[0], 16)
            link(nc.vector.tensor_copy(X[:, 0:DB, 0:512], x32[:, :, 0:512]))
            nc.vector.tensor_tensor(X[:, DB:2 * DB, 0:512], x32[:, :, 0:512], X[:, 0:DB, 0:512],
                                    ALU.subtract).then_inc(w_split, 1)
            split_shared(1, 2048, 2048, 4096).then_inc(w_split, 1)

            def splits(g, parity):
                if not (isinstance(g, int) and g < 2):
                    dve.wait_ge(y_done, g - 1)
                for j in range(4):
                    dve.wait_ge(h32_ready, g * 4 + (j + 1))
                    src = h32[:, j, :].rearrange("p (k t) -> p k t", k=2)
                    hi = hbuf[:, parity, 0, 2 * j:2 * j + 2, :]
                    nc.vector.tensor_copy(hi, src).then_inc(h_hi, 1)
                    dve.wait_ge(h_hi, g * 4 + (j + 1))
                    nc.vector.tensor_tensor(hbuf[:, parity, 1, 2 * j:2 * j + 2, :], src, hi,
                                            ALU.subtract).then_inc(h_ready, 1)

            def sums(q):
                dve.wait_ge(x_in[q], 16)
                v = x32[:, :, q * 512:(q + 1) * 512].rearrange("p d (b t) -> p d b t", t=NT)
                for r, (lo, hi) in enumerate(((0, HEAD), (HEAD, HP), (HP, NT))):
                    i = nc.vector.tensor_reduce(gsum[:, :, r, q * 8:(q + 1) * 8], v[:, :, :, lo:hi],
                                                AX.X, ALU.add)
                i.then_inc(sums_done, 1)

            splits(0, 0)
            for q in range(4):
                sums(q)
            splits(1, 1)
            for q in range(4, 8):
                sums(q)
            dve.wait_ge(sums_done, 8)
            link(nc.vector.tensor_tensor(gin[:, DB:2 * DB, :], gsum[:, :, 0, :], gsum[:, :, 1, :], ALU.add))
            link(nc.vector.tensor_tensor(gin[:, 0:DB, :], gin[:, DB:2 * DB, :], gsum[:, :, 2, :], ALU.add))
            link(nc.vector.tensor_tensor(gin[:, 2 * DB:3 * DB, :], gsum[:, :, 2, :], gsum[:, :, 1, :], ALU.add))
            link(nc.vector.tensor_scalar(gin[:, 0:DB, :], gin[:, 0:DB, :], 1.0 / NT, None, ALU.mult))
            link(nc.vector.tensor_scalar(gin[:, DB:3 * DB, :], gin[:, DB:3 * DB, :], 1.0 / HP, None, ALU.mult))
            dve.wait_ge(cond_exp, 1)
            link(nc.vector.tensor_scalar(silc[:, :, :], silc[:, :, :], 1.0, None, ALU.add))
            link(nc.vector.reciprocal(silc[:, :, :], silc[:, :, :]))
            nc.vector.tensor_tensor(silc[:, :, :], silc[:, :, :], cond[:, :, :], ALU.mult).then_inc(gate_in, 1)
            link(nc.vector.tensor_scalar(b2s[:, :], b2[:, :], WS, None, ALU.mult))
            splits(2, 0)
            dve.wait_ge(idx_in, 4 * 16)
            dve.wait_ge(const_ready, 1)
            link(nc.vector.tensor_copy(kidx, kint))
            link(nc.vector.tensor_scalar(ktmp, kidx, 0.0, float(NT), ALU.is_lt, ALU.mult))
            link(nc.vector.tensor_tensor(kidx, kidx, ktmp, ALU.add))
            link(nc.vector.tensor_scalar(ktmp, kidx, float(NT - 1), None, ALU.is_le))
            link(nc.vector.scalar_tensor_tensor(ktmp, kidx, 0.0, ktmp, ALU.is_ge, ALU.mult))
            ok, kb, kt = ktmp[:, 0, :], kidx[:, 0, :], kidx[:, 1, :]
            link(nc.vector.tensor_tensor(ok, ktmp[:, 0, :], ktmp[:, 1, :], ALU.mult))
            link(nc.vector.scalar_tensor_tensor(kb, kb, float(NT), kt, ALU.mult, ALU.add))
            link(nc.vector.tensor_scalar(ktmp[:, 1, :], kt, float(HEAD), float(NT - 2 * HEAD), ALU.is_ge, ALU.mult))
            link(nc.vector.tensor_tensor(kb, kb, ktmp[:, 1, :], ALU.add))
            link(nc.vector.tensor_scalar(ktmp[:, 1, :], kt, float(2 * HEAD), -float(NT - HEAD), ALU.is_ge, ALU.mult))
            link(nc.vector.tensor_tensor(kb, kb, ktmp[:, 1, :], ALU.add))
            link(nc.vector.scalar_tensor_tensor(kb, kb, -2.0 * TOK, ok, ALU.add, ALU.mult))
            for m in range(MG):
                link(nc.vector.scalar_tensor_tensor(kcmp, kb[:, 0:M], kb[:, M + m:M + m + 1], iot,
                                                    ALU.is_equal, ALU.mult))
                link(nc.vector.tensor_reduce(f4[:, 0, m:m + 1], kcmp, AX.X, ALU.min))
            own = kb[:, M:M + MG]
            link(nc.vector.tensor_tensor(f4[:, 2, :], f4[:, 0, :], f4[:, 1, :], ALU.is_equal))
            link(nc.vector.tensor_tensor(f4[:, 3, :], f4[:, 2, :], own, ALU.mult))
            link(nc.vector.tensor_scalar(f4[:, 4, :], f4[:, 3, :], 2.0 * TOK, None, ALU.add))
            link(nc.vector.tensor_copy(sid[:, :], f4[:, 4, :]))
            link(nc.vector.tensor_scalar(f4[:, 5, :], f4[:, 4, :], float(TOK), None, ALU.is_lt))
            link(nc.vector.tensor_tensor(f4[:, 6, :], f4[:, 5, :], f4[:, 4, :], ALU.mult))
            link(nc.vector.tensor_copy(gid[:, :], f4[:, 6, :]))

            with by_two(dve, 3, 11) as g:
                splits(g, 1)
                splits(g + 1, 0)
            dve.wait_ge(gate_mm, 1)
            link(nc.vector.tensor_tensor(G[:, 0, :], psg[0:NB, 0:E], gb[:, :], ALU.add))
            link(nc.vector.tensor_tensor(G[:, 1, :], psg[0:NB, 8:8 + E], tb[:, 0:E], ALU.add))
            link(nc.vector.tensor_tensor(G[:, 5, :], psg[0:NB, 8 + E:8 + 2 * E], tb[:, E:2 * E], ALU.add))
            link(nc.vector.scalar_tensor_tensor(G[:, 2, :], G[:, 1, :], 1.0, G[:, 0, :], ALU.add, ALU.mult))
            link(nc.vector.tensor_tensor(G[:, 2, :], G[:, 2, :], G[:, 5, :], ALU.add))
            link(nc.vector.tensor_reduce(G[:, 3, 1:2], G[:, 2, :], AX.X, ALU.max))
            nc.vector.tensor_scalar(G[:, 3, 0:1], G[:, 3, 1:2], -1.0, None, ALU.mult).then_inc(gate_log, 1)
            dve.wait_ge(gate_exp, 1)
            link(nc.vector.tensor_reduce(G[:, 3, 2:3], G[:, 4, :], AX.X, ALU.add))
            link(nc.vector.reciprocal(G[:, 3, 3:4], G[:, 3, 2:3]))
            link(nc.vector.tensor_scalar(G[:, 6, :], G[:, 4, :], G[:, 3, 3:4], None, ALU.mult))
            for n, (score, hot) in enumerate(((6, 7), (10, 8))):
                link(nc.vector.tensor_reduce(G[:, 11, n:n + 1], G[:, score, :], AX.X, ALU.max))
                link(nc.vector.scalar_tensor_tensor(G[:, 12, :], G[:, score, :], G[:, 11, n:n + 1], G[:, 20, :],
                                                    ALU.is_equal, ALU.mult))
                link(nc.vector.tensor_reduce(G[:, 13, n:n + 1], G[:, 12, :], AX.X, ALU.min))
                link(nc.vector.tensor_scalar(G[:, hot, :], G[:, 20, :], G[:, 13, n:n + 1], None, ALU.is_equal))
                if n == 0:
                    link(nc.vector.scalar_tensor_tensor(G[:, 10, :], G[:, 7, :], -2.0, G[:, 6, :],
                                                        ALU.mult, ALU.add))
            nc.vector.tensor_tensor(G[:, 9, :], G[:, 7, :], G[:, 8, :], ALU.add).then_inc(sel_ready, 1)
            dve.wait_ge(sel_ready, 1)
            link(nc.vector.tensor_tensor(G[:, 14, 0:1], G[:, 11, 0:1], G[:, 11, 1:2], ALU.add))
            link(nc.vector.tensor_scalar(G[:, 14, 0:1], G[:, 14, 0:1], 1e-8, None, ALU.add))
            link(nc.vector.reciprocal(G[:, 14, 1:2], G[:, 14, 0:1]))
            link(nc.vector.scalar_tensor_tensor(G[:, 15, :], G[:, 6, :], G[:, 14, 1:2], G[:, 9, :],
                                                ALU.mult, ALU.mult))
            splits(11, 1)
            dve.wait_ge(rank_mm, 1)
            link(nc.vector.tensor_copy(G[:, 16, :], psg[0:NB, 0:E]))
            link(nc.vector.tensor_copy(G[:, 17, :], psg[0:NB, 8:8 + E]))
            for e in range(E):
                link(nc.vector.tensor_scalar(gcnt[:, e, :], siota[:, 0:NB:SLOTS], G[:, 17, e:e + 1], None, ALU.is_lt))
            link(nc.vector.tensor_reduce(G[:, 18, :], gcnt[:, :, :], AX.X, ALU.add))
            for e in range(1, E):
                link(nc.vector.tensor_tensor(G[:, 19, e:e + 1], G[:, 19, e - 1:e], G[:, 18, e - 1:e], ALU.add))
            link(nc.vector.scalar_tensor_tensor(G[:, 22, :], G[:, 19, :], float(SLOTS), G[:, 16, :],
                                                ALU.mult, ALU.add))
            link(nc.vector.tensor_scalar(G[:, 23, :], G[:, 9, :], -1e4, 1e4, ALU.mult, ALU.add))
            link(nc.vector.tensor_tensor(G[:, 22, :], G[:, 22, :], G[:, 23, :], ALU.add))
            for e in range(E):
                i = nc.vector.tensor_scalar(onehot[:, e, :], siota, G[:, 22, e:e + 1], None, ALU.is_equal)
            i.then_inc(hot_ready, 1)
            for e in range(E):
                if e >= 2:
                    dve.wait_ge(tab_mm, e - 1)
                nc.vector.tensor_scalar(wrep[:, e % 2, :], G[:, 15, e:e + 1].to_broadcast([NB, P]), 1.0, None,
                                        ALU.mult).then_inc(hot_ready, 1)
                if e == 1:
                    splits(12, 0)
            dve.wait_ge(tab_mm, E)
            link(nc.vector.tensor_copy(wrow[:, :], psg[:, 2 * NSLOT:3 * NSLOT]))
            spare = rt[0:1, 0:NSLOT]
            fa = rt[0:1, NSLOT:2 * NSLOT]
            for j in range(SLOTS):
                link(nc.vector.memset(spare.rearrange("p (r j) -> p r j", j=SLOTS)[:, :, j], float(TOK + NT * j)))
            link(nc.vector.scalar_tensor_tensor(fa, psg[0:1, NSLOT:2 * NSLOT], -1.0, spare, ALU.mult, ALU.mult))
            link(nc.vector.tensor_tensor(fa, fa, spare, ALU.add))
            link(nc.vector.tensor_tensor(fa, psg[0:1, 0:NSLOT], fa, ALU.add))
            tv = tab[:, :].rearrange("p (r k) -> p r k", k=8)
            link(nc.vector.tensor_copy(tv[:, :, 0:SLOTS], fa.rearrange("p (r j) -> p r j", j=SLOTS)))
            ce = rt[0:1, 2 * NSLOT:2 * NSLOT + 4 * NR].rearrange("p (k r) -> p k r", k=4)
            for e in range(1, E):
                link(nc.vector.tensor_scalar(ce[:, e, :], siota[0:1, 0:NR], G[0:1, 19, e:e + 1], None, ALU.is_ge))
            link(nc.vector.tensor_tensor(ce[:, 1, :], ce[:, 1, :], ce[:, 2, :], ALU.add))
            link(nc.vector.tensor_tensor(ce[:, 1, :], ce[:, 1, :], ce[:, 3, :], ALU.add))
            nc.vector.tensor_copy(tv[:, :, 4], ce[:, 1, :]).then_inc(tab_ready, 1)
            for g in range(13, NS):
                splits(g, g % 2)

            dve.wait_ge(tab_ready, 1)
            regs = [dve.alloc_register(f"slot_address{j}") for j in range(SLOTS + 1)]

            def add_slots(g, parity):
                r = g - R0
                dve.load(regs, tab[0:1, bass.ds(r * 8, SLOTS + 1)])
                cols = [dve.snap(x, min_val=0, max_val=COLS - NT) for x in regs[:SLOTS]]
                e = dve.snap(regs[SLOTS], min_val=0, max_val=E - 1)
                dve.wait_ge(y_done, g + 1)
                dve.wait_ge(y_free, g)
                for db in range(DB):
                    i = nc.vector.scalar_tensor_tensor(
                        ytmp[:, db, :].rearrange("p (s t) -> p s t", s=SLOTS),
                        psy[parity][:, db * CH:(db + 1) * CH].rearrange("p (s t) -> p s t", s=SLOTS),
                        b2s[:, bass.ds(e * DB + db, 1)],
                        mask[:, bass.ds(e, 1), :].to_broadcast([P, SLOTS, NT]), ALU.add, ALU.mult)
                i.then_inc(y_scaled, 1)
                dve.wait_ge(y_scaled, r + 1)
                for j in range(SLOTS):
                    at = acc[:, :, bass.ds(cols[j], NT)]
                    i = nc.vector.scalar_tensor_tensor(at, ytmp[:, :, j * NT:(j + 1) * NT],
                                                       wrow[:, bass.ds(r * SLOTS + j, 1)], at, ALU.mult, ALU.add)
                i.then_inc(y_free, 1)

            splits(R0, 0)
            with by_two(dve, R0, R0 + NR - 1) as g:
                for u in range(2):
                    splits(g + (u + 1), 1 - u)
                    add_slots(g + u, u)
            add_slots(R0 + NR - 1, 0)
            stage2_dve(dve, link)

        @block.gpsimd
        def _(pool):
            steps = [0]

            def link(i):
                steps[0] += 1
                i.then_inc(pool_step, 1)
                pool.wait_ge(pool_step, steps[0])

            link(nc.gpsimd.iota(iot, pattern=[[1, M]], base=-M, channel_multiplier=0,
                                allow_small_or_imprecise_dtypes=True))
            link(nc.gpsimd.iota(f4[:, 1, :], pattern=[[P, MG]], base=-M, channel_multiplier=1,
                                allow_small_or_imprecise_dtypes=True))
            for q in range(1, 8):
                lo, hi = q * 512, (q + 1) * 512
                pool.wait_ge(x_in[q], 16)
                link(nc.gpsimd.tensor_copy(X[:, 0:DB, lo:hi], x32[:, :, lo:hi]))
                nc.gpsimd.tensor_tensor(X[:, DB:2 * DB, lo:hi], x32[:, :, lo:hi], X[:, 0:DB, lo:hi],
                                        ALU.subtract).then_inc(x_split, 1)
                if q == 1:
                    link(nc.gpsimd.iota(siota, pattern=[[1, NSLOT]], base=0, channel_multiplier=0,
                                        allow_small_or_imprecise_dtypes=True))
                    link(nc.gpsimd.iota(G[:, 20, :], pattern=[[1, E]], base=-E, channel_multiplier=0,
                                        allow_small_or_imprecise_dtypes=True))
                    link(nc.gpsimd.iota(G[:, 21, :], pattern=[[0, E]], base=0, channel_multiplier=NT,
                                        allow_small_or_imprecise_dtypes=True))
                    link(nc.gpsimd.memset(ones64, 1.0))
                    link(nc.gpsimd.affine_select(out=tri, in_=ones64, compare_op=ALU.is_gt, fill=0.0,
                                                 base=0, pattern=[[1, NB]], channel_multiplier=-1))
                    link(nc.gpsimd.memset(G[:, 19, :], 0.0))
                    link(nc.gpsimd.memset(mask[:, :, :], 1.0 / WS))
                    link(nc.gpsimd.memset(mask[:, 1, HP:NT], 0.0))
                    link(nc.gpsimd.memset(mask[:, 2, 0:HEAD], 0.0))
                    link(nc.gpsimd.memset(X[:, :, TOK:COLS], 0.0))
                    link(nc.gpsimd.memset(acc[:, :, TOK:COLS], 0.0))
                    nc.gpsimd.memset(tab[:, :], 0).then_inc(const_ready, 1)

            def split_piece(n):
                pool.wait_ge(wr_in[n % 2], 16 * (n // 2 + 1))
                size = piece_size(n)
                src = stage[:, n % 2, 0:size]
                if n < 4 * E:
                    e, k = (E - 1, 0, 1, 2)[n // 4], n % 4
                    at = e * WE + k * 1024 + (2048 if k >= 2 else 0)
                    his, los = [W[:, at:at + size]], [W[:, at + 2048:at + 2048 + size]]
                    srcs = [src]
                elif n == 4 * E:
                    his, los, srcs = [F0[:, 0:512]], [F0[:, 512:1024]], [src]
                elif n < 4 * E + 4:
                    j0, j1 = ((0, 4), (4, 8), (8, 9))[n - 4 * E - 1]
                    s3 = src.rearrange("p (j d) -> p j d", d=D)
                    his, los, srcs = [V[:, j0:j1, 0, :]], [V[:, j0:j1, 1, :]], [s3]
                else:
                    j = 2 * (n - 4 * E - 4)
                    at = [SH * WE + (j + k) * 1024 for k in range(2)]
                    his = [W[:, x:x + 512] for x in at]
                    los = [W[:, x + 512:x + 1024] for x in at]
                    srcs = [src[:, 0:512], src[:, 512:1024]]
                if 4 * E < n < 4 * E + 4:
                    j0 = ((0, 4), (4, 8), (8, 9))[n - 4 * E - 1][0]
                    if j0 == 0:
                        link(nc.gpsimd.tensor_scalar(src[:, 0:D], src[:, 0:D], gam[:, 0:1], WS, ALU.mult, ALU.mult))
                        link(nc.gpsimd.tensor_scalar(src[:, D:size], src[:, D:size], gam[:, 1:2], WS, ALU.mult, ALU.mult))
                    else:
                        link(nc.gpsimd.tensor_scalar(src, src, gam[:, 1:2], WS, ALU.mult, ALU.mult))
                else:
                    link(nc.gpsimd.tensor_scalar(src, src, WS, None, ALU.mult))
                for hi, s in zip(his, srcs):
                    link(nc.gpsimd.tensor_copy(hi, s))
                for hi, lo, s in zip(his, los, srcs):
                    i = nc.gpsimd.tensor_tensor(lo, s, hi, ALU.subtract)
                i.then_inc(r_split, 1)

            pool.wait_ge(small_in, 11 * 16)
            for n in range(4 * E):
                if n == 4:
                    pool.wait_ge(w_split, 3)
                if n == 8:
                    pool.wait_ge(sums_done, 8)
                split_piece(n)
            for n in range(4 * E, 4 * E + 4):
                split_piece(n)

            pool.wait_ge(tab_ready, 1)
            regs = [pool.alloc_register(f"pool_address{j}") for j in range(SLOTS)]

            def stage_columns(g, parity):
                pool.load(regs, tab[0:1, bass.ds((g - R0) * 8, SLOTS)])
                cols = [pool.snap(x, min_val=0, max_val=COLS - NT) for x in regs]
                if not (isinstance(g, int) and g < R0 + 2):
                    pool.wait_ge(l1_done, g * 4 - 4)
                for j in range(SLOTS):
                    i = nc.gpsimd.tensor_copy(xs[:, parity, :, j * NT:(j + 1) * NT],
                                              X[:, :, bass.ds(cols[j], NT)])
                i.then_inc(x_staged, 1)

            stage_columns(R0, 0)
            stage_columns(R0 + 1, 1)
            pool.wait_ge(y_done, NS)
            for k in range(2):
                split_piece(4 * E + 4 + 2 * k)
                split_piece(4 * E + 5 + 2 * k)
                stage_columns(R0 + 2 + k, k)
            with by_two(pool, R0 + 4, R0 + NR - 1) as g:
                stage_columns(g, 0)
                stage_columns(g + 1, 1)
            stage_columns(R0 + NR - 1, 0)
            stage2_pool(pool, link)


def kernel(**inputs):
    import numpy as np
    import concourse.bacc as bacc
    from concourse.bass_utils import run_bass_kernel_spmd as run

    v = {k.removeprefix("L0_"): np.asarray(x) for k, x in inputs.items()}
    order = np.r_[0:HEAD, 2 * HEAD:NT, HEAD:2 * HEAD]
    x = v["x"][:, order, :].reshape(TOK, D)

    def rows(*parts):
        return np.concatenate([np.asarray(q).reshape(-1, P) for q in parts], 0).T

    first = np.stack([np.concatenate([v[f"ffn_s{w}"][None], v[f"ffn_e{w}"]]) for w in ("w1", "w2")], 1)
    last = np.concatenate([v["ffn_sw3"][None], v["ffn_ew3"]])
    arrays = {
        "xT": x.T.reshape(DB, P, TOK).transpose(1, 0, 2),
        "xR": x,
        "condT": v["cond_1024"].T.reshape(DB, P, NB).transpose(1, 0, 2),
        "ew1": v["cond_ew1"], "ew2": v["cond_ew2"], "sw1": v["cond_sw1"], "sw2": v["cond_sw2"],
        "b1": rows(v["cond_eb1"], v["cond_sb1"]), "b2": rows(v["cond_eb2"], v["cond_sb2"]),
        "gate_w": v["cond_gate_w"], "gate_b": v["cond_gate_b"],
        "time_w": v["cond_time_w"], "time_b": v["cond_time_b"],
        "index_b": v["ffn_index_b"], "index_t": v["ffn_index_t"],
        "index_b4": v["ffn_index_b"].reshape(MG, P).T, "index_t4": v["ffn_index_t"].reshape(MG, P).T,
        "fw": first.reshape(NJ, 2, FH, DB, P).transpose(4, 0, 1, 3, 2).reshape(P, NJ * 2 * DB * FH),
        "w3t": last.transpose(2, 0, 1).reshape(P, NJ * D),
        "fb1": rows(v["ffn_sb1"], v["ffn_eb1"]), "fb2": rows(v["ffn_sb2"], v["ffn_eb2"]),
        "gam": rows(v["ffn_s_ln_g"], v["ffn_sel_ln_g"]), "bet": rows(v["ffn_s_ln_b"], v["ffn_sel_ln_b"]),
        "b3s": v["ffn_sb3"].reshape(1, D), "b3e": v["ffn_eb3"],
        "rw": np.concatenate([v["ffn_sg_w"], v["ffn_eg_w"]]).T.reshape(DB, P, 9).transpose(1, 0, 2),
        "rb": np.concatenate([v["ffn_sg_b"], v["ffn_eg_b"]]), "eb": v["ffn_exp_bias"],
    }
    arrays = {n: np.ascontiguousarray(q) for n, q in arrays.items()}
    nc = bacc.Bacc("TRN2", target_bir_lowering=False, num_devices=1)
    a = {n: nc.dram_tensor(f"in_{n}", q.shape, mybir.dt.from_np(q.dtype), kind="ExternalInput").ap()
         for n, q in arrays.items()}
    a["out"] = nc.dram_tensor("out_rows", (TOK, D), F32, kind="ExternalOutput").ap()
    a["scratch"] = nc.dram_tensor("stage1_rows", (TOK, 2 * D), F16, kind="Internal").ap()
    program(nc, a)
    r = run(nc, [{f"in_{n}": q for n, q in arrays.items()}], core_ids=[0])
    got = np.asarray(r.results[0]["out_rows"]).reshape(NB, NT, D)
    return got[:, np.argsort(order), :]
```

```python
from contextlib import ExitStack, contextmanager

import concourse.bass as bass
from concourse import mybir

F32 = mybir.dt.float32
F16 = mybir.dt.float16
I32 = mybir.dt.int32
ACT = mybir.ActivationFunctionType
ALU = mybir.AluOpType
AX = mybir.AxisListType

P = 128
NB, NT, D = 64, 64, 256
TOK = NB * NT
H = 1024
E, SH = 4, 4
DB, HB = D // P, H // P
HEAD = NT // 3
HP = HEAD + (NT - 2 * HEAD)
WS = 1024.0
CH = 256
NS = TOK // CH
SEG = NT - 2 * HEAD
BS = 3 * SEG
CB = CH // NT
SLOTS = 11
RC = SLOTS * SEG
KEPT = (3, 2, 2, 3)
KEPT0 = (0, 0, 1, 0)
NR = (2 * 3 * NB + E * (SLOTS - 1)) // SLOTS
NRMIN = -(-2 * 2 * NB // SLOTS)
NSLOT = NR * SLOTS
ROW = SLOTS + 1
NCNT = -(-3 * NB // SLOTS)
FAR = 16384
COLS = NB * BS + SLOTS * SEG
WE = 8192
FE, FH, M = 8, 128, 512
MG = M // P
EPS = 1e-5
NJ = FE + 1
FC = 512
NQ = TOK // FC
NK = NQ + NJ


@contextmanager
def by_two(eng, start, end):
    with eng.Fori(0, (end - start) // 2) as i:
        yield i * 2 + start


def program(nc, a):
    with ExitStack() as ctx:
        def sb(name, shape, dt=F32):
            return ctx.enter_context(nc.sbuf_tensor(name, shape, dt))

        def sem(name):
            return ctx.enter_context(nc.semaphore(name))

        W = sb("W", [P, (E + 1) * WE], F16)
        X = sb("X", [P, 2 * DB, COLS], F16)
        acc = sb("acc", [P, DB, COLS])
        hbuf = sb("hbuf", [P, 2, 2, HB, CH], F16)
        h32 = sb("h32", [P, 4, 2 * CH])
        xs = sb("xs", [P, 2, 2 * DB, CH], F16)
        ytmp = sb("ytmp", [P, 2, DB, CH])
        ident = sb("ident", [P, P])
        onesm = sb("onesm", [P, P])
        stage = sb("stage", [P, 2, 1024])
        F0 = sb("F0", [P, 1024], F16)
        V = sb("V", [P, NJ, 2, D], F16)
        b1 = sb("b1", [P, (E + 1) * HB])
        b2 = sb("b2", [P, (E + 1) * DB])
        wrow = sb("wrow", [P, NSLOT])
        tab = sb("tab", [1, NR * ROW + 4], I32)
        gw = sb("gw", [P, 3 * DB, E])
        tw = sb("tw", [P, DB, 2 * E])
        gb = sb("gb", [NB, E])
        tb = sb("tb", [NB, 2 * E])
        G = sb("G", [NB, 28, E])
        gcnt = sb("gcnt", [NB, E, NCNT])
        fb1 = sb("fb1", [P, NJ])
        fb2 = sb("fb2", [P, NJ])
        gam = sb("gam", [P, 2])
        bet = sb("bet", [P, 2])
        gid = sb("gid", [P, MG], I32)
        sid = sb("sid", [P, MG], I32)
        f4 = sb("f4", [P, 16, MG])
        kint = sb("kint", [P, 2, MG], I32)
        gams = sb("gams", [P, 2])

        W32 = W[:, :].bitcast(F32)
        ws32 = W32[:, WE // 2:WE]
        x32 = W32[:, WE:WE + DB * TOK].rearrange("p (d t) -> p d t", d=DB)
        xcols = X[:, :, 0:NB * BS].rearrange("p k (b s) -> p k b s", s=BS)
        xtok = xcols[:, :, :, 1:1 + NT]
        acols = acc[:, :, 0:NB * BS].rearrange("p k (b s) -> p k b s", s=BS)
        atok = acols[:, :, :, 1:1 + NT]

        lent = acc[:, 0, 10 * CB * BS:10 * CB * BS + 16 * NB]
        gsum = lent[:, 0:6 * NB].rearrange("p (d r b) -> p d r b", d=DB, r=3)
        gin = lent[:, 6 * NB:12 * NB].rearrange("p (k b) -> p k b", b=NB)
        cond = lent[:, 12 * NB:14 * NB].rearrange("p (d b) -> p d b", d=DB)
        silc = lent[:, 14 * NB:16 * NB].rearrange("p (d b) -> p d b", d=DB)
        iot = acc[:, 1, 14 * CB * BS:14 * CB * BS + M]
        trow = acc[0:1, 0, 14 * CB * BS:14 * CB * BS + NSLOT]
        xsw = xs[0:NB, :, :, :].rearrange("p a b c -> p (a b c)")
        hot = xsw[:, 0:2 * NSLOT].rearrange("p (u s) -> p u s", u=2)
        siota = xsw[:, 2 * NSLOT:4 * NSLOT].bitcast(F32)
        tri = xsw[:, 4 * NSLOT:4 * NSLOT + 2 * NB].bitcast(F32)
        yw = ytmp[:, :, :, :].rearrange("p a b c -> p (a b c)")
        lhs = yw[0:NB, 0:260].bitcast(F16).rearrange("p (u k c) -> p u k c", u=2, k=2)
        lval = yw[0:NB, 260:390]
        srow = yw[0:1, 512:512 + NSLOT]
        fa = yw[0:1, 0:NSLOT]
        kdiag = yw[:, 0:M].rearrange("p (g t) -> p g t", g=MG)
        kcmp = yw[:, 512:1024]

        ps1 = [ctx.enter_context(nc.psum_tensor(f"ps_hidden{j}", [P, 512], F32)) for j in range(4)]
        psy2 = ctx.enter_context(nc.psum_tensor("ps_out", [P, 2, 512], F32))
        psy = [psy2[:, j, :] for j in range(2)]
        psg = ctx.enter_context(nc.psum_tensor("ps_small", [P, 512], F32))
        pst = ctx.enter_context(nc.psum_tensor("ps_turn", [P, 512], F32))

        def w1(e, part, db, hb):
            return W[:, bass.ds(e * WE + (part * 2048 + db * 1024 + hb * P), P)]

        def w2(e, part, hb, db):
            return W[:, bass.ds(e * WE + (4096 + part * 2048 + hb * D + db * P), P)]

        def fw(j, part, which, db):
            at = (part * 2 + which) * 2 * P + db * P
            if isinstance(j, int) and j == 0:
                return F0[:, at:at + P]
            return W[:, bass.ds((j - 1) * 1024 + (SH * WE + at), P)]

        x_in = [sem(f"x_in{q}") for q in range(8)]
        ws_in = [sem(f"ws_in{q}") for q in range(2)]
        small_in = sem("small_in")
        idx_in = sem("idx_in")
        wr_in = [sem(f"wr_in{q}") for q in range(2)]
        w_split = sem("w_split")
        x_split = sem("x_split")
        r_split = sem("r_split")
        const_ready = sem("const_ready")
        x_staged = sem("x_staged")
        l1_done = sem("l1_done")
        h32_ready = sem("h32_ready")
        h_hi = sem("h_hi")
        h_ready = sem("h_ready")
        y_done = sem("y_done")
        y_taken = sem("y_taken")
        y_free = sem("y_free")
        summed_all = sem("summed_all")
        gain_ready = sem("gain_ready")
        hi_ready = sem("hi_ready")
        key_ready = sem("key_ready")
        key_mm = sem("key_mm")
        dv = sem("dv")
        cond_exp = sem("cond_exp")
        gate_in = sem("gate_in")
        gate_mm = sem("gate_mm")
        gate_log = sem("gate_log")
        gate_exp = sem("gate_exp")
        sel_ready = sem("sel_ready")
        rank_mm = sem("rank_mm")
        hot_ready = sem("hot_ready")
        tab_mm = sem("tab_mm")
        tab_ready = sem("tab_ready")
        sums_done = sem("sums_done")
        pool_step = sem("pool_step")

        block = ctx.enter_context(nc.Block())
        R0 = NS

        def piece_src(n):
            if n < 4 * E:
                e, k = n // 4, n % 4
                if k < 2:
                    return a["ew1"][e, k * P:(k + 1) * P, :]
                return a["ew2"][e, (k - 2) * 512:(k - 1) * 512, :].rearrange("(h p) d -> p h d", p=P)
            n -= 4 * E
            if n == 0:
                return a["fw"][:, 0:512]
            if n < 4:
                j0, j1 = ((0, 4), (4, 8), (8, 9))[n - 1]
                return a["w3t"][:, j0 * D:j1 * D]
            return a["fw"][:, 512 + (n - 4) * 1024:512 + (n - 3) * 1024]

        def piece_size(n):
            n -= 4 * E
            return {0: 512, 3: 256}.get(n, 1024)

        NPIECE = 4 * E + 4 + 4

        def rest_parts(n):
            src = stage[:, n % 2, 0:piece_size(n)]
            n -= 4 * E
            if n == 0:
                return [(src, F0[:, 0:512], F0[:, 512:1024], None)]
            if n < 4:
                j0, j1 = ((0, 4), (4, 8), (8, 9))[n - 1]
                s3 = src.rearrange("p (j d) -> p j d", d=D)
                cuts = ((0, 1), (1, 4)) if n == 1 else ((0, j1 - j0),)
                return [(s3[:, lo:hi, :], V[:, j0 + lo:j0 + hi, 0, :], V[:, j0 + lo:j0 + hi, 1, :],
                         0 if j0 + lo == 0 else 1) for lo, hi in cuts]
            at = [SH * WE + (2 * (n - 4) + j) * 1024 for j in range(2)]
            return [(src[:, j * 512:(j + 1) * 512], W[:, x:x + 512], W[:, x + 512:x + 1024], None)
                    for j, x in enumerate(at)]

        def expert_loops(eng, start, step):
            with by_two(eng, start, NRMIN) as r:
                step(r, 0)
                step(r + 1, 1)
            count = chunk_count(eng)
            with by_two(eng, NRMIN, NR) as r:
                for u in range(2):
                    with eng.If(r + u < count):
                        step(r + u, u)
            parity = eng.value_load(tab[0:1, NR * ROW + 1:NR * ROW + 2], min_val=0, max_val=1)
            return count - 1, parity

        def x_piece(q):
            b = slice(q * 8, (q + 1) * 8)
            return (x32[:, :, q * 512:(q + 1) * 512].rearrange("p d (b t) -> p d b t", t=NT),
                    xtok[:, 0:DB, b, :], xtok[:, DB:2 * DB, b, :])

        def chunk_count(eng):
            return eng.value_load(tab[0:1, NR * ROW:NR * ROW + 1], min_val=NRMIN - 2, max_val=NR - 2) + 2

        SW = W32[:, 0:E * WE // 2]

        def take(base, lo, shape, dt=F32):
            n = 1
            for s in shape:
                n *= s
            words = n if dt is not F16 else n // 2
            v = base[:, lo:lo + words]
            if dt is not F32:
                v = v.bitcast(dt)
            names = "abc"[:len(shape)]
            if len(shape) == 1:
                return v
            return v.rearrange(f"p ({' '.join(names)}) -> p {' '.join(names)}",
                               **{c: s for c, s in zip(names, shape)})

        gcs = take(SW, 0, [NK, 2, FC], F16)
        w3r = take(SW, 8704, [NJ, D])
        cg = take(SW, 11008, [MG, 4, P], F16)
        xg = take(SW, 12032, [MG, D])
        cgT = take(SW, 13056, [2 * DB, M], F16)
        tev = take(SW, 14080, [2, 1024], F16)
        moe = take(SW, 15104, [MG, D])
        hw = hbuf[:, :, :, :, :].rearrange("p a b c d -> p (a b c d)").bitcast(F32)
        s32 = take(hw, 0, [2, FC])
        x2 = take(hw, 1024, [2, FC])
        g32 = take(hw, 2048, [2, FC])
        ghl = take(hw, 3072, [2, 2, FC], F16)
        gc32 = h32[:, 0:2, :]
        sq = h32[:, 2:4, :]
        turned = pst[:, :].bitcast(F16)
        xrow = X[:, :, :].rearrange("p k t -> p (k t)").bitcast(F32)[:, 0:TOK // P * D] \
            .rearrange("p (n d) -> p n d", d=D)
        stf = stage[:, :, :].rearrange("p a b -> p (a b)")
        id16 = take(stf, 512, [P], F16)
        betrep = stf[:, 128:256]
        betm = take(stf, 256, [FE, FE])
        Cm = take(stf, 448, [P], F16)
        b3s = stf[0:1, 1024:1280]
        b3e = stf[0:FE, 1280:1536]
        rwr = take(stf, 1536, [DB, 9])
        rws = take(stf, 1560, [2, DB, 10], F16)
        rb = stf[:, 1584:1593]
        eb = stf[:, 1600:1608]
        io8 = stf[:, 1608:1616]
        rlg = take(stf, 1616, [MG, 9])
        rsg = take(stf, 1656, [MG, 9])
        rsel = take(stf, 1696, [MG, FE])
        rcand = take(stf, 1728, [MG, FE])
        roh = take(stf, 1760, [MG, FE])
        rm = take(stf, 1792, [8, MG])
        rstd = take(stf, 1824, [NK, MG])
        rse = take(stf, 1896, [MG, FE])
        c0b = ytmp[:, 0, 0, :]
        ce8 = ytmp[0:FE, 0, 1, :]
        ohT = xs[0:FE, :, :, :].rearrange("p a b c -> p (a b c)").bitcast(F32)[:, 0:M] \
            .rearrange("p (g t) -> p g t", g=MG)

        misc_in, xg_in, cg_in = sem("misc_in"), sem("xg_in"), sem("cg_in")
        x_rows_in = [sem(f"x_rows_in{q}") for q in range(4)]
        w3_in = sem("w3_in")
        const2_ready = sem("const2_ready")
        c_hi, c_lo, c_lo_pool = sem("c_hi"), sem("c_lo"), sem("c_lo_pool")
        ab_done, s_ready, x2_ready = sem("ab_done"), sem("s_ready"), sem("x2_ready")
        g_made, g_hi, g_ready = sem("g_made"), sem("g_hi"), sem("g_ready")
        c_done, gc32_ready, gc_hi, gc_ready, sq_ready = (sem("c_done"), sem("gc32_ready"), sem("gc_hi"),
                                                        sem("gc_ready"), sem("sq_ready"))
        turn_done, turn_act, turn_dve = sem("turn_done"), sem("turn_act"), sem("turn_dve")
        row_out = [sem("row_out_act"), sem("row_out_dve")]
        back_done, cg_hi, cg_ready = sem("back_done"), sem("cg_hi"), sem("cg_ready")
        const_mm, rw_ready, router_mm, const_taken = (sem("const_mm"), sem("rw_ready"), sem("router_mm"),
                                                      sem("const_taken"))
        logit_ready, score_ready, diff_ready, mix_ready = (sem("logit_ready"), sem("score_ready"),
                                                           sem("diff_ready"), sem("mix_ready"))
        hot2_ready, hot_turned, hot_taken, pick_mm = (sem("hot2_ready"), sem("hot_turned"), sem("hot_taken"),
                                                      sem("pick_mm"))
        var_mm, var_ready, std_ready = sem("var_mm"), sem("var_ready"), sem("std_ready")
        u_done, u_free = sem("u_done"), sem("u_free")
        x_const, moe_step, out_done, scat_done = (sem("x_const"), sem("moe_step"), sem("out_done"),
                                                  sem("scat_done"))
        scratch = a["scratch"]

        def stage2_loads(sp):
            sp.wait_ge(r_split, NPIECE)
            for dst, src in ((b3s, a["b3s"]), (b3e, a["b3e"]), (rwr, a["rw"]),
                             (rb, a["rb"].partition_broadcast(P)), (eb, a["eb"].partition_broadcast(P))):
                sp.dma_start(dst, src).then_inc(misc_in, 16)
            sp.wait_ge(summed_all, 1)
            sp.dma_start(w3r, a["w3t"].rearrange("p (j d) -> p j d", d=D)).then_inc(w3_in, 16)
            rows = scratch.rearrange("(k s p) d -> p k s d", p=P, s=2)
            with sp.Fori(0, NQ) as k:
                for f, ready in enumerate((turn_act, turn_dve)):
                    sp.wait_ge(ready, k + 1)
                    sp.dma_start(rows[:, bass.ds(2 * k + f, 1), :, :].rearrange("p o s d -> p (o s) d"),
                                 tev[:, f, :].rearrange("p (s d) -> p s d", s=2)).then_inc(row_out[f], 16)
            sp.wait_ge(ab_done, 2 * NQ)
            for q in range(4):
                n = TOK // P // 4
                sp.dma_start(xrow[:, q * n:(q + 1) * n, :],
                             a["xR"][q * n * P:(q + 1) * n * P, :].rearrange("(n p) d -> p n d", p=P)) \
                    .then_inc(x_rows_in[q], 16)
            with sp.Fori(0, TOK // P // 2) as t:
                sp.wait_ge(u_free, t + 1)
                sp.dma_start(a["out"].rearrange("(t s p) d -> p t s d", p=P, s=2)
                             [:, bass.ds(t, 1), :, :].rearrange("p o s d -> p (o s) d"),
                             xrow[:, bass.ds(2 * t, 2), :]).then_inc(out_done, 16)
            sp.wait_ge(scat_done, 16 * MG)

        def summed(k):
            return atok[:, :, bass.ds(k * (FC // NT), FC // NT), :]

        def high(k):
            return X[:, 0:DB, bass.ds(k * FC, FC)].rearrange("p d (b t) -> p d b t", t=NT)

        def low(k):
            return X[:, DB:2 * DB, bass.ds(k * FC, FC)].rearrange("p d (b t) -> p d b t", t=NT)

        def pair_loop(eng, body):
            body(0)
            with by_two(eng, 2, NQ) as k:
                body(k)

        def stage2_act(act):
            act.wait_ge(summed_all, 1)

            def c_high(k):
                nc.scalar.activation(high(k), summed(k),
                                     ACT.Copy).then_inc(c_hi, 1)

            def factors(k, j, parity, first):
                act.wait_ge(ab_done, k * 2 + 1)
                if not first:
                    act.wait_ge(g_made, k - 1)
                nc.scalar.activation(s32[:, parity, :], ps1[2 * parity][:, :], ACT.Silu,
                                     bias=fb1[:, bass.ds(j, 1)], scale=1.0 / WS)
                act.wait_ge(ab_done, k * 2 + 2)
                nc.scalar.activation(x2[:, parity, :], ps1[2 * parity + 1][:, :], ACT.Identity,
                                     bias=fb2[:, bass.ds(j, 1)], scale=1.0 / WS).then_inc(x2_ready, 1)

            def centred(k, parity, first):
                act.wait_ge(c_done, k + 1)
                if not first:
                    act.wait_ge(gc_ready, k - 1)
                    act.wait_ge(sq_ready, k - 1)
                nc.scalar.activation(gc32[:, parity, :], psy[parity][:, :], ACT.Copy).then_inc(gc32_ready, 1)

            def body(k):
                first = isinstance(k, int) and k == 0
                for u in range(2):
                    factors(k + u, 0, u, first)
                    act.wait_ge(turn_done, (k + u) * 2 + 1)
                    if not (first and u == 0):
                        act.wait_ge(row_out[0], (k + u) * 16)
                    nc.scalar.activation(tev[:, 0, :], turned, ACT.Copy).then_inc(turn_act, 1)
                for u in range(2):
                    centred(k + u, u, first)

            c_high(0)
            c_high(1)
            with_next = [True]

            def body_next(k):
                c_high(k + 2)
                c_high(k + 3)
                body(k)

            body_next(0)
            with by_two(act, 2, NQ - 2) as k:
                body_next(k)
            with by_two(act, NQ - 2, NQ) as k:
                body(k)
            act.wait_ge(back_done, 1)
            nc.scalar.activation(cgT[:, 0:2, :], ps1[0][:, :].bitcast(F16).rearrange("p (n t) -> p n t", n=2),
                                 ACT.Copy).then_inc(cg_hi, 1)
            factors(NQ, 0, 0, False)
            centred(NQ, 0, False)
            with by_two(act, NQ + 1, NK) as k:
                for u in range(2):
                    factors(k + u, k + (u - NQ), 1 - u, False)
                for u in range(2):
                    centred(k + u, 1 - u, False)
            act.wait_ge(logit_ready, 1)
            nc.scalar.activation(rsg[:, :, :], rlg[:, :, :], ACT.Sigmoid).then_inc(score_ready, 1)
            act.wait_ge(diff_ready, 1)
            nc.scalar.activation(rm[:, 3, :], rm[:, 2, :], ACT.Sigmoid)
            nc.scalar.activation(rm[:, 4, :], rm[:, 2, :], ACT.Sigmoid, scale=-1.0).then_inc(mix_ready, 1)
            act.wait_ge(var_ready, 1)
            nc.scalar.activation(rstd[:, :, :], rstd[:, :, :], ACT.Sqrt).then_inc(std_ready, 1)

        def stage2_pe(pe):
            pe.wait_ge(summed_all, 1)
            pe.wait_ge(const2_ready, 1)

            def products(k, j, parity, rhs, first):
                if not first:
                    pe.wait_ge(x2_ready, k - 1)
                for which in range(2):
                    out = ps1[2 * parity + which][:, :]
                    n = 0
                    for wp, xp in ((0, 0), (0, 1), (1, 0)):
                        for db in range(DB):
                            mm = pe.matmul(out, fw(j, wp, which, db), rhs(xp, db), start=(n == 0), stop=(n == 5))
                            n += 1
                    mm.then_inc(ab_done, 1)

            def centre(k, parity, first):
                pe.wait_ge(g_ready, k + 1)
                if not first:
                    pe.wait_ge(gc32_ready, k - 1)
                for part in range(2):
                    mm = pe.matmul(psy[parity][:, :], Cm, ghl[:, parity, part, :], start=(part == 0), stop=(part == 1))
                mm.then_inc(c_done, 1)

            def turn(k, f, first):
                if f == 1:
                    pe.wait_ge(turn_act, k + 1)
                elif not first:
                    pe.wait_ge(turn_dve, k)
                for s in range(2):
                    for n in range(2 * DB):
                        mm = pe.transpose(turned[:, (4 * s + n) * P:(4 * s + n + 1) * P],
                                          X[:, n, bass.ds(k * FC + (2 * f + s) * P, P)], id16)
                mm.then_inc(turn_done, 1)

            def variance(k, parity):
                pe.wait_ge(sq_ready, k + 1)
                for g in range(MG):
                    mm = pe.matmul(psg[:, bass.ds(k * MG + g, 1)], sq[:, parity, g * P:(g + 1) * P],
                                   onesm[:, 0:1], start=True, stop=True)
                mm.then_inc(var_mm, 1)

            def body(k):
                first = isinstance(k, int) and k == 0
                for u in range(2):
                    if first:
                        pe.wait_ge(c_lo, u + 1)
                    else:
                        pe.wait_ge(c_lo_pool, k + (u - 1))
                    products(k + u, 0, u, lambda xp, db: X[:, 2 * xp + db, bass.ds((k + u) * FC, FC)], first)
                    turn(k + u, 0, first and u == 0)
                    turn(k + u, 1, first and u == 0)
                if not first:
                    variance(k - 2, 0)
                    variance(k - 1, 1)
                for u in range(2):
                    centre(k + u, u, first)

            pair_loop(pe, body)
            pe.wait_ge(w3_in, 16)
            pe.wait_ge(misc_in, 5 * 16)
            pe.wait_ge(turn_dve, NQ)
            pe.matmul(pst[:, 0:D], betrep, w3r[:, 0, :], start=True, stop=False)
            pe.matmul(pst[:, 0:D], onesm[0:1, :], b3s, start=False, stop=True)
            for e in range(FE):
                pe.matmul(pst[0:FE, D:2 * D], betm[:, e, :], w3r[:, 1 + e, :], start=(e == 0), stop=False)
            pe.matmul(pst[0:FE, D:2 * D], ident[0:FE, 0:FE], b3e, start=False, stop=True).then_inc(const_mm, 1)
            pe.wait_ge(cg_in, 16 * MG)
            pe.wait_ge(x2_ready, NQ)
            for n in range(2 * DB):
                for g in range(MG):
                    mm = pe.transpose(ps1[n // 2][:, :].bitcast(F16)[:, (n % 2) * M + g * P:(n % 2) * M + (g + 1) * P],
                                      cg[:, g, n, :], id16)
                if n % 2 == 1:
                    mm.then_inc(back_done, 1)
            pe.wait_ge(cg_hi, 1)
            pe.wait_ge(cg_ready, 1)
            gathered = lambda xp, db: cgT[:, 2 * xp + db, :]
            products(NQ, 0, 0, gathered, False)
            pe.wait_ge(rw_ready, 1)
            pe.wait_ge(const_taken, 1)
            for g in range(MG):
                n = 0
                for xp, wp in ((0, 0), (0, 1), (1, 0)):
                    for db in range(DB):
                        mm = pe.matmul(pst[:, g * 9:(g + 1) * 9], cgT[:, 2 * xp + db, g * P:(g + 1) * P],
                                       rws[:, wp, db, 0:9], start=(n == 0), stop=(n == 5))
                        n += 1
            mm.then_inc(router_mm, 1)
            variance(NQ - 2, 0)
            centre(NQ, 0, False)
            with by_two(pe, NQ + 1, NK) as k:
                for u in range(2):
                    products(k + u, k + (u - NQ), 1 - u, gathered, False)
                variance(k - 2, 1)
                variance(k - 1, 0)
                for u in range(2):
                    centre(k + u, 1 - u, False)
            pe.wait_ge(hot2_ready, 1)
            for g in range(MG):
                mm = pe.transpose(pst[0:FE, g * P:(g + 1) * P], roh[:, g, :], ident[:, :])
            mm.then_inc(hot_turned, 1)
            variance(NK - 2, 1)
            variance(NK - 1, 0)

            def last(bank, s, k, g, j):
                out = bank[:, s * D:(s + 1) * D]
                for n, (gp, vp) in enumerate(((0, 0), (0, 1), (1, 0))):
                    mm = pe.matmul(out, gcs[:, bass.ds(k, 1), gp, bass.ds(g * P, P)].rearrange("p o t -> p (o t)"),
                                   V[:, bass.ds(j, 1), vp, :].rearrange("p o d -> p (o d)"),
                                   start=(n == 0), stop=(n == 2))
                return mm

            pe.wait_ge(gc_ready, NK)
            def main_last(q, first):
                for f in range(4):
                    if not first:
                        pe.wait_ge(u_free, q * 2 + (f - 3))
                    for s in range(2):
                        mm = last(ps1[f], s, q + f // 2, 2 * (f % 2) + s, 0)
                    mm.then_inc(u_done, 1)
            main_last(0, True)
            with by_two(pe, 2, NQ) as q:
                main_last(q, False)
            base = 2 * NQ

            def moe_last(j, parity):
                for f in range(2):
                    pe.wait_ge(u_free, j * 2 + (base + f - 3))
                    for s in range(2):
                        mm = last(ps1[2 * parity + f], s, j + NQ, 2 * f + s, j)
                    mm.then_inc(u_done, 1)

            moe_last(0, 0)
            pe.wait_ge(hot_taken, 1)
            for g in range(MG):
                mm = pe.matmul(psy[g // 2][:, (g % 2) * D:(g % 2 + 1) * D], ohT[:, g, :], ce8, start=True, stop=True)
            mm.then_inc(pick_mm, 1)
            with by_two(pe, 1, NJ) as j:
                moe_last(j, 1)
                moe_last(j + 1, 0)

        def stage2_dve(dve, link):
            dve.wait_ge(y_free, chunk_count(dve))
            nc.vector.memset(f4[0:1, 12, :], 0.0).then_inc(summed_all, 1)

            def c_low(k):
                dve.wait_ge(c_hi, k + 1)
                nc.vector.tensor_tensor(low(k), summed(k), high(k),
                                        ALU.subtract).then_inc(c_lo, 1)

            def gate_product(k, parity, first):
                dve.wait_ge(x2_ready, k + 1)
                nc.vector.tensor_tensor(g32[:, parity, :], s32[:, parity, :], x2[:, parity, :],
                                        ALU.mult).then_inc(g_made, 1)
                dve.wait_ge(g_made, k + 1)
                if not first:
                    dve.wait_ge(c_done, k - 1)
                nc.vector.tensor_copy(ghl[:, parity, 0, :], g32[:, parity, :]).then_inc(g_hi, 1)
                dve.wait_ge(g_hi, k + 1)
                nc.vector.tensor_tensor(ghl[:, parity, 1, :], g32[:, parity, :], ghl[:, parity, 0, :],
                                        ALU.subtract).then_inc(g_ready, 1)

            def keep(k, parity):
                dve.wait_ge(gc32_ready, k + 1)
                out = [gcs[:, bass.ds(k, 1), part, :].rearrange("p o t -> p (o t)") for part in range(2)]
                nc.vector.tensor_copy(out[0], gc32[:, parity, :]).then_inc(gc_hi, 1)
                dve.wait_ge(gc_hi, k + 1)
                nc.vector.tensor_tensor(out[1], gc32[:, parity, :], out[0], ALU.subtract).then_inc(gc_ready, 1)

            def body(k):
                first = isinstance(k, int) and k == 0
                for u in range(2):
                    gate_product(k + u, u, first)
                    dve.wait_ge(turn_done, (k + u) * 2 + 2)
                    if not (first and u == 0):
                        dve.wait_ge(row_out[1], (k + u) * 16)
                    nc.vector.tensor_copy(tev[:, 1, :], turned).then_inc(turn_dve, 1)
                for u in range(2):
                    keep(k + u, u)

            c_low(0)
            c_low(1)
            pair_loop(dve, body)
            dve.wait_ge(const_mm, 1)
            link(nc.vector.tensor_copy(c0b, pst[:, 0:D]))
            nc.vector.tensor_copy(ce8, pst[0:FE, D:2 * D]).then_inc(const_taken, 1)
            link(nc.vector.tensor_scalar(rws[:, 0, :, 0:9], rwr, WS, None, ALU.mult))
            nc.vector.scalar_tensor_tensor(rws[:, 1, :, 0:9], rwr, WS, rws[:, 0, :, 0:9],
                                           ALU.mult, ALU.subtract).then_inc(rw_ready, 1)
            dve.wait_ge(back_done, 2)
            nc.vector.tensor_copy(cgT[:, 2:4, :], ps1[1][:, :].bitcast(F16)
                                  .rearrange("p (n t) -> p n t", n=2)).then_inc(cg_ready, 1)
            gate_product(NQ, 0, False)
            keep(NQ, 0)
            dve.wait_ge(router_mm, 1)
            nc.vector.scalar_tensor_tensor(rlg[:, :, :], pst[:, 0:MG * 9].rearrange("p (g e) -> p g e", e=9),
                                           1.0 / WS, rb.unsqueeze(1).to_broadcast([P, MG, 9]),
                                           ALU.mult, ALU.add).then_inc(logit_ready, 1)
            with by_two(dve, NQ + 1, NK) as k:
                for u in range(2):
                    gate_product(k + u, 1 - u, False)
                for u in range(2):
                    keep(k + u, 1 - u)
            dve.wait_ge(score_ready, 1)

            def over_e(v):
                return v.unsqueeze(2).to_broadcast([P, MG, FE])

            iob = io8.unsqueeze(1).to_broadcast([P, MG, FE])
            link(nc.vector.tensor_tensor(rsel, rsg[:, :, 1:9], eb.unsqueeze(1).to_broadcast([P, MG, FE]), ALU.add))
            link(nc.vector.tensor_reduce(rm[:, 0, :], rsel, AX.X, ALU.max))
            link(nc.vector.tensor_tensor(rcand, rsel, over_e(rm[:, 0, :]), ALU.is_equal))
            link(nc.vector.tensor_tensor(rcand, rcand, iob, ALU.mult))
            link(nc.vector.tensor_reduce(rm[:, 1, :], rcand, AX.X, ALU.min))
            nc.vector.tensor_tensor(roh, iob, over_e(rm[:, 1, :]), ALU.is_equal).then_inc(hot2_ready, 1)
            dve.wait_ge(hot2_ready, 1)
            link(nc.vector.tensor_tensor(rcand, roh, rsg[:, :, 1:9], ALU.mult))
            link(nc.vector.tensor_reduce(rm[:, 5, :], rcand, AX.X, ALU.add))
            nc.vector.tensor_tensor(rm[:, 2, :], rsg[:, :, 0], rm[:, 5, :], ALU.subtract).then_inc(diff_ready, 1)
            dve.wait_ge(hot_turned, 1)
            nc.vector.tensor_copy(ohT, pst[0:FE, :].rearrange("p (g t) -> p g t", g=MG)).then_inc(hot_taken, 1)
            dve.wait_ge(mix_ready, 1)
            dve.wait_ge(var_mm, NK)
            nc.vector.tensor_scalar(rstd[:, :, :], psg[:, 0:NK * MG].rearrange("p (k g) -> p k g", g=MG),
                                    1.0 / FH, EPS, ALU.mult, ALU.add).then_inc(var_ready, 1)
            dve.wait_ge(std_ready, 1)
            link(nc.vector.reciprocal(rstd[:, :, :], rstd[:, :, :]))
            link(nc.vector.tensor_scalar(rstd[:, :, :], rstd[:, :, :], 1.0 / WS, None, ALU.mult))
            link(nc.vector.tensor_tensor(rse, roh, over_e(rm[:, 4, :]), ALU.mult))
            link(nc.vector.tensor_tensor(rse, rse, rstd[:, NQ + 1:NK, :].rearrange("p e g -> p g e"), ALU.mult))
            rflat = rstd.rearrange("p k g -> p (k g)")
            with dve.Fori(0, 4) as q:
                dve.wait_ge(x_const, q + 1)
                for f in range(4):
                    dve.wait_ge(u_done, q * 4 + (f + 1))
                    for s in range(2):
                        row = xrow[:, bass.ds(q * 8 + (2 * f + s), 1), :].rearrange("p o d -> p (o d)")
                        i = nc.vector.scalar_tensor_tensor(row, ps1[f][:, s * D:(s + 1) * D],
                                                           rflat[:, bass.ds(q * 8 + (2 * f + s), 1)], row,
                                                           ALU.mult, ALU.add)
                    i.then_inc(u_free, 1)
            dve.wait_ge(xg_in, 16 * MG)
            for g in range(MG):
                if g % 2 == 0:
                    dve.wait_ge(u_done, 2 * NQ + g // 2 + 1)
                i = nc.vector.scalar_tensor_tensor(moe[:, g, :], ps1[g // 2][:, (g % 2) * D:(g % 2 + 1) * D],
                                                   rstd[:, NQ, g:g + 1], c0b, ALU.mult, ALU.add)
                if g % 2 == 1:
                    i.then_inc(u_free, 1)
            dve.wait_ge(u_free, 2 * NQ + 2)
            for g in range(MG):
                i = nc.vector.scalar_tensor_tensor(moe[:, g, :], moe[:, g, :], rm[:, 3, g:g + 1], xg[:, g, :],
                                                   ALU.mult, ALU.add)
            i.then_inc(moe_step, 1)
            dve.wait_ge(moe_step, 1)
            dve.wait_ge(pick_mm, 1)
            for g in range(MG):
                i = nc.vector.scalar_tensor_tensor(moe[:, g, :], psy[g // 2][:, (g % 2) * D:(g % 2 + 1) * D],
                                                   rm[:, 4, g:g + 1], moe[:, g, :], ALU.mult, ALU.add)
            i.then_inc(moe_step, 1)
            dve.wait_ge(moe_step, 2)
            sflat = rse.rearrange("p g e -> p (g e)")
            with by_two(dve, 1, NJ) as j:
                for u in range(2):
                    dve.wait_ge(u_free, j * 2 + (2 * NQ + 2 * u))
                    for g in range(MG):
                        if g % 2 == 0:
                            dve.wait_ge(u_done, j * 2 + (2 * NQ + 2 * u + g // 2 + 1))
                        bank = ps1[2 * (1 - u) + g // 2]
                        i = nc.vector.scalar_tensor_tensor(moe[:, g, :], bank[:, (g % 2) * D:(g % 2 + 1) * D],
                                                           sflat[:, bass.ds(j + (g * FE + u - 1), 1)],
                                                           moe[:, g, :], ALU.mult, ALU.add)
                        if g == 1:
                            i.then_inc(u_free, 1)
                    i.then_inc(u_free, 1)

        def stage2_pool(pool, link):
            link(nc.gpsimd.tensor_scalar(Cm, ident[:, :], -1.0 / FH, None, ALU.add))
            link(nc.gpsimd.tensor_scalar(betrep, onesm[:, :], bet[:, 0:1], None, ALU.mult))
            link(nc.gpsimd.memset(betm[:, :, :], 0.0))
            for e in range(FE):
                link(nc.gpsimd.tensor_copy(betm[:, e, e:e + 1], bet[:, 1:2]))
            link(nc.gpsimd.iota(io8, pattern=[[1, FE]], base=-FE, channel_multiplier=0,
                                allow_small_or_imprecise_dtypes=True))
            pool.wait_ge(summed_all, 1)
            nc.gpsimd.tensor_copy(id16, ident[:, :]).then_inc(const2_ready, 1)
            for g in range(MG):
                nc.gpsimd.indirect_dma_start(
                    out=xg[:, g, :], out_offset=None, in_=a["xR"],
                    in_offset=bass.IndirectOffsetOnAxis(ap=gid[:, g:g + 1], axis=0)).then_inc(xg_in, 16)

            def c_low(k):
                pool.wait_ge(c_hi, k + 1)
                nc.gpsimd.tensor_tensor(low(k), summed(k), high(k),
                                        ALU.subtract).then_inc(c_lo_pool, 1)

            def squares(k, parity):
                pool.wait_ge(gc32_ready, k + 1)
                if not (isinstance(k, int) and k < 2):
                    pool.wait_ge(var_mm, k - 1)
                nc.gpsimd.tensor_tensor(sq[:, parity, :], gc32[:, parity, :], gc32[:, parity, :],
                                        ALU.mult).then_inc(sq_ready, 1)

            def body(k):
                c_low(k + 2)
                c_low(k + 3)
                squares(k, 0)
                squares(k + 1, 1)

            body(0)
            with by_two(pool, 2, NQ - 2) as k:
                body(k)
            squares(NQ - 2, 0)
            squares(NQ - 1, 1)
            for f in range(2):
                pool.wait_ge(row_out[f], 16 * NQ)
            for g in range(MG):
                nc.gpsimd.indirect_dma_start(
                    out=cg[:, g, :, :].rearrange("p n d -> p (n d)"), out_offset=None, in_=scratch,
                    in_offset=bass.IndirectOffsetOnAxis(ap=gid[:, g:g + 1], axis=0)).then_inc(cg_in, 16)
            pool.wait_ge(const_taken, 1)
            squares(NQ, 0)
            for q in range(4):
                squares(NQ + 1 + 2 * q, 1)
                squares(NQ + 2 + 2 * q, 0)
                pool.wait_ge(x_rows_in[q], 16)
                rows = xrow[:, q * 8:(q + 1) * 8, :]
                nc.gpsimd.tensor_tensor(rows, rows, c0b.unsqueeze(1).to_broadcast([P, 8, D]),
                                        ALU.add).then_inc(x_const, 1)
            pool.wait_ge(out_done, 16 * 2 * NQ)
            pool.wait_ge(u_free, 2 * NQ + 2 * NJ)
            for g in range(MG):
                nc.gpsimd.indirect_dma_start(
                    out=a["out"], out_offset=bass.IndirectOffsetOnAxis(ap=sid[:, g:g + 1], axis=0),
                    in_=moe[:, g, :], in_offset=None, bounds_check=TOK - 1,
                    oob_is_err=False).then_inc(scat_done, 16)
            pool.wait_ge(scat_done, 16 * MG)

        @block.sync
        def _(sp):
            sp.dma_start(ws32[:, 0:2048].rearrange("p (k h) -> p k h", k=DB),
                         a["sw1"].rearrange("(k p) h -> p k h", p=P)).then_inc(ws_in[0], 16)
            sp.dma_start(x32[:, :, 0:512], a["xT"][:, :, 0:512]).then_inc(x_in[0], 16)
            sp.dma_start(b1[:, :], a["b1"]).then_inc(small_in, 16)
            sp.dma_start(ws32[:, 2048:4096].rearrange("p (k h) -> p k h", k=HB),
                         a["sw2"].rearrange("(k p) h -> p k h", p=P)).then_inc(ws_in[1], 16)
            for q in range(1, 8):
                sp.dma_start(x32[:, :, q * 512:(q + 1) * 512],
                             a["xT"][:, :, q * 512:(q + 1) * 512]).then_inc(x_in[q], 16)
            for n in range(NPIECE):
                if n >= 2:
                    sp.wait_ge(r_split, n - 1)
                src = piece_src(n)
                dst = stage[:, n % 2, 0:piece_size(n)]
                if len(src.shape) == 3:
                    dst = dst.rearrange("p (h d) -> p h d", d=D)
                sp.dma_start(dst, src).then_inc(wr_in[n % 2], 16)
            stage2_loads(sp)

        @block.scalar
        def _(act):
            act.dma_start(cond[:, :, :], a["condT"]).then_inc(small_in, 16)
            act.dma_start(b2[:, :], a["b2"]).then_inc(small_in, 16)
            act.dma_start(gw[:, :, :], a["gate_w"].rearrange("(k p) e -> p k e", p=P)).then_inc(small_in, 16)
            act.dma_start(tw[:, :, :], a["time_w"].rearrange("(k p) e -> p k e", p=P)).then_inc(small_in, 16)
            act.dma_start(gb[:, :], a["gate_b"].partition_broadcast(NB)).then_inc(small_in, 16)
            act.dma_start(tb[:, :], a["time_b"].partition_broadcast(NB)).then_inc(small_in, 16)
            act.dma_start(fb1[:, :], a["fb1"]).then_inc(small_in, 16)
            act.dma_start(fb2[:, :], a["fb2"]).then_inc(small_in, 16)
            act.dma_start(gam[:, :], a["gam"]).then_inc(small_in, 16)
            act.dma_start(bet[:, :], a["bet"]).then_inc(small_in, 16)
            act.dma_start(kint[:, 0, :], a["index_b4"]).then_inc(idx_in, 16)
            act.dma_start(kint[:, 1, :], a["index_t4"]).then_inc(idx_in, 16)
            act.wait_ge(small_in, 11 * 16)
            nc.scalar.activation(silc[:, :, :], cond[:, :, :], ACT.Exp, scale=-1.0).then_inc(cond_exp, 1)

            def gelus(g, e, size=CH):
                first = isinstance(g, int) and g == 0
                for j in range(4):
                    act.wait_ge(l1_done, g * 4 + (j + 1))
                    if not first:
                        act.wait_ge(h_ready, g * 4 + (j - 3))
                    for k in range(2):
                        hb = 2 * j + k
                        i = nc.scalar.activation(
                            h32[:, j, k * size:(k + 1) * size], ps1[j][:, k * size:(k + 1) * size],
                            ACT.Gelu_apprx_tanh, bias=b1[:, bass.ds(e * HB + hb, 1)], scale=1.0 / WS)
                    i.then_inc(h32_ready, 1)

            def store(g, parity):
                act.wait_ge(y_done, g + 1)
                for db in range(DB):
                    i = nc.scalar.activation(
                        atok[:, db, bass.ds(g * CB, CB), :],
                        psy[parity][:, db * CH:(db + 1) * CH].rearrange("p (b t) -> p b t", t=NT),
                        ACT.Identity, bias=b2[:, SH * DB + db:SH * DB + db + 1], scale=1.0 / WS)
                i.then_inc(y_taken, 1)

            def high_piece(e, k):
                act.wait_ge(wr_in[k % 2], e * 32 + 16 * (k // 2 + 1))
                at = k * 1024 + (2048 if k >= 2 else 0)
                nc.scalar.activation(W[:, bass.ds(e * WE + at, 1024)], stage[:, k % 2, :], ACT.Copy,
                                     scale=WS).then_inc(hi_ready, 1)

            def high_rest(n):
                act.wait_ge(wr_in[n % 2], 16 * (n // 2 + 1))
                parts = rest_parts(n)
                for c, (src, hi, lo, gain) in enumerate(parts):
                    scale = WS if gain is None else gams[:, gain:gain + 1]
                    i = nc.scalar.activation(hi, src, ACT.Copy, scale=scale)
                i.then_inc(hi_ready, 1)

            gelus(0, SH)
            gelus(1, SH)
            store(0, 0)
            gelus(2, SH)
            store(1, 1)
            def weigh(e):
                for u in range(2):
                    gelus(e * 2 + (3 + u), SH)
                    high_piece(e, 2 * u)
                    store(e * 2 + (2 + u), u)
                    high_piece(e, 2 * u + 1)

            weigh(0)
            act.wait_ge(w_split, 3)
            weigh(1)
            act.wait_ge(sums_done, 8)
            act.wait_ge(x_split, 7)
            with act.Fori(2, E) as e:
                weigh(e)
            act.wait_ge(gate_log, 1)
            nc.scalar.activation(G[:, 4, :], G[:, 2, :], ACT.Exp, bias=G[:, 3, 0:1]).then_inc(gate_exp, 1)
            act.wait_ge(gain_ready, 1)
            for g in range(10, NS - 1):
                gelus(g + 1, SH)
                store(g, g % 2)
                if g < 14:
                    high_rest(4 * E + g - 10)

            def expert_of(eng, r):
                return eng.value_load(tab[0:1, bass.ds(r * ROW + SLOTS, 1)], min_val=0, max_val=E - 1)

            def bias(r, parity):
                e = expert_of(act, r)
                act.wait_ge(y_done, r + (R0 + 1))
                if not (isinstance(r, int) and r < 2):
                    act.wait_ge(y_free, r - 1)
                for db in range(DB):
                    i = nc.scalar.activation(
                        ytmp[:, bass.ds(parity, 1), db, 0:RC].rearrange("p o c -> p (o c)"),
                        psy2[:, bass.ds(parity, 1), db * RC:(db + 1) * RC].rearrange("p o c -> p (o c)"),
                        ACT.Identity, bias=b2[:, bass.ds(e * DB + db, 1)], scale=1.0 / WS)
                i.then_inc(y_taken, 1)

            act.wait_ge(tab_ready, 1)
            gelus(R0, expert_of(act, 0), RC)
            store(NS - 1, 1)

            def step(r, parity):
                gelus(r + R0, expert_of(act, r), RC)
                bias(r - 1, 1 - parity)

            step(1, 1)
            for n in range(4):
                high_rest(4 * E + 4 + n)
                step(2 + n, n % 2)
            last, parity = expert_loops(act, 6, step)
            bias(last, parity)
            stage2_act(act)

        @block.tensor
        def _(pe):
            def hidden(g, e, rhs, size=CH):
                first = isinstance(g, int) and g == 0
                for j in range(4):
                    if not first:
                        pe.wait_ge(h32_ready, g * 4 + (j - 3))
                    for k in range(2):
                        hb = 2 * j + k
                        out = ps1[j][:, k * size:(k + 1) * size]
                        n = 0
                        for wp, xp in ((0, 0), (0, 1), (1, 0)):
                            for db in range(DB):
                                mm = pe.matmul(out, w1(e, wp, db, hb), rhs(xp, db),
                                               start=(n == 0), stop=(n == 5))
                                n += 1
                    mm.then_inc(l1_done, 1)

            def hidden_shared(g):
                if isinstance(g, int) and g % 2 == 0 and g >= 2:
                    pe.wait_ge(x_split, g // 2)
                hidden(g, SH, lambda xp, db: xtok[:, 2 * xp + db, bass.ds(g * CB, CB), :])

            def expert_of(r):
                return pe.value_load(tab[0:1, bass.ds(r * ROW + SLOTS, 1)], min_val=0, max_val=E - 1)

            def hidden_expert(r, parity):
                pe.wait_ge(x_staged, r + 1)
                hidden(r + R0, expert_of(r), lambda xp, db: xs[:, parity, 2 * xp + db, 0:RC], RC)

            def output(g, e, parity, size=CH):
                if not (isinstance(g, int) and g < 2):
                    pe.wait_ge(y_taken, g - 1)
                pe.wait_ge(h_ready, g * 4 + 4)
                for db in range(DB):
                    out = psy2[:, bass.ds(parity, 1), db * size:(db + 1) * size].rearrange("p o c -> p (o c)")
                    n = 0
                    for hb in range(HB):
                        for wp, hp in ((0, 0), (0, 1), (1, 0)):
                            h = hbuf[:, bass.ds(parity, 1), hp, hb, 0:size].rearrange("p o c -> p (o c)")
                            mm = pe.matmul(out, w2(e, wp, hb, db), h, start=(n == 0), stop=(n == 3 * HB - 1))
                            n += 1
                mm.then_inc(y_done, 1)

            pe.wait_ge(w_split, 2)
            hidden_shared(0)
            hidden_shared(1)
            pe.wait_ge(w_split, 3)
            output(0, SH, 0)
            hidden_shared(2)
            output(1, SH, 1)
            with pe.Fori(1, 5) as q:
                hidden_shared(q * 2 + 1)
                output(q * 2, SH, 0)
                pe.wait_ge(x_split, q + 1)
                hidden_shared(q * 2 + 2)
                output(q * 2 + 1, SH, 1)
            pe.wait_ge(gate_in, 1)
            for k in range(3 * DB):
                pe.matmul(psg[0:NB, 0:E], gin[:, k, :], gw[:, k, :], start=(k == 0), stop=(k == 3 * DB - 1))
            for k in range(DB):
                mm = pe.matmul(psg[0:NB, 8:8 + 2 * E], silc[:, k, :], tw[:, k, :], start=(k == 0), stop=(k == DB - 1))
            mm.then_inc(gate_mm, 1)
            hidden_shared(11)
            output(10, SH, 0)
            pe.wait_ge(sel_ready, 1)
            pe.matmul(psg[0:NB, 0:E], tri, G[:, 9, :], start=True, stop=True)
            pe.matmul(psg[0:NB, 8:8 + E], onesm[0:NB, 0:NB], G[:, 9, :], start=True, stop=True).then_inc(rank_mm, 1)
            hidden_shared(12)
            output(11, SH, 1)
            for e in range(E):
                pe.wait_ge(hot_ready, e + 1)
                for part in range(2):
                    pe.matmul(psg[0:1, 0:NSLOT], lhs[:, e % 2, part, 0:1], hot[:, e % 2, :],
                              start=(e == 0 and part == 0), stop=(e == E - 1 and part == 1))
                for part in range(2):
                    mm = pe.matmul(pst[:, 0:NSLOT], lhs[:, e % 2, part, 1:1 + P], hot[:, e % 2, :],
                                   start=(e == 0 and part == 0), stop=(e == E - 1 and part == 1))
                mm.then_inc(tab_mm, 1)
            hidden_shared(13)
            output(12, SH, 0)
            pe.wait_ge(key_ready, 1)
            for g in range(MG):
                mm = pe.matmul(pst[:, g * P:(g + 1) * P], onesm[:, :], kdiag[:, g, :], start=True, stop=True)
            mm.then_inc(key_mm, 1)
            for g in range(13, NS - 1):
                hidden_shared(g + 1)
                output(g, SH, g % 2)
            pe.wait_ge(r_split, 4 * E)
            hidden_expert(0, 0)
            output(NS - 1, SH, 1)

            def step(r, parity):
                hidden_expert(r, parity)
                output(r + (R0 - 1), expert_of(r - 1), 1 - parity, RC)

            step(1, 1)
            last, parity = expert_loops(pe, 2, step)
            output(last + R0, expert_of(last), parity, RC)
            stage2_pe(pe)

        @block.vector
        def _(dve):
            steps = [0]

            def link(i):
                steps[0] += 1
                i.then_inc(dv, 1)
                dve.wait_ge(dv, steps[0])

            def split_shared(k, lo, n, part_off):
                src = ws32[:, lo:lo + n]
                hi = W[:, SH * WE + part_off:SH * WE + part_off + n]
                low = W[:, SH * WE + part_off + 2048:SH * WE + part_off + 2048 + n]
                dve.wait_ge(ws_in[k], 16)
                link(nc.vector.tensor_scalar(hi, src, WS, None, ALU.mult))
                return nc.vector.scalar_tensor_tensor(low, src, WS, hi, ALU.mult, ALU.subtract)

            split_shared(0, 0, 2048, 0).then_inc(w_split, 1)
            dve.wait_ge(x_in[0], 16)
            src, hi, low = x_piece(0)
            link(nc.vector.tensor_copy(hi, src))
            nc.vector.tensor_tensor(low, src, hi, ALU.subtract).then_inc(w_split, 1)
            split_shared(1, 2048, 2048, 4096).then_inc(w_split, 1)

            def splits(g, parity, size=CH):
                if not (isinstance(g, int) and g < 2):
                    dve.wait_ge(y_done, g - 1)
                for j in range(4):
                    dve.wait_ge(h32_ready, g * 4 + (j + 1))
                    src = h32[:, j, 0:2 * size].rearrange("p (k t) -> p k t", k=2)
                    hi = hbuf[:, parity, 0, 2 * j:2 * j + 2, 0:size]
                    nc.vector.tensor_copy(hi, src).then_inc(h_hi, 1)
                    dve.wait_ge(h_hi, g * 4 + (j + 1))
                    nc.vector.tensor_tensor(hbuf[:, parity, 1, 2 * j:2 * j + 2, 0:size], src, hi,
                                            ALU.subtract).then_inc(h_ready, 1)

            def low_piece(e, k):
                dve.wait_ge(hi_ready, e * 4 + (k + 1))
                at = k * 1024 + (2048 if k >= 2 else 0)
                nc.vector.scalar_tensor_tensor(W[:, bass.ds(e * WE + (at + 2048), 1024)], stage[:, k % 2, :], WS,
                                               W[:, bass.ds(e * WE + at, 1024)],
                                               ALU.mult, ALU.subtract).then_inc(r_split, 1)

            def low_rest(n):
                dve.wait_ge(hi_ready, n + 1)
                for src, hi, lo, gain in rest_parts(n):
                    scale = WS if gain is None else gams[:, gain:gain + 1]
                    i = nc.vector.scalar_tensor_tensor(lo, src, scale, hi, ALU.mult, ALU.subtract)
                i.then_inc(r_split, 1)

            def sums(q):
                dve.wait_ge(x_in[q], 16)
                v = x32[:, :, q * 512:(q + 1) * 512].rearrange("p d (b t) -> p d b t", t=NT)
                for r, (lo, hi) in enumerate(((0, HEAD), (HEAD, HP), (HP, NT))):
                    i = nc.vector.tensor_reduce(gsum[:, :, r, q * 8:(q + 1) * 8], v[:, :, :, lo:hi],
                                                AX.X, ALU.add)
                i.then_inc(sums_done, 1)

            for g in range(4):
                splits(g, g % 2)
                sums(2 * g)
                sums(2 * g + 1)
                if g == 0:
                    dve.wait_ge(cond_exp, 1)
                    link(nc.vector.tensor_scalar(silc, silc, 1.0, None, ALU.add))
                    link(nc.vector.reciprocal(silc, silc))
                    link(nc.vector.tensor_tensor(silc, silc, cond, ALU.mult))
            low_piece(0, 0)
            low_piece(0, 1)
            splits(4, 0)
            low_piece(0, 2)
            low_piece(0, 3)
            dve.wait_ge(sums_done, 8)
            link(nc.vector.tensor_tensor(gin[:, DB:2 * DB, :], gsum[:, :, 0, :], gsum[:, :, 1, :], ALU.add))
            link(nc.vector.tensor_tensor(gin[:, 0:DB, :], gin[:, DB:2 * DB, :], gsum[:, :, 2, :], ALU.add))
            link(nc.vector.tensor_tensor(gin[:, 2 * DB:3 * DB, :], gsum[:, :, 2, :], gsum[:, :, 1, :], ALU.add))
            link(nc.vector.tensor_scalar(gin[:, 0:DB, :], gin[:, 0:DB, :], 1.0 / NT, None, ALU.mult))
            nc.vector.tensor_scalar(gin[:, DB:3 * DB, :], gin[:, DB:3 * DB, :], 1.0 / HP, None,
                                    ALU.mult).then_inc(gate_in, 1)
            with dve.Fori(1, E) as e:
                splits(e * 2 + 3, 1)
                low_piece(e, 0)
                low_piece(e, 1)
                splits(e * 2 + 4, 0)
                low_piece(e, 2)
                low_piece(e, 3)
            dve.wait_ge(const_ready, 1)
            dve.wait_ge(gate_mm, 1)
            link(nc.vector.tensor_tensor(G[:, 0, :], psg[0:NB, 0:E], gb[:, :], ALU.add))
            link(nc.vector.tensor_tensor(G[:, 1, :], psg[0:NB, 8:8 + E], tb[:, 0:E], ALU.add))
            link(nc.vector.tensor_tensor(G[:, 5, :], psg[0:NB, 8 + E:8 + 2 * E], tb[:, E:2 * E], ALU.add))
            link(nc.vector.scalar_tensor_tensor(G[:, 2, :], G[:, 1, :], 1.0, G[:, 0, :], ALU.add, ALU.mult))
            link(nc.vector.tensor_tensor(G[:, 2, :], G[:, 2, :], G[:, 5, :], ALU.add))
            link(nc.vector.tensor_reduce(G[:, 3, 1:2], G[:, 2, :], AX.X, ALU.max))
            nc.vector.tensor_scalar(G[:, 3, 0:1], G[:, 3, 1:2], -1.0, None, ALU.mult).then_inc(gate_log, 1)
            dve.wait_ge(gate_exp, 1)
            link(nc.vector.tensor_reduce(G[:, 3, 2:3], G[:, 4, :], AX.X, ALU.add))
            link(nc.vector.reciprocal(G[:, 3, 3:4], G[:, 3, 2:3]))
            link(nc.vector.tensor_scalar(G[:, 6, :], G[:, 4, :], G[:, 3, 3:4], None, ALU.mult))
            for n, (score, pick) in enumerate(((6, 7), (10, 8))):
                link(nc.vector.tensor_reduce(G[:, 11, n:n + 1], G[:, score, :], AX.X, ALU.max))
                link(nc.vector.scalar_tensor_tensor(G[:, 12, :], G[:, score, :], G[:, 11, n:n + 1], G[:, 20, :],
                                                    ALU.is_equal, ALU.mult))
                link(nc.vector.tensor_reduce(G[:, 13, n:n + 1], G[:, 12, :], AX.X, ALU.min))
                link(nc.vector.tensor_scalar(G[:, pick, :], G[:, 20, :], G[:, 13, n:n + 1], None, ALU.is_equal))
                if n == 0:
                    link(nc.vector.scalar_tensor_tensor(G[:, 10, :], G[:, 7, :], -2.0, G[:, 6, :],
                                                        ALU.mult, ALU.add))
            nc.vector.tensor_tensor(G[:, 9, :], G[:, 7, :], G[:, 8, :], ALU.add).then_inc(sel_ready, 1)
            dve.wait_ge(sel_ready, 1)
            link(nc.vector.tensor_tensor(G[:, 14, 0:1], G[:, 11, 0:1], G[:, 11, 1:2], ALU.add))
            link(nc.vector.tensor_scalar(G[:, 14, 0:1], G[:, 14, 0:1], 1e-8, None, ALU.add))
            link(nc.vector.reciprocal(G[:, 14, 1:2], G[:, 14, 0:1]))
            link(nc.vector.scalar_tensor_tensor(G[:, 15, :], G[:, 6, :], G[:, 14, 1:2], G[:, 9, :],
                                                ALU.mult, ALU.mult))
            splits(11, 1)
            low_rest(4 * E)
            dve.wait_ge(rank_mm, 1)
            link(nc.vector.tensor_copy(G[:, 16, :], psg[0:NB, 0:E]))
            link(nc.vector.tensor_tensor(G[:, 17, :], psg[0:NB, 8:8 + E], G[:, 24, :], ALU.mult))
            for e in range(E):
                link(nc.vector.tensor_scalar(gcnt[:, e, :], siota[:, 0:NCNT * SLOTS:SLOTS], G[:, 17, e:e + 1],
                                             None, ALU.is_lt))
            link(nc.vector.tensor_reduce(G[:, 18, :], gcnt[:, :, :], AX.X, ALU.add))
            for e in range(1, E):
                link(nc.vector.tensor_tensor(G[:, 19, e:e + 1], G[:, 19, e - 1:e], G[:, 18, e - 1:e], ALU.add))
            link(nc.vector.tensor_tensor(G[:, 22, :], G[:, 16, :], G[:, 24, :], ALU.mult))
            link(nc.vector.scalar_tensor_tensor(G[:, 22, :], G[:, 19, :], float(SLOTS), G[:, 22, :],
                                                ALU.mult, ALU.add))
            link(nc.vector.tensor_scalar(G[:, 23, :], G[:, 9, :], -1e4, 1e4, ALU.mult, ALU.add))
            link(nc.vector.tensor_tensor(G[:, 22, :], G[:, 22, :], G[:, 23, :], ALU.add))
            link(nc.vector.tensor_tensor(G[:, 23, :], G[:, 22, :], G[:, 24, :], ALU.add))
            link(nc.vector.scalar_tensor_tensor(G[:, 26, :], G[:, 22, :], -float(SEG), G[:, 25, :],
                                                ALU.mult, ALU.add))
            link(nc.vector.tensor_tensor(G[:, 26, :], G[:, 26, :], G[:, 9, :], ALU.mult))
            for e in range(E):
                if e >= 2:
                    dve.wait_ge(tab_mm, e - 1)
                link(nc.vector.tensor_scalar(hot[:, e % 2, :], siota, G[:, 22, e:e + 1], None, ALU.is_ge))
                link(nc.vector.scalar_tensor_tensor(hot[:, e % 2, :], siota, G[:, 23, e:e + 1], hot[:, e % 2, :],
                                                    ALU.is_lt, ALU.mult))
                link(nc.vector.tensor_copy(lval[:, 0:1], G[:, 26, e:e + 1]))
                link(nc.vector.tensor_copy(lval[:, 1:1 + P], G[:, 15, e:e + 1].to_broadcast([NB, P])))
                link(nc.vector.tensor_copy(lhs[:, e % 2, 0, 0:1 + P], lval[:, 0:1 + P]))
                nc.vector.tensor_tensor(lhs[:, e % 2, 1, 0:1 + P], lval[:, 0:1 + P], lhs[:, e % 2, 0, 0:1 + P],
                                        ALU.subtract).then_inc(hot_ready, 1)
            splits(12, 0)
            low_rest(4 * E + 1)
            dve.wait_ge(tab_mm, E)
            link(nc.vector.tensor_copy(wrow[:, :], pst[:, 0:NSLOT]))
            link(nc.vector.tensor_tensor(fa, psg[0:1, 0:NSLOT], trow, ALU.add))
            link(nc.vector.scalar_tensor_tensor(fa, psg[0:1, 0:NSLOT], 0.5, fa, ALU.is_gt, ALU.mult))
            link(nc.vector.tensor_tensor(fa, fa, srow, ALU.add))
            tv = tab[:, 0:NR * ROW].rearrange("p (r k) -> p r k", k=ROW)
            link(nc.vector.tensor_copy(tv[:, :, 0:SLOTS], fa.rearrange("p (r j) -> p r j", j=SLOTS)))
            ce = yw[0:1, 0:4 * NR].rearrange("p (k r) -> p k r", k=4)
            for e in range(1, E):
                link(nc.vector.tensor_scalar(ce[:, e, :], siota[0:1, 0:NR], G[0:1, 19, e:e + 1], None, ALU.is_ge))
            link(nc.vector.tensor_tensor(ce[:, 1, :], ce[:, 1, :], ce[:, 2, :], ALU.add))
            link(nc.vector.tensor_tensor(ce[:, 1, :], ce[:, 1, :], ce[:, 3, :], ALU.add))
            link(nc.vector.tensor_copy(tv[:, :, SLOTS], ce[:, 1, :]))
            total, even = G[0:1, 27, 0:1], G[0:1, 27, 1:2]
            link(nc.vector.tensor_tensor(total, G[0:1, 19, E - 1:E], G[0:1, 18, E - 1:E], ALU.add))
            link(nc.vector.tensor_scalar(ce[:, 0, 0:NR // 2], siota[0:1, 0:NR:2], total, None, ALU.is_lt))
            link(nc.vector.tensor_reduce(even, ce[:, 0, 0:NR // 2], AX.X, ALU.add))
            link(nc.vector.tensor_scalar(even, even, -2.0, 1.0, ALU.mult, ALU.add))
            link(nc.vector.tensor_tensor(even, even, total, ALU.add))
            link(nc.vector.tensor_scalar(total, total, -2.0, None, ALU.add))
            link(nc.vector.tensor_copy(tab[:, NR * ROW:NR * ROW + 2], G[0:1, 27, 0:2]))
            dve.wait_ge(idx_in, 2 * 16)
            kb, kt, t0, t1 = (f4[:, n, :] for n in (8, 9, 10, 11))
            kk, tt = f4[:, 8:10, :], f4[:, 10:12, :]
            link(nc.vector.tensor_copy(kk, kint[:, :, :]))
            link(nc.vector.tensor_scalar(tt, kk, 0.0, float(NT), ALU.is_lt, ALU.mult))
            link(nc.vector.tensor_tensor(kk, kk, tt, ALU.add))
            link(nc.vector.tensor_scalar(tt, kk, float(NT - 1), None, ALU.is_le))
            link(nc.vector.scalar_tensor_tensor(tt, kk, 0.0, tt, ALU.is_ge, ALU.mult))
            link(nc.vector.tensor_tensor(t0, t0, t1, ALU.mult))
            link(nc.vector.scalar_tensor_tensor(kb, kb, float(NT), kt, ALU.mult, ALU.add))
            for edge, move in ((HEAD, NT - 2 * HEAD), (2 * HEAD, HEAD - NT)):
                link(nc.vector.tensor_scalar(t1, kt, float(edge), float(move), ALU.is_ge, ALU.mult))
                link(nc.vector.tensor_tensor(kb, kb, t1, ALU.add))
            link(nc.vector.scalar_tensor_tensor(kb, kb, -2.0 * TOK, t0, ALU.add, ALU.mult))
            for g in range(MG):
                i = nc.vector.tensor_scalar(kdiag[:, g, :], ident[:, :], kb[:, g:g + 1], None, ALU.mult)
            i.then_inc(key_ready, 1)
            splits(13, 1)
            low_rest(4 * E + 2)
            dve.wait_ge(key_mm, 1)
            for m in range(MG):
                link(nc.vector.scalar_tensor_tensor(kcmp, pst[:, :], kb[:, m:m + 1], iot,
                                                    ALU.is_equal, ALU.mult))
                link(nc.vector.tensor_reduce(f4[:, 0, m:m + 1], kcmp, AX.X, ALU.min))
            link(nc.vector.tensor_tensor(f4[:, 2, :], f4[:, 0, :], f4[:, 1, :], ALU.is_equal))
            link(nc.vector.tensor_tensor(f4[:, 3, :], f4[:, 2, :], kb, ALU.mult))
            link(nc.vector.tensor_scalar(f4[:, 4, :], f4[:, 3, :], 2.0 * TOK, None, ALU.add))
            link(nc.vector.tensor_copy(sid[:, :], f4[:, 4, :]))
            link(nc.vector.tensor_scalar(f4[:, 5, :], f4[:, 4, :], float(TOK), None, ALU.is_lt))
            link(nc.vector.tensor_tensor(f4[:, 6, :], f4[:, 5, :], f4[:, 4, :], ALU.mult))
            nc.vector.tensor_copy(gid[:, :], f4[:, 6, :]).then_inc(tab_ready, 1)
            splits(14, 0)
            low_rest(4 * E + 3)
            splits(15, 1)

            dve.wait_ge(tab_ready, 1)
            regs = [dve.alloc_register(f"slot_address{j}") for j in range(SLOTS)]

            def add_slots(r, parity):
                dve.load(regs, tab[0:1, bass.ds(r * ROW, SLOTS)])
                cols = [dve.snap(x, min_val=0, max_val=COLS - SEG) for x in regs]
                dve.wait_ge(y_taken, r + (R0 + 1))
                if not isinstance(r, int):
                    dve.wait_ge(y_free, r)
                for j in range(SLOTS):
                    at = acc[:, :, bass.ds(cols[j], SEG)]
                    y = ytmp[:, bass.ds(parity, 1), :, j * SEG:(j + 1) * SEG].rearrange("p o d c -> p (o d) c")
                    i = nc.vector.scalar_tensor_tensor(at, y, wrow[:, bass.ds(r * SLOTS + j, 1)], at,
                                                       ALU.mult, ALU.add)
                i.then_inc(y_free, 1)

            splits(R0, 0, RC)

            def step(r, parity):
                splits(r + R0, parity, RC)
                add_slots(r - 1, 1 - parity)

            step(1, 1)
            for n in range(4):
                low_rest(4 * E + 4 + n)
                step(2 + n, n % 2)
            last, parity = expert_loops(dve, 6, step)
            add_slots(last, parity)
            stage2_dve(dve, link)

        @block.gpsimd
        def _(pool):
            steps = [0]

            def link(i):
                steps[0] += 1
                i.then_inc(pool_step, 1)
                pool.wait_ge(pool_step, steps[0])

            def count_up(out, pattern, base, channel):
                link(nc.gpsimd.iota(out, pattern=pattern, base=base, channel_multiplier=channel,
                                    allow_small_or_imprecise_dtypes=True))

            def split_x(q):
                pool.wait_ge(x_in[q], 16)
                src, hi, lo = x_piece(q)
                link(nc.gpsimd.tensor_copy(hi, src))
                nc.gpsimd.tensor_tensor(lo, src, hi, ALU.subtract).then_inc(x_split, 1)

            for q in range(1, 8):
                split_x(q)
            pool.wait_ge(small_in, 11 * 16)
            nc.gpsimd.tensor_scalar(gams[:, :], gam[:, :], WS, None, ALU.mult).then_inc(gain_ready, 1)
            for c in (0, BS - 1):
                link(nc.gpsimd.memset(xcols[:, :, :, c:c + 1], 0.0))
            link(nc.gpsimd.memset(X[:, :, NB * BS:COLS], 0.0))
            link(nc.gpsimd.memset(onesm[:, :], 1.0))
            link(nc.gpsimd.affine_select(out=ident[:, :], in_=onesm[:, :], compare_op=ALU.is_equal, fill=0.0,
                                         base=0, pattern=[[1, P]], channel_multiplier=-1))
            link(nc.gpsimd.affine_select(out=tri, in_=onesm[0:NB, 0:NB], compare_op=ALU.is_gt, fill=0.0,
                                         base=0, pattern=[[1, NB]], channel_multiplier=-1))
            count_up(siota, [[1, NSLOT]], 0, 0)
            count_up(G[:, 20, :], [[1, E]], -E, 0)
            for e in range(E):
                link(nc.gpsimd.memset(G[:, 24, e:e + 1], float(KEPT[e])))
                count_up(G[:, 25, e:e + 1], [[0, 1]], SEG * KEPT0[e] + FAR, BS)
            link(nc.gpsimd.memset(G[:, 19, :], 0.0))
            count_up(trow, [[RC, NR], [0, SLOTS]], -FAR - NB * BS, 0)
            count_up(srow, [[0, NR], [SEG, SLOTS]], NB * BS, 0)
            count_up(iot, [[1, M]], -M, 0)
            count_up(f4[:, 1, :], [[P, MG]], -M, 1)
            nc.gpsimd.memset(tab[:, :], 0).then_inc(const_ready, 1)
            pool.wait_ge(tab_ready, 1)
            for c in (0, BS - 1):
                link(nc.gpsimd.memset(acols[:, :, :, c:c + 1], 0.0))
            link(nc.gpsimd.memset(acc[:, :, NB * BS:COLS], 0.0))
            regs = [pool.alloc_register(f"pool_address{j}") for j in range(SLOTS)]

            def stage_columns(r, parity):
                pool.load(regs, tab[0:1, bass.ds(r * ROW, SLOTS)])
                cols = [pool.snap(x, min_val=0, max_val=COLS - SEG) for x in regs]
                if not (isinstance(r, int) and r < 2):
                    pool.wait_ge(l1_done, r * 4 + (R0 * 4 - 4))
                for j in range(SLOTS):
                    i = nc.gpsimd.tensor_copy(xs[:, parity, :, j * SEG:(j + 1) * SEG],
                                              X[:, :, bass.ds(cols[j], SEG)])
                i.then_inc(x_staged, 1)

            stage_columns(0, 0)
            stage_columns(1, 1)
            expert_loops(pool, 2, stage_columns)
            stage2_pool(pool, link)


def kernel(**inputs):
    import numpy as np
    import concourse.bacc as bacc
    from concourse.bass_utils import run_bass_kernel_spmd as run

    v = {k.removeprefix("L0_"): np.asarray(x) for k, x in inputs.items()}
    order = np.r_[0:HEAD, 2 * HEAD:NT, HEAD:2 * HEAD]
    x = v["x"][:, order, :].reshape(TOK, D)

    def rows(*parts):
        return np.concatenate([np.asarray(q).reshape(-1, P) for q in parts], 0).T

    first = np.stack([np.concatenate([v[f"ffn_s{w}"][None], v[f"ffn_e{w}"]]) for w in ("w1", "w2")], 1)
    last = np.concatenate([v["ffn_sw3"][None], v["ffn_ew3"]])
    arrays = {
        "xT": x.T.reshape(DB, P, TOK).transpose(1, 0, 2),
        "xR": x,
        "condT": v["cond_1024"].T.reshape(DB, P, NB).transpose(1, 0, 2),
        "ew1": v["cond_ew1"], "ew2": v["cond_ew2"], "sw1": v["cond_sw1"], "sw2": v["cond_sw2"],
        "b1": rows(v["cond_eb1"], v["cond_sb1"]), "b2": rows(v["cond_eb2"], v["cond_sb2"]),
        "gate_w": v["cond_gate_w"], "gate_b": v["cond_gate_b"],
        "time_w": v["cond_time_w"], "time_b": v["cond_time_b"],
        "index_b4": v["ffn_index_b"].reshape(MG, P).T, "index_t4": v["ffn_index_t"].reshape(MG, P).T,
        "fw": first.reshape(NJ, 2, FH, DB, P).transpose(4, 0, 1, 3, 2).reshape(P, NJ * 2 * DB * FH),
        "w3t": last.transpose(2, 0, 1).reshape(P, NJ * D),
        "fb1": rows(v["ffn_sb1"], v["ffn_eb1"]), "fb2": rows(v["ffn_sb2"], v["ffn_eb2"]),
        "gam": rows(v["ffn_s_ln_g"], v["ffn_sel_ln_g"]), "bet": rows(v["ffn_s_ln_b"], v["ffn_sel_ln_b"]),
        "b3s": v["ffn_sb3"].reshape(1, D), "b3e": v["ffn_eb3"],
        "rw": np.concatenate([v["ffn_sg_w"], v["ffn_eg_w"]]).T.reshape(DB, P, 9).transpose(1, 0, 2),
        "rb": np.concatenate([v["ffn_sg_b"], v["ffn_eg_b"]]), "eb": v["ffn_exp_bias"],
    }
    arrays = {n: np.ascontiguousarray(q) for n, q in arrays.items()}
    nc = bacc.Bacc("TRN2", target_bir_lowering=False, num_devices=1)
    a = {n: nc.dram_tensor(f"in_{n}", q.shape, mybir.dt.from_np(q.dtype), kind="ExternalInput").ap()
         for n, q in arrays.items()}
    a["out"] = nc.dram_tensor("out_rows", (TOK, D), F32, kind="ExternalOutput").ap()
    a["scratch"] = nc.dram_tensor("stage1_rows", (TOK, 2 * D), F16, kind="Internal").ap()
    program(nc, a)
    r = run(nc, [{f"in_{n}": q for n, q in arrays.items()}], core_ids=[0])
    got = np.asarray(r.results[0]["out_rows"]).reshape(NB, NT, D)
    return got[:, np.argsort(order), :]
```

```python
from contextlib import ExitStack, contextmanager

import concourse.bass as bass
from concourse import mybir

F32 = mybir.dt.float32
F16 = mybir.dt.float16
I32 = mybir.dt.int32
ACT = mybir.ActivationFunctionType
ALU = mybir.AluOpType
AX = mybir.AxisListType

P = 128
NB, NT, D = 64, 64, 256
TOK = NB * NT
H = 1024
E, SH = 4, 4
DB, HB = D // P, H // P
HEAD = NT // 3
HP = HEAD + (NT - 2 * HEAD)
WS = 1024.0
CH = 256
NS = TOK // CH
SEG = NT - 2 * HEAD
BS = 3 * SEG
CB = CH // NT
SLOTS = 11
RC = SLOTS * SEG
KEPT = (3, 2, 2, 3)
KEPT0 = (0, 0, 1, 0)
NR = (2 * 3 * NB + E * (SLOTS - 1)) // SLOTS
NRMIN = -(-2 * 2 * NB // SLOTS)
NSLOT = NR * SLOTS
ROW = SLOTS + 1
NCNT = -(-3 * NB // SLOTS)
FAR = 16384
COLS = NB * BS + SLOTS * SEG + 6
WE = 8192
FE, FH, M = 8, 128, 512
MG = M // P
EPS = 1e-5
NJ = FE + 1
FC = 512
NQ = TOK // FC
NH = 2 * NQ


@contextmanager
def by_two(eng, start, end):
    with eng.Fori(0, (end - start) // 2) as i:
        yield i * 2 + start


def program(nc, a):
    with ExitStack() as ctx:
        def sb(name, shape, dt=F32):
            return ctx.enter_context(nc.sbuf_tensor(name, shape, dt))

        def sem(name):
            return ctx.enter_context(nc.semaphore(name))

        W = sb("W", [P, (E + 1) * WE], F16)
        X = sb("X", [P, 2 * DB, COLS], F16)
        acc = sb("acc", [P, DB, COLS])
        hbuf = sb("hbuf", [P, 2, 2, HB, CH], F16)
        h32 = sb("h32", [P, 4, 2 * CH])
        xs = sb("xs", [P, 2, 2 * DB, CH], F16)
        ytmp = sb("ytmp", [P, 2, DB, CH])
        ident = sb("ident", [P, P])
        onesm = sb("onesm", [P, P])
        tri = sb("tri", [P, P])
        stage = sb("stage", [P, 2, 1024])
        F0 = sb("F0", [P, 1024], F16)
        V = sb("V", [P, NJ, 2, D], F16)
        b1 = sb("b1", [P, (E + 1) * HB])
        b2 = sb("b2", [P, (E + 1) * DB])
        wrow = sb("wrow", [P, NSLOT])
        vals = sb("vals", [P, MG, 2], F16)
        tab = sb("tab", [1, NR * ROW + 4], I32)
        gw = sb("gw", [P, 3 * DB, E])
        tw = sb("tw", [P, DB, 2 * E])
        gb = sb("gb", [NB, E])
        tb = sb("tb", [NB, 2 * E])
        G = sb("G", [NB, 28, E])
        gcnt = sb("gcnt", [NB, E, NCNT])
        fb1 = sb("fb1", [P, NJ])
        fb2 = sb("fb2", [P, NJ])
        gam = sb("gam", [P, 2])
        bet = sb("bet", [P, 2])
        gid = sb("gid", [P, MG], I32)
        sid = sb("sid", [P, MG], I32)
        f4 = sb("f4", [P, 16, MG])
        kint = sb("kint", [P, 2, MG], I32)
        gams = sb("gams", [P, 2])

        W32 = W[:, :].bitcast(F32)
        ws32 = W32[:, WE // 2:WE]
        x32 = W32[:, WE:WE + DB * TOK].rearrange("p (d t) -> p d t", d=DB)
        xcols = X[:, :, 0:NB * BS].rearrange("p k (b s) -> p k b s", s=BS)
        xtok = xcols[:, :, :, 1:1 + NT]
        acols = acc[:, :, 0:NB * BS].rearrange("p k (b s) -> p k b s", s=BS)
        atok = acols[:, :, :, 1:1 + NT]

        lent = acc[:, 0, 10 * CB * BS:10 * CB * BS + 16 * NB]
        gsum = lent[:, 0:6 * NB].rearrange("p (d r b) -> p d r b", d=DB, r=3)
        gin = lent[:, 6 * NB:12 * NB].rearrange("p (k b) -> p k b", b=NB)
        cond = lent[:, 12 * NB:14 * NB].rearrange("p (d b) -> p d b", d=DB)
        silc = lent[:, 14 * NB:16 * NB].rearrange("p (d b) -> p d b", d=DB)
        iot = acc[:, 1, 15 * CB * BS:15 * CB * BS + M]
        trow = acc[0:1, 0, 14 * CB * BS:14 * CB * BS + NSLOT]
        xsw = xs[:, :, :, :].rearrange("p a b c -> p (a b c)")
        hot = xsw[0:NB, 0:2 * NSLOT].rearrange("p (u s) -> p u s", u=2)
        siota = xsw[0:NB, 2 * NSLOT:4 * NSLOT].bitcast(F32)
        yw = ytmp[:, :, :, :].rearrange("p a b c -> p (a b c)")
        lhs = yw[0:NB, 0:260].bitcast(F16).rearrange("p (u k c) -> p u k c", u=2, k=2)
        lval = yw[0:NB, 260:390]
        srow = yw[0:1, 512:512 + NSLOT]
        fa = yw[0:1, 0:NSLOT]
        kdiag = yw[:, 0:M].rearrange("p (g t) -> p g t", g=MG)
        kcmp = yw[:, 512:1024]
        oh16 = yw.bitcast(F16).rearrange("p (g s) -> p g s", g=MG)

        ps1 = [ctx.enter_context(nc.psum_tensor(f"ps_hidden{j}", [P, 512], F32)) for j in range(4)]
        psy2 = ctx.enter_context(nc.psum_tensor("ps_out", [P, 2, 512], F32))
        psy = [psy2[:, j, :] for j in range(2)]
        psg = ctx.enter_context(nc.psum_tensor("ps_small", [P, 512], F32))
        pst = ctx.enter_context(nc.psum_tensor("ps_turn", [P, 512], F32))

        def w1(e, part, db, hb):
            return W[:, bass.ds(e * WE + (part * 2048 + db * 1024 + hb * P), P)]

        def w2(e, part, hb, db):
            return W[:, bass.ds(e * WE + (4096 + part * 2048 + hb * D + db * P), P)]

        def fw(j, part, which, db):
            at = (part * 2 + which) * 2 * P + db * P
            if isinstance(j, int) and j == 0:
                return F0[:, at:at + P]
            return W[:, bass.ds((j - 1) * 1024 + (SH * WE + at), P)]

        start_in = [sem(f"start_in{n}") for n in range(8)]
        x_in = {q: sem(f"x_in{q}") for q in range(1, 8)}
        cond_in = sem("cond_in")
        first_in = sem("first_in")
        small_in = sem("small_in")
        idx_in = sem("idx_in")
        wr_in = [sem(f"wr_in{q}") for q in range(2)]
        start_hi = sem("start_hi")
        w_split = sem("w_split")
        x_split = sem("x_split")
        r_split = sem("r_split")
        const_ready = sem("const_ready")
        x_staged = sem("x_staged")
        l1_done = sem("l1_done")
        h32_ready = sem("h32_ready")
        h_hi = sem("h_hi")
        h_ready = sem("h_ready")
        y_done = sem("y_done")
        y_taken = sem("y_taken")
        y_free = sem("y_free")
        summed_all = sem("summed_all")
        gain_ready = sem("gain_ready")
        hi_ready = sem("hi_ready")
        key_ready = sem("key_ready")
        key_mm = sem("key_mm")
        valid_ready, place_mm, place_ready = sem("valid_ready"), sem("place_mm"), sem("place_ready")
        slots_ready, spare_ready = sem("slots_ready"), sem("spare_ready")
        pack_mm, rows_ready = sem("pack_mm"), sem("rows_ready")
        dv = sem("dv")
        cond_exp = sem("cond_exp")
        gate_in = sem("gate_in")
        gate_mm = sem("gate_mm")
        gate_log = sem("gate_log")
        gate_exp = sem("gate_exp")
        sel_ready = sem("sel_ready")
        rank_mm = sem("rank_mm")
        hot_ready = sem("hot_ready")
        tab_mm = sem("tab_mm")
        tab_ready = sem("tab_ready")
        sums_done = sem("sums_done")
        pool_step = sem("pool_step")

        block = ctx.enter_context(nc.Block())
        R0 = NS

        def half_x(f):
            b, t = slice(f * CB, (f + 1) * CB), slice(f * CH, (f + 1) * CH)
            return (a["xT"][:, :, t], x32[:, :, t], x32[:, :, t].rearrange("p d (b t) -> p d b t", t=NT),
                    xtok[:, 0:DB, b, :], xtok[:, DB:2 * DB, b, :], 1.0)

        def quarter_w1(c):
            h = slice(c * 2 * P, (c + 1) * 2 * P)
            v = [t.rearrange("p (k h) -> p k h", k=DB)[:, :, h]
                 for t in (ws32[:, 0:2048], W[:, SH * WE:SH * WE + 2048], W[:, SH * WE + 2048:SH * WE + 4096])]
            return (a["sw1"].rearrange("(k p) h -> p k h", p=P)[:, :, h], v[0], *v, WS)

        def half_w2(c):
            at = SH * WE + 4096 + c * 1024
            src = ws32[:, 2048 + c * 1024:3072 + c * 1024]
            return (a["sw2"][c * 512:(c + 1) * 512, :].rearrange("(k p) d -> p k d", p=P),
                    src.rearrange("p (k d) -> p k d", d=D), src, W[:, at:at + 1024], W[:, at + 2048:at + 3072], WS)

        opening = [half_x(0)] + [quarter_w1(c) for c in range(4)] + [half_x(1), half_w2(0), half_w2(1)]

        def piece_src(n):
            if n < 4 * E:
                e, k = n // 4, n % 4
                if k < 2:
                    return a["ew1"][e, k * P:(k + 1) * P, :]
                return a["ew2"][e, (k - 2) * 512:(k - 1) * 512, :].rearrange("(h p) d -> p h d", p=P)
            n -= 4 * E
            if n == 0:
                return a["fw"][:, 0:512]
            if n < 4:
                j0, j1 = ((0, 4), (4, 8), (8, 9))[n - 1]
                return a["w3t"][:, j0 * D:j1 * D]
            return a["fw"][:, 512 + (n - 4) * 1024:512 + (n - 3) * 1024]

        def piece_size(n):
            n -= 4 * E
            return {0: 512, 3: 256}.get(n, 1024)

        NPIECE = 4 * E + 4 + 4

        def rest_parts(n):
            src = stage[:, n % 2, 0:piece_size(n)]
            n -= 4 * E
            if n == 0:
                return [(src, F0[:, 0:512], F0[:, 512:1024], None)]
            if n < 4:
                j0, j1 = ((0, 4), (4, 8), (8, 9))[n - 1]
                s3 = src.rearrange("p (j d) -> p j d", d=D)
                cuts = ((0, 1), (1, 4)) if n == 1 else ((0, j1 - j0),)
                return [(s3[:, lo:hi, :], V[:, j0 + lo:j0 + hi, 0, :], V[:, j0 + lo:j0 + hi, 1, :],
                         0 if j0 + lo == 0 else 1) for lo, hi in cuts]
            at = [SH * WE + (2 * (n - 4) + j) * 1024 for j in range(2)]
            return [(src[:, j * 512:(j + 1) * 512], W[:, x:x + 512], W[:, x + 512:x + 1024], None)
                    for j, x in enumerate(at)]

        def expert_loops(eng, start, step):
            turns = (NRMIN - start) // 4
            with eng.Fori(0, turns) as q:
                for u in range(4):
                    step(q * 4 + (start + u), u % 2)
            for r in range(start + 4 * turns, NRMIN):
                step(r, r % 2)
            count = chunk_count(eng)

            def up_to(r, u, n):
                with eng.If(count > r + u):
                    step(r + u, u % 2)
                    if u + 1 < n:
                        up_to(r, u + 1, n)

            quads = (NR - NRMIN) // 4
            with eng.Fori(0, quads) as q:
                up_to(q * 4 + NRMIN, 0, 4)
            up_to(NRMIN + 4 * quads, 0, (NR - NRMIN) % 4)
            parity = eng.value_load(tab[0:1, NR * ROW + 1:NR * ROW + 2], min_val=0, max_val=1)
            return count - 1, parity

        def x_piece(q):
            b = slice(q * 8, (q + 1) * 8)
            return (x32[:, :, q * 512:(q + 1) * 512].rearrange("p d (b t) -> p d b t", t=NT),
                    xtok[:, 0:DB, b, :], xtok[:, DB:2 * DB, b, :])

        def chunk_count(eng):
            return eng.value_load(tab[0:1, NR * ROW:NR * ROW + 1], min_val=NRMIN - 2, max_val=NR - 2) + 2

        SW = W32[:, 0:E * WE // 2]

        def take(base, lo, shape, dt=F32):
            n = 1
            for s in shape:
                n *= s
            words = n if dt is not F16 else n // 2
            v = base[:, lo:lo + words]
            if dt is not F32:
                v = v.bitcast(dt)
            names = "abc"[:len(shape)]
            if len(shape) == 1:
                return v
            return v.rearrange(f"p ({' '.join(names)}) -> p {' '.join(names)}",
                               **{c: s for c, s in zip(names, shape)})

        gcs = take(SW, 0, [NQ, 2, FC], F16)
        w3r = take(SW, 4096, [NJ, D])
        cg = take(SW, 7552, [4, P], F16)
        xg = take(SW, 7808, [D])
        cgT = take(SW, 8064, [2 * DB, P], F16)
        tev = take(SW, 8320, [2, 1024], F16)
        moe = take(SW, 9344, [D])
        moe2 = ytmp[:, 1, 1, :]
        GC = NJ * P
        gcg = take(SW, 6400, [2, GC], F16)
        sg = take(SW, 9600, [GC])
        gg = take(SW, 9600 + GC, [GC])
        ggp = take(SW, 9600 + 2 * GC, [2, GC], F16)
        gcg32 = take(SW, 9600 + 3 * GC, [GC])
        sqg = take(SW, 9600 + 4 * GC, [GC])
        ut = take(SW, 9600 + 5 * GC, [2, 2 * D])
        hw = hbuf[:, :, :, :, :].rearrange("p a b c d -> p (a b c d)").bitcast(F32)
        s32 = take(hw, 0, [2, FC])
        g32 = take(hw, 1024, [2, FC])
        ghl = take(hw, 2048, [2, 2, FC], F16)
        gc32 = h32[:, 0:2, :]
        sq = h32[:, 2:4, :]
        turned = [pst[:, :].bitcast(F16), psy[1].bitcast(F16)]
        xw = X[:, :, :].bitcast(F32)
        stf = stage[:, :, :].rearrange("p a b -> p (a b)")
        id16 = take(stf, 512, [P], F16)
        betrep = stf[:, 128:256]
        betm = take(stf, 256, [FE, FE])
        Cm = take(stf, 448, [P], F16)
        b3s = stf[0:1, 1024:1280]
        b3e = stf[0:FE, 1280:1536]
        rwr = take(stf, 1536, [DB, 9])
        rws = take(stf, 1560, [2, DB, 10], F16)
        rb = stf[:, 1584:1593]
        eb = stf[:, 1600:1608]
        io8 = stf[:, 1608:1616]
        fb2s = stf[:, 1620:1620 + NJ]
        rlg = stf[:, 1640:1649]
        rsg = stf[:, 1650:1659]
        rsel = stf[:, 1660:1668]
        rcand = stf[:, 1670:1678]
        roh = stf[:, 1680:1688]
        rm = stf[:, 1690:1698]
        rse = stf[:, 1700:1708]
        rstdg = stf[:, 1710:1710 + NJ]
        rstd = stf[:, 1720:1720 + NQ * MG]
        c0b = ytmp[:, 0, 0, :]
        ce8 = ytmp[0:FE, 0, 1, :]
        ohT = ytmp[0:FE, 1, 0, 0:P]

        misc_in, w3_in, xg_in, cg_in = sem("misc_in"), sem("w3_in"), sem("xg_in"), sem("cg_in")
        w3s_in = sem("w3s_in")
        x_rows_in = [sem(f"x_rows_in{q}") for q in range(NQ // 2)]
        const2_ready = sem("const2_ready")
        c_hi, c_lo, c_lo_pool = sem("c_hi"), sem("c_lo"), sem("c_lo_pool")
        ab_done, s_ready = sem("ab_done"), sem("s_ready")
        g_made, g_hi, g_ready = sem("g_made"), sem("g_hi"), sem("g_ready")
        c_done, gc32_ready, gc_hi, gc_ready, sq_ready = (sem("c_done"), sem("gc32_ready"), sem("gc_hi"),
                                                        sem("gc_ready"), sem("sq_ready"))
        turn_done = [sem("turn_done0"), sem("turn_done1")]
        turn_act, turn_dve = sem("turn_act"), sem("turn_dve")
        row_out = [sem("row_out_act"), sem("row_out_dve")]
        c0_mm, c0_ready, ce_mm, ce_taken = sem("c0_mm"), sem("c0_ready"), sem("ce_mm"), sem("ce_taken")
        rw_ready, rstd_ready = sem("rw_ready"), sem("rstd_ready")
        var_mm, var_ready, std_ready = sem("var_mm"), sem("var_ready"), sem("std_ready")
        u_done = [sem("u_done0"), sem("u_done1")]
        sum_done, u_taken, sum_pool = sem("sum_done"), sem("u_taken"), sem("sum_pool")
        x_const, out_done, scat_done = sem("x_const"), sem("out_done"), sem("scat_done")
        back_done, back_taken, router_mm, logit_ready = (sem("back_done"), sem("back_taken"),
                                                         sem("router_mm"), sem("logit_ready"))
        score_ready, diff_ready, mix_ready = sem("score_ready"), sem("diff_ready"), sem("mix_ready")
        hot2_ready, hot_turned, hot_taken, pick_mm = (sem("hot2_ready"), sem("hot_turned"), sem("hot_taken"),
                                                      sem("pick_mm"))
        gab_done, gs_ready, gg_made, gg_ready = sem("gab_done"), sem("gs_ready"), sem("gg_made"), sem("gg_ready")
        gcen_done, gcg32_ready, gcg_ready, gsq_ready = (sem("gcen_done"), sem("gcg32_ready"), sem("gcg_ready"),
                                                        sem("gsq_ready"))
        gvar_mm, gvar_ready, gstd_ready = sem("gvar_mm"), sem("gvar_ready"), sem("gstd_ready")
        gu_done, moe_ready, gstep = sem("gu_done"), sem("moe_ready"), sem("gstep")
        moe_step = [sem("moe_step0"), sem("moe_step1")]
        scratch = a["scratch"]

        PAIRS = ((0, 1), (1, 2), (3, 2), (5, 2), (7, 2))
        PARTS = ((0, 1), (1, 4), (5, 4))

        def summed(k):
            return atok[:, :, bass.ds(k * (FC // NT), FC // NT), :]

        def high(k):
            return X[:, 0:DB, bass.ds(k * FC, FC)].rearrange("p d (b t) -> p d b t", t=NT)

        def low(k):
            return X[:, DB:2 * DB, bass.ds(k * FC, FC)].rearrange("p d (b t) -> p d b t", t=NT)

        def steps_of(eng, step):
            for k in range(3):
                step(k, k % 2)
            with by_two(eng, 3, NQ - 1) as k:
                step(k, 1)
                step(k + 1, 0)
            step(NQ - 1, 1)

        def groups_of(eng, body):
            body(0)
            eng.wait_ge(rows_ready, 1)
            groups = eng.value_load(tab[0:1, NR * ROW + 2:NR * ROW + 3], min_val=1, max_val=MG)
            with eng.Fori(1, MG) as g:
                with eng.If(g < groups):
                    body(g)

        def stage2_loads(sp):
            sp.wait_ge(r_split, NPIECE)
            for dst, src in ((b3s, a["b3s"]), (b3e, a["b3e"]), (rwr, a["rw"]),
                             (rb, a["rb"].partition_broadcast(P)), (eb, a["eb"].partition_broadcast(P))):
                sp.dma_start(dst, src).then_inc(misc_in, 16)
            sp.wait_ge(summed_all, 1)
            sp.dma_start(w3r[:, 0, :], a["w3t"][:, 0:D]).then_inc(w3s_in, 16)
            rows = scratch.rearrange("(h s p) d -> p h s d", p=P, s=2)
            for k in range(NQ):
                for f, ready in enumerate((turn_act, turn_dve)):
                    sp.wait_ge(ready, k + 1)
                    sp.dma_start(rows[:, 2 * k + f, :, :],
                                 tev[:, f, :].rearrange("p (s d) -> p s d", s=2)).then_inc(row_out[f], 16)
                if k % 2 == 1:
                    for j in (k - 1, k):
                        sp.dma_start(xw[:, :, j * D:(j + 1) * D],
                                     a["xR"][j * FC:(j + 1) * FC, :].rearrange("(n p) d -> p n d", p=P)) \
                            .then_inc(x_rows_in[k // 2], 16)
                if k == 1:
                    sp.dma_start(w3r[:, 1:NJ, :],
                                 a["w3t"][:, D:NJ * D].rearrange("p (j d) -> p j d", d=D)).then_inc(w3_in, 16)
            out = a["out"].rearrange("(k f s p) d -> p k f s d", p=P, s=2, f=2)
            with sp.Fori(0, NQ) as k:
                for f, done in enumerate((sum_done, sum_pool)):
                    sp.wait_ge(done, k + 1)
                    sp.dma_start(out[:, bass.ds(k, 1), f, :, :].rearrange("p o s d -> p (o s) d"),
                                 xw[:, 2 * f:2 * f + 2, bass.ds(k * D, D)]).then_inc(out_done, 16)
            sp.wait_ge(out_done, 16 * NH)

        def stage2_act(act):
            act.wait_ge(summed_all, 1)

            def c_high(k):
                nc.scalar.activation(high(k), summed(k), ACT.Copy).then_inc(c_hi, 1)

            def centred(k, parity):
                act.wait_ge(c_done, k + 1)
                if not (isinstance(k, int) and k < 2):
                    act.wait_ge(gc_ready, k - 1)
                    act.wait_ge(sq_ready, k - 1)
                nc.scalar.activation(gc32[:, parity, :], psy[0], ACT.Copy).then_inc(gc32_ready, 1)

            def step(k, parity):
                if not (isinstance(k, int) and k in (0, NQ - 1)):
                    c_high(k + 1)
                act.wait_ge(ab_done, k * 2 + 1)
                if not (isinstance(k, int) and k < 2):
                    act.wait_ge(g_made, k - 1)
                nc.scalar.activation(s32[:, parity, :], ps1[2 * parity][:, :], ACT.Silu,
                                     bias=fb1[:, 0:1], scale=1.0 / WS).then_inc(s_ready, 1)
                act.wait_ge(turn_done[0], k + 1)
                if not (isinstance(k, int) and k < 1):
                    act.wait_ge(row_out[0], k * 16)
                nc.scalar.activation(tev[:, 0, :], turned[0], ACT.Copy).then_inc(turn_act, 1)
                if not (isinstance(k, int) and k < 1):
                    centred(k - 1, 1 - parity)

            c_high(0)
            c_high(1)
            steps_of(act, step)
            centred(NQ - 1, 1)
            act.wait_ge(var_ready, 1)
            nc.scalar.activation(rstd, rstd, ACT.Sqrt).then_inc(std_ready, 1)

            def main_take(k):
                act.wait_ge(u_done[1], k + 1)
                if k >= 2:
                    act.wait_ge(sum_pool, k - 1)
                for s in range(2):
                    i = nc.scalar.activation(ut[:, k % 2, s * D:(s + 1) * D],
                                             main_bank(k, 1)[:, s * D:(s + 1) * D], ACT.Copy,
                                             scale=rstd[:, k * MG + 2 + s:k * MG + 3 + s])
                i.then_inc(u_taken, 1)


            def group(g):
                first = isinstance(g, int)
                act.wait_ge(back_done, g + 1)
                nc.scalar.activation(cgT[:, :, :], turned[0][:, 0:4 * P].rearrange("p (n t) -> p n t", t=P),
                                     ACT.Copy).then_inc(back_taken, 1)
                if first:
                    act.wait_ge(rstd_ready, 1)
                    main_take(0)
                for n, (j0, m) in enumerate(PAIRS):
                    act.wait_ge(gab_done, g * 5 + (n + 1))
                    for j in range(j0, j0 + m):
                        i = nc.scalar.activation(sg[:, j * P:(j + 1) * P], product(0, j), ACT.Silu,
                                                 bias=fb1[:, j:j + 1], scale=1.0 / WS)
                    i.then_inc(gs_ready, 1)
                if first:
                    main_take(1)
                act.wait_ge(logit_ready, g + 1)
                nc.scalar.activation(rsg, rlg, ACT.Sigmoid).then_inc(score_ready, 1)
                if first:
                    main_take(2)
                act.wait_ge(diff_ready, g + 1)
                nc.scalar.activation(rm[:, 3:4], rm[:, 2:3], ACT.Sigmoid)
                nc.scalar.activation(rm[:, 4:5], rm[:, 2:3], ACT.Sigmoid, scale=-1.0).then_inc(mix_ready, 1)
                for n, (j0, m) in enumerate(PARTS):
                    act.wait_ge(gcen_done, g * 3 + (n + 1))
                    nc.scalar.activation(gcg32[:, j0 * P:(j0 + m) * P], centre_bank(n), ACT.Copy) \
                        .then_inc(gcg32_ready, 1)
                nc.scalar.activation(rm[:, 6:7], onesm[:, 0:1], ACT.Sqrt)
                if first:
                    for k in range(3, 5):
                        main_take(k)
                act.wait_ge(gvar_ready, g + 1)
                nc.scalar.activation(rstdg, rstdg, ACT.Sqrt).then_inc(gstd_ready, 1)
                if first:
                    for k in range(5, NQ):
                        main_take(k)

            groups_of(act, group)

        def product(which, j):
            if j == 0:
                return pst[:, (2 + which) * P:(3 + which) * P]
            pair = (j - 1) // 2
            c = ((j - 1) % 2 + pair // 2 * 2) * P
            return (ps1[2 + which][:, c:c + P], psy[which][:, c:c + P])[pair % 2]

        def main_bank(k, f):
            return (ps1[3][:, :], psy[1])[f] if k in (4, 6) else ps1[f][:, :]

        def centre_bank(n):
            return (psg[:, 3 * P:4 * P], ps1[2][:, :], psy[0])[n]

        def last_bank(j):
            if j == 0:
                return pst[:, 0:D]
            return (ps1[3][:, :], psy[1], ps1[2][:, :], psy[0])[(j - 1) // 2][:, (j - 1) % 2 * D:((j - 1) % 2 + 1) * D]

        def stage2_pe(pe):
            pe.wait_ge(summed_all, 1)
            pe.wait_ge(const2_ready, 1)

            def variance(k, parity):
                pe.wait_ge(sq_ready, k + 1)
                for g in range(MG):
                    mm = pe.matmul(psg[:, bass.ds(k * MG + g, 1)], sq[:, parity, g * P:(g + 1) * P],
                                   onesm[:, 0:1], start=True, stop=True)
                mm.then_inc(var_mm, 1)

            def centre(k, parity):
                pe.wait_ge(g_ready, k + 1)
                if not (isinstance(k, int) and k < 1):
                    pe.wait_ge(gc32_ready, k)
                for part in range(2):
                    mm = pe.matmul(psy[0], Cm, ghl[:, parity, part, :], start=(part == 0), stop=(part == 1))
                mm.then_inc(c_done, 1)

            def step(k, parity):
                first = isinstance(k, int) and k < 2
                pe.wait_ge(c_hi, k + 1)
                if not first:
                    pe.wait_ge(g_made, k - 1)
                for xp in range(2):
                    if xp == 1:
                        if first:
                            pe.wait_ge(c_lo, k + 1)
                        else:
                            pe.wait_ge(c_lo_pool, k - 1)
                    for which in range(2):
                        for wp in range(2 - xp):
                            for db in range(DB):
                                mm = pe.matmul(ps1[2 * parity + which][:, :], fw(0, wp, which, db),
                                               X[:, 2 * xp + db, bass.ds(k * FC, FC)],
                                               start=(xp + wp + db == 0), stop=(xp == 1 and db == DB - 1))
                        if xp == 1:
                            mm.then_inc(ab_done, 1)
                for f, taken in enumerate((turn_act, turn_dve)):
                    if not (isinstance(k, int) and k < 1):
                        pe.wait_ge(taken, k)
                    for s in range(2):
                        for n in range(2 * DB):
                            mm = pe.transpose(turned[f][:, (4 * s + n) * P:(4 * s + n + 1) * P],
                                              X[:, n, bass.ds(k * FC + (2 * f + s) * P, P)], id16)
                    mm.then_inc(turn_done[f], 1)
                if not (isinstance(k, int) and k < 1):
                    centre(k - 1, 1 - parity)
                if isinstance(k, int) and k == 2:
                    pe.wait_ge(c0_ready, 1)
                if not (isinstance(k, int) and k < 2):
                    variance(k - 2, parity)
                if isinstance(k, int) and k == 1:
                    pe.wait_ge(w3s_in, 16)
                    pe.wait_ge(misc_in, 5 * 16)
                    pe.matmul(psg[:, P:P + D], betrep, w3r[:, 0, :], start=True, stop=False)
                    pe.matmul(psg[:, P:P + D], onesm[0:1, :], b3s, start=False, stop=True).then_inc(c0_mm, 1)

            steps_of(pe, step)
            pe.wait_ge(w3_in, 16)
            pe.wait_ge(turn_dve, NQ)
            for e in range(FE):
                if e == 2:
                    centre(NQ - 1, 1)
                    variance(NQ - 2, 0)
                if e == 4:
                    variance(NQ - 1, 1)
                pe.matmul(psy[1][0:FE, 0:D], betm[:, e, :], w3r[:, 1 + e, :], start=(e == 0), stop=False)
            pe.matmul(psy[1][0:FE, 0:D], ident[0:FE, 0:FE], b3e, start=False, stop=True).then_inc(ce_mm, 1)

            def main_last(k):
                for f, taken in enumerate((sum_done, u_taken)):
                    if k not in (0, 4):
                        pe.wait_ge(taken, k if k < 4 else k - 1)
                    for s in range(2):
                        for n, (gp, vp) in enumerate(((0, 0), (0, 1), (1, 0))):
                            mm = pe.matmul(main_bank(k, f)[:, s * D:(s + 1) * D],
                                           gcs[:, k, gp, (2 * f + s) * P:(2 * f + s + 1) * P],
                                           V[:, 0, vp, :], start=(n == 0), stop=(n == 2))
                    mm.then_inc(u_done[f], 1)

            pe.wait_ge(gc_ready, NQ)
            pe.wait_ge(g_made, NQ)
            main_last(0)

            def group(g):
                first = isinstance(g, int)
                pe.wait_ge(cg_in, g * 16 + 16)
                for n in range(2 * DB):
                    mm = pe.transpose(turned[0][:, n * P:(n + 1) * P], cg[:, n, :], id16)
                mm.then_inc(back_done, 1)
                pe.wait_ge(back_taken, g + 1)
                if first:
                    pe.wait_ge(var_ready, 1)
                    pe.wait_ge(rw_ready, 1)
                n = 0
                for xp, wp in ((0, 0), (0, 1), (1, 0)):
                    for db in range(DB):
                        mm = pe.matmul(psg[:, 48:57], cgT[:, 2 * xp + db, :], rws[:, wp, db, 0:9],
                                       start=(n == 0), stop=(n == 5))
                        n += 1
                mm.then_inc(router_mm, 1)
                for pair, (j0, m) in enumerate(PAIRS):
                    if pair == 2 and first:
                        pe.wait_ge(ce_taken, 1)
                    if pair >= 3:
                        pe.wait_ge(gg_made, g * 5 + (pair - 1))
                    for j in range(j0, j0 + m):
                        for which in range(2):
                            n = 0
                            for wp, xp in ((0, 0), (0, 1), (1, 0)):
                                for db in range(DB):
                                    mm = pe.matmul(product(which, j), fw(j, wp, which, db), cgT[:, 2 * xp + db, :],
                                                   start=(n == 0), stop=(n == 5))
                                    n += 1
                    mm.then_inc(gab_done, 1)
                if first:
                    main_last(1)
                    main_last(2)
                pe.wait_ge(hot2_ready, g + 1)
                pe.wait_ge(gg_made, g * 5 + 1)
                pe.transpose(pst[0:FE, 0:P], roh, ident[:, :]).then_inc(hot_turned, 1)
                for n, (j0, m) in enumerate(PARTS):
                    pe.wait_ge(gg_ready, g * 5 + (2 * n + 1))
                    for part in range(2):
                        mm = pe.matmul(centre_bank(n), Cm, ggp[:, part, j0 * P:(j0 + m) * P],
                                       start=(part == 0), stop=(part == 1))
                    mm.then_inc(gcen_done, 1)
                if first:
                    main_last(3)
                    main_last(4)
                pe.wait_ge(gsq_ready, g + 1)
                for j in range(NJ):
                    mm = pe.matmul(psg[:, 32 + j:33 + j], sqg[:, j * P:(j + 1) * P], onesm[:, 0:1],
                                   start=True, stop=True)
                mm.then_inc(gvar_mm, 1)
                if first:
                    for k in range(5, NQ):
                        main_last(k)
                    pe.wait_ge(sum_done, NQ - 1)
                    pe.wait_ge(u_taken, NQ - 1)
                pe.wait_ge(hot_taken, g + 1)
                pe.matmul(pst[:, D:2 * D], ohT, ce8, start=True, stop=True).then_inc(pick_mm, 1)
                pe.wait_ge(gcg_ready, g + 1)
                for j in range(NJ):
                    for n, (gp, vp) in enumerate(((0, 0), (0, 1), (1, 0))):
                        mm = pe.matmul(last_bank(j), gcg[:, gp, j * P:(j + 1) * P], V[:, j, vp, :],
                                       start=(n == 0), stop=(n == 2))
                    if j % 2 == 0:
                        mm.then_inc(gu_done, 1)

            groups_of(pe, group)

        def stage2_dve(dve, link):
            dve.wait_ge(y_free, chunk_count(dve))
            nc.vector.memset(f4[0:1, 12, :], 0.0).then_inc(summed_all, 1)

            def c_low(k):
                dve.wait_ge(c_hi, k + 1)
                nc.vector.tensor_tensor(low(k), summed(k), high(k), ALU.subtract).then_inc(c_lo, 1)

            def keep(k, parity):
                dve.wait_ge(gc32_ready, k + 1)
                out = [gcs[:, bass.ds(k, 1), part, :].rearrange("p o t -> p (o t)") for part in range(2)]
                nc.vector.tensor_copy(out[0], gc32[:, parity, :]).then_inc(gc_hi, 1)
                if not (isinstance(k, int) and k < 2):
                    dve.wait_ge(var_mm, k - 1)
                nc.vector.tensor_tensor(sq[:, parity, :], gc32[:, parity, :], gc32[:, parity, :],
                                        ALU.mult).then_inc(sq_ready, 1)
                dve.wait_ge(gc_hi, k + 1)
                nc.vector.tensor_tensor(out[1], gc32[:, parity, :], out[0], ALU.subtract).then_inc(gc_ready, 1)

            def step(k, parity):
                dve.wait_ge(s_ready, k + 1)
                dve.wait_ge(ab_done, k * 2 + 2)
                nc.vector.scalar_tensor_tensor(g32[:, parity, :], ps1[2 * parity + 1][:, :], fb2s[:, 0:1],
                                               s32[:, parity, :], ALU.add, ALU.mult).then_inc(g_made, 1)
                dve.wait_ge(g_made, k + 1)
                if not (isinstance(k, int) and k < 2):
                    dve.wait_ge(c_done, k - 1)
                nc.vector.tensor_scalar(ghl[:, parity, 0, :], g32[:, parity, :], 1.0 / WS, None,
                                        ALU.mult).then_inc(g_hi, 1)
                dve.wait_ge(g_hi, k + 1)
                nc.vector.scalar_tensor_tensor(ghl[:, parity, 1, :], g32[:, parity, :], 1.0 / WS,
                                               ghl[:, parity, 0, :], ALU.mult, ALU.subtract).then_inc(g_ready, 1)
                dve.wait_ge(turn_done[1], k + 1)
                if not (isinstance(k, int) and k < 1):
                    dve.wait_ge(row_out[1], k * 16)
                nc.vector.tensor_copy(tev[:, 1, :], turned[1]).then_inc(turn_dve, 1)
                if not (isinstance(k, int) and k < 1):
                    keep(k - 1, 1 - parity)
                if isinstance(k, int) and k == 1:
                    dve.wait_ge(c0_mm, 1)
                    nc.vector.tensor_copy(c0b, psg[:, P:P + D]).then_inc(c0_ready, 1)

            link(nc.vector.tensor_scalar(fb2s, fb2[:, :], WS, None, ALU.mult))
            c_low(0)
            c_low(1)
            steps_of(dve, step)
            keep(NQ - 1, 1)
            dve.wait_ge(misc_in, 5 * 16)
            link(nc.vector.tensor_scalar(rws[:, 0, :, 0:9], rwr, WS, None, ALU.mult))
            nc.vector.scalar_tensor_tensor(rws[:, 1, :, 0:9], rwr, WS, rws[:, 0, :, 0:9],
                                           ALU.mult, ALU.subtract).then_inc(rw_ready, 1)
            dve.wait_ge(var_mm, NQ)
            nc.vector.tensor_scalar(rstd, psg[:, 0:NQ * MG], 1.0 / FH, EPS, ALU.mult, ALU.add).then_inc(var_ready, 1)
            dve.wait_ge(std_ready, 1)
            link(nc.vector.reciprocal(rstd, rstd))
            nc.vector.tensor_scalar(rstd, rstd, 1.0 / WS, None, ALU.mult).then_inc(rstd_ready, 1)
            dve.wait_ge(rstd_ready, 1)

            def main_sum(k):
                dve.wait_ge(x_const, k + 1)
                dve.wait_ge(u_done[0], k + 1)
                for s in range(2):
                    row = xw[:, s, k * D:(k + 1) * D]
                    i = nc.vector.scalar_tensor_tensor(row, main_bank(k, 0)[:, s * D:(s + 1) * D],
                                                       rstd[:, k * MG + s:k * MG + s + 1], row, ALU.mult, ALU.add)
                i.then_inc(sum_done, 1)

            main_sum(0)
            dve.wait_ge(ce_mm, 1)
            nc.vector.tensor_copy(ce8, psy[1][0:FE, 0:D]).then_inc(ce_taken, 1)
            nsteps = [0]

            def group(g):
                first = isinstance(g, int)
                count = [0]

                def glink(i):
                    count[0] += 1
                    i.then_inc(gstep, 1)
                    dve.wait_ge(gstep, g * nsteps[0] + count[0])

                dve.wait_ge(router_mm, g + 1)
                nc.vector.scalar_tensor_tensor(rlg, psg[:, 48:57], 1.0 / WS, rb, ALU.mult,
                                               ALU.add).then_inc(logit_ready, 1)
                for n, (j0, m) in enumerate(PAIRS):
                    dve.wait_ge(gs_ready, g * 5 + (n + 1))
                    cols = slice(j0 * P, (j0 + m) * P)
                    for j in range(j0, j0 + m):
                        i = nc.vector.scalar_tensor_tensor(gg[:, j * P:(j + 1) * P], product(1, j), fb2s[:, j:j + 1],
                                                           sg[:, j * P:(j + 1) * P], ALU.add, ALU.mult)
                    i.then_inc(gg_made, 1)
                    dve.wait_ge(gg_made, g * 5 + (n + 1))
                    glink(nc.vector.tensor_scalar(ggp[:, 0, cols], gg[:, cols], 1.0 / WS, None, ALU.mult))
                    nc.vector.scalar_tensor_tensor(ggp[:, 1, cols], gg[:, cols], 1.0 / WS, ggp[:, 0, cols],
                                                   ALU.mult, ALU.subtract).then_inc(gg_ready, 1)
                if first:
                    main_sum(1)
                dve.wait_ge(score_ready, g + 1)
                glink(nc.vector.tensor_tensor(rsel, rsg[:, 1:9], eb, ALU.add))
                glink(nc.vector.tensor_reduce(rm[:, 0:1], rsel, AX.X, ALU.max))
                glink(nc.vector.scalar_tensor_tensor(rcand, rsel, rm[:, 0:1], io8, ALU.is_equal, ALU.mult))
                glink(nc.vector.tensor_reduce(rm[:, 1:2], rcand, AX.X, ALU.min))
                nc.vector.tensor_scalar(roh, io8, rm[:, 1:2], None, ALU.is_equal).then_inc(hot2_ready, 1)
                dve.wait_ge(hot2_ready, g + 1)
                glink(nc.vector.tensor_tensor(rcand, roh, rsg[:, 1:9], ALU.mult))
                glink(nc.vector.tensor_reduce(rm[:, 5:6], rcand, AX.X, ALU.add))
                nc.vector.tensor_tensor(rm[:, 2:3], rsg[:, 0:1], rm[:, 5:6], ALU.subtract).then_inc(diff_ready, 1)
                dve.wait_ge(hot_turned, g + 1)
                nc.vector.tensor_copy(ohT, pst[0:FE, 0:P]).then_inc(hot_taken, 1)
                if first:
                    main_sum(2)
                dve.wait_ge(gcg32_ready, g * 3 + 3)
                glink(nc.vector.tensor_copy(gcg[:, 0, :], gcg32))
                nc.vector.tensor_tensor(gcg[:, 1, :], gcg32, gcg[:, 0, :], ALU.subtract).then_inc(gcg_ready, 1)
                if first:
                    main_sum(3)
                    main_sum(4)
                dve.wait_ge(gvar_mm, g + 1)
                nc.vector.tensor_scalar(rstdg, psg[:, 32:32 + NJ], 1.0 / FH, EPS, ALU.mult,
                                        ALU.add).then_inc(gvar_ready, 1)
                dve.wait_ge(mix_ready, g + 1)
                if first:
                    main_sum(5)
                glink(nc.vector.tensor_scalar(rse, roh, rm[:, 4:5], 1.0 / WS, ALU.mult, ALU.mult))
                dve.wait_ge(gstd_ready, g + 1)
                glink(nc.vector.reciprocal(rstdg, rstdg))
                glink(nc.vector.tensor_tensor(rse, rse, rstdg[:, 1:NJ], ALU.mult))
                glink(nc.vector.tensor_scalar(rstdg[:, 0:1], rstdg[:, 0:1], 1.0 / WS, None, ALU.mult))
                if first:
                    main_sum(6)
                    main_sum(7)
                dve.wait_ge(gu_done, g * 5 + 1)
                glink(nc.vector.scalar_tensor_tensor(moe, last_bank(0), rstdg[:, 0:1], c0b, ALU.mult, ALU.add))
                dve.wait_ge(xg_in, g * 16 + 16)
                glink(nc.vector.scalar_tensor_tensor(moe, moe, rm[:, 3:4], xg, ALU.mult, ALU.add))
                dve.wait_ge(gu_done, g * 5 + 2)
                nc.vector.scalar_tensor_tensor(moe, last_bank(1), rse[:, 0:1], moe, ALU.mult,
                                               ALU.add).then_inc(moe_step[0], 1)
                dve.wait_ge(pick_mm, g + 1)
                nc.vector.tensor_scalar(moe2, pst[:, D:2 * D], rm[:, 4:5], None, ALU.mult).then_inc(moe_step[1], 1)
                for j in range(2, NJ):
                    if j % 2 == 1:
                        dve.wait_ge(gu_done, g * 5 + (2 + j // 2))
                    dve.wait_ge(moe_step[j % 2], g * 5 + j // 2 if j % 2 == 0 else g * 4 + j // 2)
                    part = (moe, moe2)[j % 2]
                    nc.vector.scalar_tensor_tensor(part, last_bank(j), rse[:, j - 1:j], part, ALU.mult,
                                                   ALU.add).then_inc(moe_step[j % 2], 1)
                dve.wait_ge(moe_step[0], g * 5 + 5)
                dve.wait_ge(moe_step[1], g * 4 + 4)
                nc.vector.tensor_tensor(moe, moe, moe2, ALU.add).then_inc(moe_ready, 1)
                nsteps[0] = count[0]

            groups_of(dve, group)

        def stage2_pool(pool, link):
            link(nc.gpsimd.tensor_scalar(Cm, ident[:, :], -1.0 / FH, None, ALU.add))
            link(nc.gpsimd.tensor_scalar(betrep, onesm[:, :], bet[:, 0:1], None, ALU.mult))
            link(nc.gpsimd.memset(betm[:, :, :], 0.0))
            for e in range(FE):
                link(nc.gpsimd.tensor_copy(betm[:, e, e:e + 1], bet[:, 1:2]))
            link(nc.gpsimd.iota(io8, pattern=[[1, FE]], base=-FE, channel_multiplier=0,
                                allow_small_or_imprecise_dtypes=True))
            nc.gpsimd.tensor_copy(id16, ident[:, :]).then_inc(const2_ready, 1)
            pool.wait_ge(rows_ready, 1)
            pool.wait_ge(summed_all, 1)

            def gather(g):
                nc.gpsimd.indirect_dma_start(
                    out=cg[:, :, :].rearrange("p n d -> p (n d)"), out_offset=None, in_=scratch,
                    in_offset=bass.IndirectOffsetOnAxis(ap=gid[:, g:g + 1], axis=0)).then_inc(cg_in, 16)
                nc.gpsimd.indirect_dma_start(
                    out=xg, out_offset=None, in_=a["xR"],
                    in_offset=bass.IndirectOffsetOnAxis(ap=gid[:, g:g + 1], axis=0)).then_inc(xg_in, 16)

            def squares(g):
                pool.wait_ge(gcg32_ready, g * 3 + 3)
                nc.gpsimd.tensor_tensor(sqg, gcg32, gcg32, ALU.mult).then_inc(gsq_ready, 1)

            def scatter(g):
                pool.wait_ge(moe_ready, g + 1)
                nc.gpsimd.indirect_dma_start(
                    out=a["out"], out_offset=bass.IndirectOffsetOnAxis(ap=sid[:, g:g + 1], axis=0),
                    in_=moe, in_offset=None, bounds_check=TOK - 1, oob_is_err=False).then_inc(scat_done, 16)
                pool.wait_ge(scat_done, 16 * (g + 1))

            def c_low(k):
                pool.wait_ge(c_hi, k + 1)
                nc.gpsimd.tensor_tensor(low(k), summed(k), high(k), ALU.subtract).then_inc(c_lo_pool, 1)

            def add_const(k):
                if k % 2 == 0:
                    pool.wait_ge(x_rows_in[k // 2], 32)
                rows = xw[:, :, k * D:(k + 1) * D]
                nc.gpsimd.tensor_tensor(rows, rows, c0b.unsqueeze(1).to_broadcast([P, MG, D]),
                                        ALU.add).then_inc(x_const, 1)

            for k in range(2, NQ):
                c_low(k)
                if k == 4:
                    pool.wait_ge(c0_ready, 1)
                if k >= 4:
                    add_const(k - 4)
            for f in range(2):
                pool.wait_ge(row_out[f], 16 * NQ)
            gather(0)
            for k in range(NQ - 4, NQ):
                add_const(k)

            def add_taken(k):
                pool.wait_ge(u_taken, k + 1)
                rows = xw[:, 2:4, k * D:(k + 1) * D]
                nc.gpsimd.tensor_tensor(rows, rows, ut[:, k % 2, :].rearrange("p (s d) -> p s d", s=2),
                                        ALU.add).then_inc(sum_pool, 1)

            for k in range(3):
                add_taken(k)
            squares(0)
            for k in range(3, NQ):
                add_taken(k)
            pool.wait_ge(out_done, 16 * NH)
            scatter(0)
            groups = pool.value_load(tab[0:1, NR * ROW + 2:NR * ROW + 3], min_val=1, max_val=MG)
            for g in range(1, MG):
                with pool.If(groups > g):
                    gather(g)
                    squares(g)
                    scatter(g)

        @block.sync
        def _(sp):
            for n, (dram, place, *_) in enumerate(opening):
                sp.dma_start(place, dram).then_inc(start_in[n], 16)
                if n == 1:
                    for dst, src in ((b1[:, :], a["b1"]), (b2[:, :], a["b2"])):
                        sp.dma_start(dst, src).then_inc(first_in, 16)
            for q in range(1, 8):
                sp.dma_start(x32[:, :, q * 512:(q + 1) * 512],
                             a["xT"][:, :, q * 512:(q + 1) * 512]).then_inc(x_in[q], 16)
            for dst, src in ((gw[:, :, :], a["gate_w"].rearrange("(k p) e -> p k e", p=P)),
                             (tw[:, :, :], a["time_w"].rearrange("(k p) e -> p k e", p=P)),
                             (gb[:, :], a["gate_b"].partition_broadcast(NB)),
                             (tb[:, :], a["time_b"].partition_broadcast(NB)),
                             (fb1[:, :], a["fb1"]), (fb2[:, :], a["fb2"]), (gam[:, :], a["gam"]), (bet[:, :], a["bet"])):
                sp.dma_start(dst, src).then_inc(small_in, 16)
            sp.dma_start(cond[:, :, :], a["condT"]).then_inc(cond_in, 16)
            sp.dma_start(kint[:, 0, :], a["index_b4"]).then_inc(idx_in, 16)
            sp.dma_start(kint[:, 1, :], a["index_t4"]).then_inc(idx_in, 16)
            for n in range(NPIECE):
                if n >= 2:
                    sp.wait_ge(r_split, n - 1)
                src = piece_src(n)
                dst = stage[:, n % 2, 0:piece_size(n)]
                if len(src.shape) == 3:
                    dst = dst.rearrange("p (h d) -> p h d", d=D)
                sp.dma_start(dst, src).then_inc(wr_in[n % 2], 16)
            stage2_loads(sp)

        @block.scalar
        def _(act):
            def open_high(start, end):
                for n in range(start, end):
                    src, hi, lo, scale = opening[n][2:]
                    act.wait_ge(start_in[n], 16)
                    nc.scalar.activation(hi, src, ACT.Copy, scale=scale).then_inc(start_hi, 1)

            open_high(0, 6)
            act.wait_ge(first_in, 2 * 16)

            def gelus(g, e, size=CH):
                first = isinstance(g, int) and g == 0
                for j in range(4):
                    act.wait_ge(l1_done, g * 4 + (j + 1))
                    if not first:
                        act.wait_ge(h_ready, g * 4 + (j - 3))
                    for k in range(2):
                        hb = 2 * j + k
                        i = nc.scalar.activation(
                            h32[:, j, k * size:(k + 1) * size], ps1[j][:, k * size:(k + 1) * size],
                            ACT.Gelu_apprx_tanh, bias=b1[:, bass.ds(e * HB + hb, 1)], scale=1.0 / WS)
                    i.then_inc(h32_ready, 1)

            def store(g, parity):
                act.wait_ge(y_done, g + 1)
                for db in range(DB):
                    i = nc.scalar.activation(
                        atok[:, db, bass.ds(g * CB, CB), :],
                        psy[parity][:, db * CH:(db + 1) * CH].rearrange("p (b t) -> p b t", t=NT),
                        ACT.Identity, bias=b2[:, SH * DB + db:SH * DB + db + 1], scale=1.0 / WS)
                i.then_inc(y_taken, 1)

            def high_piece(e, k):
                act.wait_ge(wr_in[k % 2], e * 32 + 16 * (k // 2 + 1))
                at = k * 1024 + (2048 if k >= 2 else 0)
                nc.scalar.activation(W[:, bass.ds(e * WE + at, 1024)], stage[:, k % 2, :], ACT.Copy,
                                     scale=WS).then_inc(hi_ready, 1)

            def high_rest(n):
                act.wait_ge(wr_in[n % 2], 16 * (n // 2 + 1))
                parts = rest_parts(n)
                for c, (src, hi, lo, gain) in enumerate(parts):
                    scale = WS if gain is None else gams[:, gain:gain + 1]
                    i = nc.scalar.activation(hi, src, ACT.Copy, scale=scale)
                i.then_inc(hi_ready, 1)

            gelus(0, SH)
            open_high(6, 8)
            gelus(1, SH)
            store(0, 0)
            gelus(2, SH)
            store(1, 1)
            act.wait_ge(cond_in, 16)
            nc.scalar.activation(silc[:, :, :], cond[:, :, :], ACT.Exp, scale=-1.0).then_inc(cond_exp, 1)
            def weigh(e):
                for u in range(2):
                    gelus(e * 2 + (3 + u), SH)
                    high_piece(e, 2 * u)
                    store(e * 2 + (2 + u), u)
                    high_piece(e, 2 * u + 1)

            weigh(0)
            act.wait_ge(w_split, 8)
            weigh(1)
            act.wait_ge(sums_done, 8)
            act.wait_ge(x_split, 7)
            with act.Fori(2, E) as e:
                weigh(e)
            act.wait_ge(gate_log, 1)
            nc.scalar.activation(G[:, 4, :], G[:, 2, :], ACT.Exp, bias=G[:, 3, 0:1]).then_inc(gate_exp, 1)
            act.wait_ge(gain_ready, 1)
            for g in range(10, NS - 1):
                gelus(g + 1, SH)
                store(g, g % 2)

            def expert_of(eng, r):
                return eng.value_load(tab[0:1, bass.ds(r * ROW + SLOTS, 1)], min_val=0, max_val=E - 1)

            def bias(r, parity):
                e = expert_of(act, r)
                act.wait_ge(y_done, r + (R0 + 1))
                if not (isinstance(r, int) and r < 2):
                    act.wait_ge(y_free, r - 1)
                for db in range(DB):
                    i = nc.scalar.activation(
                        ytmp[:, bass.ds(parity, 1), db, 0:RC].rearrange("p o c -> p (o c)"),
                        psy2[:, bass.ds(parity, 1), db * RC:(db + 1) * RC].rearrange("p o c -> p (o c)"),
                        ACT.Identity, bias=b2[:, bass.ds(e * DB + db, 1)], scale=1.0 / WS)
                i.then_inc(y_taken, 1)

            act.wait_ge(tab_ready, 1)
            gelus(R0, expert_of(act, 0), RC)
            store(NS - 1, 1)

            def step(r, parity):
                gelus(r + R0, expert_of(act, r), RC)
                bias(r - 1, 1 - parity)

            step(1, 1)
            for n in range(8):
                high_rest(4 * E + n)
                step(2 + n, n % 2)
            last, parity = expert_loops(act, 10, step)
            bias(last, parity)
            stage2_act(act)

        @block.tensor
        def _(pe):
            def hidden(g, e, rhs, size=CH):
                first = isinstance(g, int) and g == 0
                for j in range(4):
                    if not first:
                        pe.wait_ge(h32_ready, g * 4 + (j - 3))
                    else:
                        pe.wait_ge(w_split, j + 2)
                    for k in range(2):
                        hb = 2 * j + k
                        out = ps1[j][:, k * size:(k + 1) * size]
                        n = 0
                        for wp, xp in ((0, 0), (0, 1), (1, 0)):
                            for db in range(DB):
                                mm = pe.matmul(out, w1(e, wp, db, hb), rhs(xp, db),
                                               start=(n == 0), stop=(n == 5))
                                n += 1
                    mm.then_inc(l1_done, 1)

            def hidden_shared(g):
                if isinstance(g, int) and g % 2 == 0 and g >= 2:
                    pe.wait_ge(x_split, g // 2)
                hidden(g, SH, lambda xp, db: xtok[:, 2 * xp + db, bass.ds(g * CB, CB), :])

            def expert_of(r):
                return pe.value_load(tab[0:1, bass.ds(r * ROW + SLOTS, 1)], min_val=0, max_val=E - 1)

            def hidden_expert(r, parity):
                pe.wait_ge(x_staged, r + 1)
                hidden(r + R0, expert_of(r), lambda xp, db: xs[:, parity, 2 * xp + db, 0:RC], RC)

            def output(g, e, parity, size=CH):
                if not (isinstance(g, int) and g < 2):
                    pe.wait_ge(y_taken, g - 1)
                pe.wait_ge(h_ready, g * 4 + 4)
                for db in range(DB):
                    out = psy2[:, bass.ds(parity, 1), db * size:(db + 1) * size].rearrange("p o c -> p (o c)")
                    n = 0
                    for hb in range(HB):
                        for wp, hp in ((0, 0), (0, 1), (1, 0)):
                            h = hbuf[:, bass.ds(parity, 1), hp, hb, 0:size].rearrange("p o c -> p (o c)")
                            mm = pe.matmul(out, w2(e, wp, hb, db), h, start=(n == 0), stop=(n == 3 * HB - 1))
                            n += 1
                mm.then_inc(y_done, 1)

            hidden_shared(0)
            pe.wait_ge(w_split, 6)
            hidden_shared(1)
            pe.wait_ge(w_split, 8)
            output(0, SH, 0)
            hidden_shared(2)
            output(1, SH, 1)
            with pe.Fori(1, 5) as q:
                hidden_shared(q * 2 + 1)
                output(q * 2, SH, 0)
                pe.wait_ge(x_split, q + 1)
                hidden_shared(q * 2 + 2)
                output(q * 2 + 1, SH, 1)
            pe.wait_ge(small_in, 8 * 16)
            pe.wait_ge(gate_in, 1)
            for k in range(3 * DB):
                pe.matmul(psg[0:NB, 0:E], gin[:, k, :], gw[:, k, :], start=(k == 0), stop=(k == 3 * DB - 1))
            for k in range(DB):
                mm = pe.matmul(psg[0:NB, 8:8 + 2 * E], silc[:, k, :], tw[:, k, :], start=(k == 0), stop=(k == DB - 1))
            mm.then_inc(gate_mm, 1)
            hidden_shared(11)
            output(10, SH, 0)
            pe.wait_ge(sel_ready, 1)
            pe.matmul(psg[0:NB, 0:E], tri[0:NB, 0:NB], G[:, 9, :], start=True, stop=True)
            pe.matmul(psg[0:NB, 8:8 + E], onesm[0:NB, 0:NB], G[:, 9, :], start=True, stop=True).then_inc(rank_mm, 1)
            hidden_shared(12)
            output(11, SH, 1)
            for e in range(E):
                pe.wait_ge(hot_ready, e + 1)
                for part in range(2):
                    pe.matmul(psg[0:1, 0:NSLOT], lhs[:, e % 2, part, 0:1], hot[:, e % 2, :],
                              start=(e == 0 and part == 0), stop=(e == E - 1 and part == 1))
                for part in range(2):
                    mm = pe.matmul(pst[:, 0:NSLOT], lhs[:, e % 2, part, 1:1 + P], hot[:, e % 2, :],
                                   start=(e == 0 and part == 0), stop=(e == E - 1 and part == 1))
                mm.then_inc(tab_mm, 1)
            hidden_shared(13)
            output(12, SH, 0)
            pe.wait_ge(key_ready, 1)
            for g in range(MG):
                mm = pe.matmul(pst[:, g * P:(g + 1) * P], onesm[:, :], kdiag[:, g, :], start=True, stop=True)
            mm.then_inc(key_mm, 1)
            hidden_shared(14)
            output(13, SH, 1)
            pe.wait_ge(valid_ready, 1)
            pe.matmul(psg[:, 0:MG], tri[:, :], f4[:, 3, :], start=True, stop=True)
            pe.matmul(psg[:, 8:8 + MG], onesm[:, :], f4[:, 3, :], start=True, stop=True).then_inc(place_mm, 1)
            hidden_shared(15)
            output(14, SH, 0)
            pe.wait_ge(place_ready, 1)
            for j in range(MG):
                for g in range(MG):
                    mm = pe.matmul(psg[:, 16 + 2 * j:18 + 2 * j], oh16[:, g, j * P:(j + 1) * P], vals[:, g, :],
                                   start=(g == 0), stop=(g == MG - 1))
            mm.then_inc(pack_mm, 1)
            pe.wait_ge(r_split, 4 * E)
            hidden_expert(0, 0)
            output(NS - 1, SH, 1)

            def step(r, parity):
                hidden_expert(r, parity)
                output(r + (R0 - 1), expert_of(r - 1), 1 - parity, RC)

            step(1, 1)
            last, parity = expert_loops(pe, 2, step)
            output(last + R0, expert_of(last), parity, RC)
            stage2_pe(pe)

        @block.vector
        def _(dve):
            steps = [0]

            def link(i):
                steps[0] += 1
                i.then_inc(dv, 1)
                dve.wait_ge(dv, steps[0])

            def open_low(start, end):
                for n in range(start, end):
                    src, hi, lo, scale = opening[n][2:]
                    dve.wait_ge(start_hi, n + 1)
                    if scale == 1.0:
                        i = nc.vector.tensor_tensor(lo, src, hi, ALU.subtract)
                    else:
                        i = nc.vector.scalar_tensor_tensor(lo, src, scale, hi, ALU.mult, ALU.subtract)
                    i.then_inc(w_split, 1)

            open_low(0, 6)

            def splits(g, parity, size=CH):
                if not (isinstance(g, int) and g < 2):
                    dve.wait_ge(y_done, g - 1)
                for j in range(4):
                    dve.wait_ge(h32_ready, g * 4 + (j + 1))
                    src = h32[:, j, 0:2 * size].rearrange("p (k t) -> p k t", k=2)
                    hi = hbuf[:, parity, 0, 2 * j:2 * j + 2, 0:size]
                    nc.vector.tensor_copy(hi, src).then_inc(h_hi, 1)
                    dve.wait_ge(h_hi, g * 4 + (j + 1))
                    nc.vector.tensor_tensor(hbuf[:, parity, 1, 2 * j:2 * j + 2, 0:size], src, hi,
                                            ALU.subtract).then_inc(h_ready, 1)

            def low_piece(e, k):
                dve.wait_ge(hi_ready, e * 4 + (k + 1))
                at = k * 1024 + (2048 if k >= 2 else 0)
                nc.vector.scalar_tensor_tensor(W[:, bass.ds(e * WE + (at + 2048), 1024)], stage[:, k % 2, :], WS,
                                               W[:, bass.ds(e * WE + at, 1024)],
                                               ALU.mult, ALU.subtract).then_inc(r_split, 1)

            def low_rest(n):
                dve.wait_ge(hi_ready, n + 1)
                for src, hi, lo, gain in rest_parts(n):
                    scale = WS if gain is None else gams[:, gain:gain + 1]
                    i = nc.vector.scalar_tensor_tensor(lo, src, scale, hi, ALU.mult, ALU.subtract)
                i.then_inc(r_split, 1)

            def sums(q):
                if q > 0:
                    dve.wait_ge(x_in[q], 16)
                v = x32[:, :, q * 512:(q + 1) * 512].rearrange("p d (b t) -> p d b t", t=NT)
                for r, (lo, hi) in enumerate(((0, HEAD), (HEAD, HP), (HP, NT))):
                    i = nc.vector.tensor_reduce(gsum[:, :, r, q * 8:(q + 1) * 8], v[:, :, :, lo:hi],
                                                AX.X, ALU.add)
                i.then_inc(sums_done, 1)

            for g in range(4):
                splits(g, g % 2)
                if g == 0:
                    open_low(6, 8)
                sums(2 * g)
                sums(2 * g + 1)
                if g == 3:
                    dve.wait_ge(cond_exp, 1)
                    link(nc.vector.tensor_scalar(silc, silc, 1.0, None, ALU.add))
                    link(nc.vector.reciprocal(silc, silc))
                    link(nc.vector.tensor_tensor(silc, silc, cond, ALU.mult))
            low_piece(0, 0)
            low_piece(0, 1)
            splits(4, 0)
            low_piece(0, 2)
            low_piece(0, 3)
            dve.wait_ge(sums_done, 8)
            link(nc.vector.tensor_tensor(gin[:, DB:2 * DB, :], gsum[:, :, 0, :], gsum[:, :, 1, :], ALU.add))
            link(nc.vector.tensor_tensor(gin[:, 0:DB, :], gin[:, DB:2 * DB, :], gsum[:, :, 2, :], ALU.add))
            link(nc.vector.tensor_tensor(gin[:, 2 * DB:3 * DB, :], gsum[:, :, 2, :], gsum[:, :, 1, :], ALU.add))
            link(nc.vector.tensor_scalar(gin[:, 0:DB, :], gin[:, 0:DB, :], 1.0 / NT, None, ALU.mult))
            nc.vector.tensor_scalar(gin[:, DB:3 * DB, :], gin[:, DB:3 * DB, :], 1.0 / HP, None,
                                    ALU.mult).then_inc(gate_in, 1)
            with dve.Fori(1, E) as e:
                splits(e * 2 + 3, 1)
                low_piece(e, 0)
                low_piece(e, 1)
                splits(e * 2 + 4, 0)
                low_piece(e, 2)
                low_piece(e, 3)
            dve.wait_ge(const_ready, 1)
            dve.wait_ge(small_in, 8 * 16)
            dve.wait_ge(gate_mm, 1)
            link(nc.vector.tensor_tensor(G[:, 0, :], psg[0:NB, 0:E], gb[:, :], ALU.add))
            link(nc.vector.tensor_tensor(G[:, 1, :], psg[0:NB, 8:8 + E], tb[:, 0:E], ALU.add))
            link(nc.vector.tensor_tensor(G[:, 5, :], psg[0:NB, 8 + E:8 + 2 * E], tb[:, E:2 * E], ALU.add))
            link(nc.vector.scalar_tensor_tensor(G[:, 2, :], G[:, 1, :], 1.0, G[:, 0, :], ALU.add, ALU.mult))
            link(nc.vector.tensor_tensor(G[:, 2, :], G[:, 2, :], G[:, 5, :], ALU.add))
            link(nc.vector.tensor_reduce(G[:, 3, 1:2], G[:, 2, :], AX.X, ALU.max))
            nc.vector.tensor_scalar(G[:, 3, 0:1], G[:, 3, 1:2], -1.0, None, ALU.mult).then_inc(gate_log, 1)
            dve.wait_ge(gate_exp, 1)
            link(nc.vector.tensor_reduce(G[:, 3, 2:3], G[:, 4, :], AX.X, ALU.add))
            link(nc.vector.reciprocal(G[:, 3, 3:4], G[:, 3, 2:3]))
            link(nc.vector.tensor_scalar(G[:, 6, :], G[:, 4, :], G[:, 3, 3:4], None, ALU.mult))
            for n, (score, pick) in enumerate(((6, 7), (10, 8))):
                link(nc.vector.tensor_reduce(G[:, 11, n:n + 1], G[:, score, :], AX.X, ALU.max))
                link(nc.vector.scalar_tensor_tensor(G[:, 12, :], G[:, score, :], G[:, 11, n:n + 1], G[:, 20, :],
                                                    ALU.is_equal, ALU.mult))
                link(nc.vector.tensor_reduce(G[:, 13, n:n + 1], G[:, 12, :], AX.X, ALU.min))
                link(nc.vector.tensor_scalar(G[:, pick, :], G[:, 20, :], G[:, 13, n:n + 1], None, ALU.is_equal))
                if n == 0:
                    link(nc.vector.scalar_tensor_tensor(G[:, 10, :], G[:, 7, :], -2.0, G[:, 6, :],
                                                        ALU.mult, ALU.add))
            nc.vector.tensor_tensor(G[:, 9, :], G[:, 7, :], G[:, 8, :], ALU.add).then_inc(sel_ready, 1)
            dve.wait_ge(sel_ready, 1)
            link(nc.vector.tensor_tensor(G[:, 14, 0:1], G[:, 11, 0:1], G[:, 11, 1:2], ALU.add))
            link(nc.vector.tensor_scalar(G[:, 14, 0:1], G[:, 14, 0:1], 1e-8, None, ALU.add))
            link(nc.vector.reciprocal(G[:, 14, 1:2], G[:, 14, 0:1]))
            link(nc.vector.scalar_tensor_tensor(G[:, 15, :], G[:, 6, :], G[:, 14, 1:2], G[:, 9, :],
                                                ALU.mult, ALU.mult))
            splits(11, 1)
            dve.wait_ge(rank_mm, 1)
            link(nc.vector.tensor_copy(G[:, 16, :], psg[0:NB, 0:E]))
            link(nc.vector.tensor_tensor(G[:, 17, :], psg[0:NB, 8:8 + E], G[:, 24, :], ALU.mult))
            for e in range(E):
                link(nc.vector.tensor_scalar(gcnt[:, e, :], siota[:, 0:NCNT * SLOTS:SLOTS], G[:, 17, e:e + 1],
                                             None, ALU.is_lt))
            link(nc.vector.tensor_reduce(G[:, 18, :], gcnt[:, :, :], AX.X, ALU.add))
            for e in range(1, E):
                link(nc.vector.tensor_tensor(G[:, 19, e:e + 1], G[:, 19, e - 1:e], G[:, 18, e - 1:e], ALU.add))
            link(nc.vector.tensor_tensor(G[:, 22, :], G[:, 16, :], G[:, 24, :], ALU.mult))
            link(nc.vector.scalar_tensor_tensor(G[:, 22, :], G[:, 19, :], float(SLOTS), G[:, 22, :],
                                                ALU.mult, ALU.add))
            link(nc.vector.tensor_scalar(G[:, 23, :], G[:, 9, :], -1e4, 1e4, ALU.mult, ALU.add))
            link(nc.vector.tensor_tensor(G[:, 22, :], G[:, 22, :], G[:, 23, :], ALU.add))
            link(nc.vector.tensor_tensor(G[:, 23, :], G[:, 22, :], G[:, 24, :], ALU.add))
            link(nc.vector.scalar_tensor_tensor(G[:, 26, :], G[:, 22, :], -float(SEG), G[:, 25, :],
                                                ALU.mult, ALU.add))
            link(nc.vector.tensor_tensor(G[:, 26, :], G[:, 26, :], G[:, 9, :], ALU.mult))
            for e in range(E):
                if e >= 2:
                    dve.wait_ge(tab_mm, e - 1)
                link(nc.vector.tensor_scalar(hot[:, e % 2, :], siota, G[:, 22, e:e + 1], None, ALU.is_ge))
                link(nc.vector.scalar_tensor_tensor(hot[:, e % 2, :], siota, G[:, 23, e:e + 1], hot[:, e % 2, :],
                                                    ALU.is_lt, ALU.mult))
                link(nc.vector.tensor_copy(lval[:, 0:1], G[:, 26, e:e + 1]))
                link(nc.vector.tensor_copy(lval[:, 1:1 + P], G[:, 15, e:e + 1].to_broadcast([NB, P])))
                link(nc.vector.tensor_copy(lhs[:, e % 2, 0, 0:1 + P], lval[:, 0:1 + P]))
                nc.vector.tensor_tensor(lhs[:, e % 2, 1, 0:1 + P], lval[:, 0:1 + P], lhs[:, e % 2, 0, 0:1 + P],
                                        ALU.subtract).then_inc(hot_ready, 1)
            splits(12, 0)
            dve.wait_ge(tab_mm, E)
            link(nc.vector.tensor_copy(wrow[:, :], pst[:, 0:NSLOT]))
            link(nc.vector.tensor_tensor(fa, psg[0:1, 0:NSLOT], trow, ALU.add))
            link(nc.vector.scalar_tensor_tensor(fa, psg[0:1, 0:NSLOT], 0.5, fa, ALU.is_gt, ALU.mult))
            link(nc.vector.tensor_tensor(fa, fa, srow, ALU.add))
            tv = tab[:, 0:NR * ROW].rearrange("p (r k) -> p r k", k=ROW)
            link(nc.vector.tensor_copy(tv[:, :, 0:SLOTS], fa.rearrange("p (r j) -> p r j", j=SLOTS)))
            ce = yw[0:1, 0:4 * NR].rearrange("p (k r) -> p k r", k=4)
            for e in range(1, E):
                link(nc.vector.tensor_scalar(ce[:, e, :], siota[0:1, 0:NR], G[0:1, 19, e:e + 1], None, ALU.is_ge))
            link(nc.vector.tensor_tensor(ce[:, 1, :], ce[:, 1, :], ce[:, 2, :], ALU.add))
            link(nc.vector.tensor_tensor(ce[:, 1, :], ce[:, 1, :], ce[:, 3, :], ALU.add))
            link(nc.vector.tensor_copy(tv[:, :, SLOTS], ce[:, 1, :]))
            total, even = G[0:1, 27, 0:1], G[0:1, 27, 1:2]
            link(nc.vector.tensor_tensor(total, G[0:1, 19, E - 1:E], G[0:1, 18, E - 1:E], ALU.add))
            link(nc.vector.tensor_scalar(ce[:, 0, 0:NR // 2], siota[0:1, 0:NR:2], total, None, ALU.is_lt))
            link(nc.vector.tensor_reduce(even, ce[:, 0, 0:NR // 2], AX.X, ALU.add))
            link(nc.vector.tensor_scalar(even, even, -2.0, 1.0, ALU.mult, ALU.add))
            link(nc.vector.tensor_tensor(even, even, total, ALU.add))
            link(nc.vector.tensor_scalar(total, total, -2.0, None, ALU.add))
            nc.vector.tensor_copy(tab[:, NR * ROW:NR * ROW + 2], G[0:1, 27, 0:2]).then_inc(slots_ready, 1)
            dve.wait_ge(idx_in, 2 * 16)
            kb, kt, t0, t1 = (f4[:, n, :] for n in (8, 9, 10, 11))
            kk, tt = f4[:, 8:10, :], f4[:, 10:12, :]
            link(nc.vector.tensor_copy(kk, kint[:, :, :]))
            link(nc.vector.tensor_scalar(tt, kk, 0.0, float(NT), ALU.is_lt, ALU.mult))
            link(nc.vector.tensor_tensor(kk, kk, tt, ALU.add))
            link(nc.vector.tensor_scalar(tt, kk, float(NT - 1), None, ALU.is_le))
            link(nc.vector.scalar_tensor_tensor(tt, kk, 0.0, tt, ALU.is_ge, ALU.mult))
            link(nc.vector.tensor_tensor(t0, t0, t1, ALU.mult))
            link(nc.vector.scalar_tensor_tensor(kb, kb, float(NT), kt, ALU.mult, ALU.add))
            for edge, move in ((HEAD, NT - 2 * HEAD), (2 * HEAD, HEAD - NT)):
                link(nc.vector.tensor_scalar(t1, kt, float(edge), float(move), ALU.is_ge, ALU.mult))
                link(nc.vector.tensor_tensor(kb, kb, t1, ALU.add))
            link(nc.vector.scalar_tensor_tensor(kb, kb, -2.0 * TOK, t0, ALU.add, ALU.mult))
            for g in range(MG):
                i = nc.vector.tensor_scalar(kdiag[:, g, :], ident[:, :], kb[:, g:g + 1], None, ALU.mult)
            i.then_inc(key_ready, 1)
            splits(13, 1)
            dve.wait_ge(key_mm, 1)
            for m in range(MG):
                link(nc.vector.scalar_tensor_tensor(kcmp, pst[:, :], kb[:, m:m + 1], iot,
                                                    ALU.is_equal, ALU.mult))
                link(nc.vector.tensor_reduce(f4[:, 0, m:m + 1], kcmp, AX.X, ALU.min))
            link(nc.vector.tensor_tensor(f4[:, 2, :], f4[:, 0, :], f4[:, 1, :], ALU.is_equal))
            link(nc.vector.tensor_scalar(f4[:, 3, :], kb, 0.0, None, ALU.is_lt))
            link(nc.vector.tensor_tensor(f4[:, 3, :], f4[:, 3, :], f4[:, 2, :], ALU.mult))
            link(nc.vector.tensor_scalar(f4[:, 4, :], kb, 2.0 * TOK + 1.0, None, ALU.add))
            link(nc.vector.tensor_copy(vals[:, :, 0], f4[:, 4, :]))
            nc.vector.tensor_tensor(vals[:, :, 1], f4[:, 4, :], vals[:, :, 0], ALU.subtract).then_inc(valid_ready, 1)
            splits(14, 0)
            dve.wait_ge(place_mm, 1)
            before = f4[:, 7, :]
            link(nc.vector.tensor_copy(f4[:, 5, :], psg[:, 8:8 + MG]))
            link(nc.vector.memset(before, 0.0))
            for g in range(1, MG):
                link(nc.vector.tensor_tensor(before[:, g:g + 1], before[:, g - 1:g], f4[:, 5, g - 1:g], ALU.add))
            link(nc.vector.tensor_tensor(f4[:, 6, :], psg[:, 0:MG], before, ALU.add))
            link(nc.vector.scalar_tensor_tensor(f4[:, 6, :], f4[:, 6, :], 1.0, f4[:, 3, :], ALU.add, ALU.mult))
            link(nc.vector.tensor_scalar(f4[:, 6, :], f4[:, 6, :], -1.0 - M, None, ALU.add))
            for g in range(MG):
                i = nc.vector.tensor_scalar(oh16[:, g, :], iot, f4[:, 6, g:g + 1], None, ALU.is_equal)
            i.then_inc(place_ready, 1)
            link(nc.vector.tensor_tensor(f4[0:1, 14, 0:1], before[0:1, MG - 1:MG], f4[0:1, 5, MG - 1:MG], ALU.add))
            link(nc.vector.tensor_scalar(f4[0:1, 14, 0:1], f4[0:1, 14, 0:1], -float(M), None, ALU.add))
            link(nc.vector.tensor_scalar(f4[0:1, 15, :], f4[0:1, 1, :], f4[0:1, 14, 0:1], None, ALU.is_lt))
            link(nc.vector.tensor_reduce(f4[0:1, 14, 1:2], f4[0:1, 15, :], AX.X, ALU.add))
            link(nc.vector.tensor_scalar(f4[0:1, 14, 1:2], f4[0:1, 14, 1:2], 1.0, None, ALU.max))
            nc.vector.tensor_copy(tab[:, NR * ROW + 2:NR * ROW + 3], f4[0:1, 14, 1:2]).then_inc(tab_ready, 1)
            splits(15, 1)
            dve.wait_ge(pack_mm, 1)
            link(nc.vector.tensor_reduce(f4[:, 2, :], psg[:, 16:16 + 2 * MG].rearrange("p (g u) -> p g u", u=2),
                                         AX.X, ALU.add))
            link(nc.vector.tensor_scalar(f4[:, 3, :], f4[:, 2, :], 0.0, 2.0 * TOK, ALU.is_equal, ALU.mult))
            link(nc.vector.scalar_tensor_tensor(f4[:, 4, :], f4[:, 2, :], -1.0, f4[:, 3, :], ALU.add, ALU.add))
            link(nc.vector.tensor_copy(sid[:, :], f4[:, 4, :]))
            link(nc.vector.tensor_scalar(f4[:, 6, :], f4[:, 2, :], -1.0, 0.0, ALU.add, ALU.max))
            nc.vector.tensor_copy(gid[:, :], f4[:, 6, :]).then_inc(rows_ready, 1)

            dve.wait_ge(tab_ready, 1)
            regs = [dve.alloc_register(f"slot_address{j}") for j in range(SLOTS)]

            def add_slots(r, parity):
                dve.load(regs, tab[0:1, bass.ds(r * ROW, SLOTS)])
                cols = [dve.snap(x, min_val=0, max_val=COLS - SEG) for x in regs]
                dve.wait_ge(y_taken, r + (R0 + 1))
                if not (isinstance(r, int) and r == 0):
                    dve.wait_ge(y_free, r)
                for j in range(SLOTS):
                    at = acc[:, :, bass.ds(cols[j], SEG)]
                    y = ytmp[:, bass.ds(parity, 1), :, j * SEG:(j + 1) * SEG].rearrange("p o d c -> p (o d) c")
                    i = nc.vector.scalar_tensor_tensor(at, y, wrow[:, bass.ds(r * SLOTS + j, 1)], at,
                                                       ALU.mult, ALU.add)
                i.then_inc(y_free, 1)

            splits(R0, 0, RC)
            dve.wait_ge(spare_ready, 1)

            def step(r, parity):
                splits(r + R0, parity, RC)
                add_slots(r - 1, 1 - parity)

            step(1, 1)
            for n in range(8):
                low_rest(4 * E + n)
                step(2 + n, n % 2)
            last, parity = expert_loops(dve, 10, step)
            add_slots(last, parity)
            stage2_dve(dve, link)

        @block.gpsimd
        def _(pool):
            steps = [0]

            def link(i):
                steps[0] += 1
                i.then_inc(pool_step, 1)
                pool.wait_ge(pool_step, steps[0])

            def count_up(out, pattern, base, channel):
                link(nc.gpsimd.iota(out, pattern=pattern, base=base, channel_multiplier=channel,
                                    allow_small_or_imprecise_dtypes=True))

            def split_x(q):
                pool.wait_ge(x_in[q], 16)
                src, hi, lo = x_piece(q)
                link(nc.gpsimd.tensor_copy(hi, src))
                nc.gpsimd.tensor_tensor(lo, src, hi, ALU.subtract).then_inc(x_split, 1)

            for q in range(1, 8):
                split_x(q)
            pool.wait_ge(small_in, 8 * 16)
            nc.gpsimd.tensor_scalar(gams[:, :], gam[:, :], WS, None, ALU.mult).then_inc(gain_ready, 1)
            for c in (0, BS - 1):
                link(nc.gpsimd.memset(xcols[:, :, :, c:c + 1], 0.0))
            link(nc.gpsimd.memset(X[:, :, NB * BS:COLS], 0.0))
            link(nc.gpsimd.memset(onesm[:, :], 1.0))
            link(nc.gpsimd.affine_select(out=ident[:, :], in_=onesm[:, :], compare_op=ALU.is_equal, fill=0.0,
                                         base=0, pattern=[[1, P]], channel_multiplier=-1))
            link(nc.gpsimd.affine_select(out=tri[:, :], in_=onesm[:, :], compare_op=ALU.is_gt, fill=0.0,
                                         base=0, pattern=[[1, P]], channel_multiplier=-1))
            count_up(siota, [[1, NSLOT]], 0, 0)
            count_up(G[:, 20, :], [[1, E]], -E, 0)
            for e in range(E):
                link(nc.gpsimd.memset(G[:, 24, e:e + 1], float(KEPT[e])))
                count_up(G[:, 25, e:e + 1], [[0, 1]], SEG * KEPT0[e] + FAR, BS)
            link(nc.gpsimd.memset(G[:, 19, :], 0.0))
            count_up(trow, [[RC, NR], [0, SLOTS]], -FAR - NB * BS, 0)
            count_up(srow, [[0, NR], [SEG, SLOTS]], NB * BS, 0)
            count_up(iot, [[1, M]], -M, 0)
            count_up(f4[:, 1, :], [[P, MG]], -M, 1)
            nc.gpsimd.memset(tab[:, :], 0).then_inc(const_ready, 1)
            pool.wait_ge(slots_ready, 1)
            regs = [pool.alloc_register(f"pool_address{j}") for j in range(SLOTS)]

            def stage_columns(r, parity):
                pool.load(regs, tab[0:1, bass.ds(r * ROW, SLOTS)])
                cols = [pool.snap(x, min_val=0, max_val=COLS - SEG) for x in regs]
                if not (isinstance(r, int) and r < 2):
                    pool.wait_ge(l1_done, r * 4 + (R0 * 4 - 4))
                for j in range(SLOTS):
                    i = nc.gpsimd.tensor_copy(xs[:, parity, :, j * SEG:(j + 1) * SEG],
                                              X[:, :, bass.ds(cols[j], SEG)])
                i.then_inc(x_staged, 1)

            stage_columns(0, 0)
            stage_columns(1, 1)
            pool.wait_ge(tab_ready, 1)
            for c in (0, BS - 1):
                nc.gpsimd.memset(acols[:, :, :, c:c + 1], 0.0)
            nc.gpsimd.memset(acc[:, :, NB * BS:COLS], 0.0).then_inc(spare_ready, 1)
            expert_loops(pool, 2, stage_columns)
            stage2_pool(pool, link)


def kernel(**inputs):
    import numpy as np
    import concourse.bacc as bacc
    from concourse.bass_utils import run_bass_kernel_spmd as run

    v = {k.removeprefix("L0_"): np.asarray(x) for k, x in inputs.items()}
    order = np.r_[0:HEAD, 2 * HEAD:NT, HEAD:2 * HEAD]
    x = v["x"][:, order, :].reshape(TOK, D)

    def rows(*parts):
        return np.concatenate([np.asarray(q).reshape(-1, P) for q in parts], 0).T

    first = np.stack([np.concatenate([v[f"ffn_s{w}"][None], v[f"ffn_e{w}"]]) for w in ("w1", "w2")], 1)
    last = np.concatenate([v["ffn_sw3"][None], v["ffn_ew3"]])
    arrays = {
        "xT": x.T.reshape(DB, P, TOK).transpose(1, 0, 2),
        "xR": x,
        "condT": v["cond_1024"].T.reshape(DB, P, NB).transpose(1, 0, 2),
        "ew1": v["cond_ew1"], "ew2": v["cond_ew2"], "sw1": v["cond_sw1"], "sw2": v["cond_sw2"],
        "b1": rows(v["cond_eb1"], v["cond_sb1"]), "b2": rows(v["cond_eb2"], v["cond_sb2"]),
        "gate_w": v["cond_gate_w"], "gate_b": v["cond_gate_b"],
        "time_w": v["cond_time_w"], "time_b": v["cond_time_b"],
        "index_b4": v["ffn_index_b"].reshape(MG, P).T, "index_t4": v["ffn_index_t"].reshape(MG, P).T,
        "fw": first.reshape(NJ, 2, FH, DB, P).transpose(4, 0, 1, 3, 2).reshape(P, NJ * 2 * DB * FH),
        "w3t": last.transpose(2, 0, 1).reshape(P, NJ * D),
        "fb1": rows(v["ffn_sb1"], v["ffn_eb1"]), "fb2": rows(v["ffn_sb2"], v["ffn_eb2"]),
        "gam": rows(v["ffn_s_ln_g"], v["ffn_sel_ln_g"]), "bet": rows(v["ffn_s_ln_b"], v["ffn_sel_ln_b"]),
        "b3s": v["ffn_sb3"].reshape(1, D), "b3e": v["ffn_eb3"],
        "rw": np.concatenate([v["ffn_sg_w"], v["ffn_eg_w"]]).T.reshape(DB, P, 9).transpose(1, 0, 2),
        "rb": np.concatenate([v["ffn_sg_b"], v["ffn_eg_b"]]), "eb": v["ffn_exp_bias"],
    }
    arrays = {n: np.ascontiguousarray(q) for n, q in arrays.items()}
    nc = bacc.Bacc("TRN2", target_bir_lowering=False, num_devices=1)
    a = {n: nc.dram_tensor(f"in_{n}", q.shape, mybir.dt.from_np(q.dtype), kind="ExternalInput").ap()
         for n, q in arrays.items()}
    a["out"] = nc.dram_tensor("out_rows", (TOK, D), F32, kind="ExternalOutput").ap()
    a["scratch"] = nc.dram_tensor("stage1_rows", (TOK, 2 * D), F16, kind="Internal").ap()
    program(nc, a)
    r = run(nc, [{f"in_{n}": q for n, q in arrays.items()}], core_ids=[0])
    got = np.asarray(r.results[0]["out_rows"]).reshape(NB, NT, D)
    return got[:, np.argsort(order), :]
```
